# Optimizing a Trainium2 kernel written in Bass

```python
import numpy as np
import jax
import jax.numpy as jnp

def _softmax(x, axis=-1):
    return jax.nn.softmax(x, axis=axis)

def _gelu(x):
    return jax.nn.gelu(x, approximate=True)

def _silu(x):
    return jax.nn.silu(x)

def _sigmoid(x):
    return jax.nn.sigmoid(x)

def _layernorm(x, axis=-1, eps=1e-05):
    m = jnp.mean(x, axis=axis, keepdims=True)
    v = jnp.var(x, axis=axis, keepdims=True)
    return (x - m) / jnp.sqrt(v + eps)

def _scatter_add(tgt, idx, src, axis=0):
    return tgt.at[idx].add(src)

def _segment_sum(src, seg, n):
    return jax.ops.segment_sum(src, seg, n)
kernel_name = 'mk_gnn_preln_d4_gnn_r64_3d1b52'

def setup_inputs(seed: int=0):
    np.random.seed(seed)
    _w = jnp.asarray

    def _rec_inputs():
        import jax
        import jax.numpy as jnp
        _gk = jax.random.key(seed)
        x = -0.000202 + 1 * jax.random.normal(jax.random.fold_in(_gk, 1), (100000, 64), jnp.float32)
        src = jax.random.randint(jax.random.fold_in(_gk, 2), (50000,), 0, 100000, jnp.int32)
        dst = jax.random.randint(jax.random.fold_in(_gk, 3), (50000,), 0, 100000, jnp.int32)
        _o = jnp.argsort(dst, stable=True)
        src = src[_o]
        dst = dst[_o]
        edge_attr_64 = 7.68618e-05 + 1.00005 * jax.random.normal(jax.random.fold_in(_gk, 12), (50000, 64), jnp.float32)
        return (x, src, dst, edge_attr_64)
    x, src, dst, edge_attr_64 = _rec_inputs()

    def _L0_gnn_setup():
        import jax, jax.numpy as jnp
        import numpy as np
        N = 100000
        E = 25000
        C_IN = 64
        C_HID = 2 * C_IN
        C_OUT = 64

        def _sgconv(x, W, b, src, dst, n):
            loop = jnp.arange(n, dtype=src.dtype)
            s = jnp.concatenate([src, loop])
            d = jnp.concatenate([dst, loop])
            w = jnp.ones(s.shape[0], dtype=x.dtype)
            deg = jax.ops.segment_sum(w, d, num_segments=n)
            dinv = jnp.where(deg > 0, jax.lax.rsqrt(deg), 0.0)
            norm = dinv[s] * dinv[d]
            msgs = norm[:, None] * x[s]
            agg = jax.ops.segment_sum(msgs, d, num_segments=n)
            return agg @ W.T + b
        key = jax.random.key(seed)
        k1, k2, k3, k4, k5, k6, k7 = jax.random.split(key, 7)
        x = jax.random.normal(k1, (N, C_IN), dtype=jnp.float32)
        edge_index = jax.random.randint(k2, (2, E), 0, N, dtype=jnp.int64)
        lim3 = 1.0 / np.sqrt(C_IN)
        W3 = jax.random.uniform(k3, (C_HID, C_IN), jnp.float32, -lim3, lim3)
        b3 = jax.random.uniform(k4, (C_HID,), jnp.float32, -lim3, lim3)
        lim4 = 1.0 / np.sqrt(C_HID)
        W4 = jax.random.uniform(k5, (C_OUT, C_HID), jnp.float32, -lim4, lim4)
        b4 = jax.random.uniform(k6, (C_OUT,), jnp.float32, -lim4, lim4)
        return {'x': x, 'edge_index': edge_index, 'W3': W3, 'b3': b3, 'W4': W4, 'b4': b4}
    _L0_gnn_all = _L0_gnn_setup()
    _L0_gnn_in = {k: v for k, v in _L0_gnn_all.items() if k in ('W3', 'b3', 'W4', 'b4')}
    del _L0_gnn_all

    def _L1_gnn_setup():
        import jax, jax.numpy as jnp
        import numpy as np
        N_NODES = 100000
        N_EDGES = 15625
        D_IN = 64
        D_OUT = 64
        key = jax.random.key(seed)
        k_x, k_ei, k_ea, k_w, k_b = jax.random.split(key, 5)
        x = jax.random.normal(k_x, (N_NODES, D_IN), dtype=jnp.float32)
        edge_index = jax.random.randint(k_ei, (2, N_EDGES), 0, N_NODES, dtype=jnp.int64)
        edge_attr = jax.random.normal(k_ea, (N_EDGES, D_IN), dtype=jnp.float32)
        bound = 1.0 / np.sqrt(D_IN)
        W = jax.random.uniform(k_w, (D_OUT, D_IN), dtype=jnp.float32, minval=-bound, maxval=bound)
        b = jax.random.uniform(k_b, (D_OUT,), dtype=jnp.float32, minval=-bound, maxval=bound)
        eps = jnp.zeros((), dtype=jnp.float32)
        return {'x': x, 'edge_index': edge_index, 'edge_attr': edge_attr, 'W': W, 'b': b, 'eps': eps}
    _L1_gnn_all = _L1_gnn_setup()
    _L1_gnn_in = {k: v for k, v in _L1_gnn_all.items() if k in ('W', 'b', 'eps')}
    del _L1_gnn_all

    def _L2_gnn_setup():
        import jax, jax.numpy as jnp
        import numpy as np
        N, E, D, K = (50000, 12500, 64, 8)
        ALPHA = 0.1

        def _edge_softmax(e, dst, n):
            m = jax.ops.segment_max(e, dst, num_segments=n)
            a = jnp.exp(e - m[dst])
            s = jax.ops.segment_sum(a, dst, num_segments=n)
            return a / s[dst]
        key = jax.random.key(seed)
        ks = jax.random.split(key, 4)
        x = jax.random.normal(ks[0], (N, D), dtype=jnp.float32)
        src = jax.random.randint(ks[1], (E,), 0, N, dtype=jnp.int32)
        dst = jax.random.randint(ks[2], (E,), 0, N, dtype=jnp.int32)
        attn_w = jax.random.normal(ks[3], (1, 2 * D), dtype=jnp.float32) * np.float32(1.0 / np.sqrt(2 * D))
        temp = np.asarray(ALPHA * (1.0 - ALPHA) ** np.arange(K + 1), dtype=np.float32)
        temp[-1] = np.float32((1.0 - ALPHA) ** K)
        return {'x': x, 'attn_w': attn_w, 'temp': jnp.asarray(temp), 'src': src, 'dst': dst}
    _L2_gnn_all = _L2_gnn_setup()
    _L2_gnn_in = {k: v for k, v in _L2_gnn_all.items() if k in ('attn_w', 'temp')}
    del _L2_gnn_all

    def _L3_gnn_setup():
        import jax, jax.numpy as jnp
        import numpy as np
        import math
        K = 10
        BETA = 2.0
        N_NODES = 100000
        N_EDGES = 15625
        HIDDEN = 64
        key = jax.random.key(seed)
        k1, k2, k3 = jax.random.split(key, 3)
        feat = jax.random.normal(k1, (N_NODES, HIDDEN), dtype=jnp.float32)
        src = jax.random.randint(k2, (N_EDGES,), 0, N_NODES, dtype=jnp.int64)
        dst = jax.random.randint(k3, (N_EDGES,), 0, N_NODES, dtype=jnp.int64)
        return {'feat': feat, 'src': src, 'dst': dst}
    _L3_gnn_all = _L3_gnn_setup()
    _L3_gnn_in = {k: v for k, v in _L3_gnn_all.items() if k in ()}
    del _L3_gnn_all
    return {'x': x, 'src': src, 'dst': dst, 'edge_attr_64': edge_attr_64, 'L0_gnn_W3': _L0_gnn_in['W3'], 'L0_gnn_b3': _L0_gnn_in['b3'], 'L0_gnn_W4': _L0_gnn_in['W4'], 'L0_gnn_b4': _L0_gnn_in['b4'], 'L1_gnn_W': _L1_gnn_in['W'], 'L1_gnn_b': _L1_gnn_in['b'], 'L1_gnn_eps': _L1_gnn_in['eps'], 'L2_gnn_attn_w': _L2_gnn_in['attn_w'], 'L2_gnn_temp': _L2_gnn_in['temp']}

def reference(x, src, dst, edge_attr_64, L0_gnn_W3, L0_gnn_b3, L0_gnn_W4, L0_gnn_b4, L1_gnn_W, L1_gnn_b, L1_gnn_eps, L2_gnn_attn_w, L2_gnn_temp):
    import jax
    import jax.numpy as jnp

    def _L0_gnn_ref(x, edge_index, W3, b3, W4, b4):
        import jax, jax.numpy as jnp
        import numpy as np
        N = 100000
        E = 25000
        C_IN = 64
        C_HID = 2 * C_IN
        C_OUT = 64

        def _sgconv(x, W, b, src, dst, n):
            loop = jnp.arange(n, dtype=src.dtype)
            s = jnp.concatenate([src, loop])
            d = jnp.concatenate([dst, loop])
            w = jnp.ones(s.shape[0], dtype=x.dtype)
            deg = jax.ops.segment_sum(w, d, num_segments=n)
            dinv = jnp.where(deg > 0, jax.lax.rsqrt(deg), 0.0)
            norm = dinv[s] * dinv[d]
            msgs = norm[:, None] * x[s]
            agg = jax.ops.segment_sum(msgs, d, num_segments=n)
            return agg @ W.T + b
        src, dst = (edge_index[0], edge_index[1])
        n = x.shape[0]
        h = jax.nn.relu(_sgconv(x, W3, b3, src, dst, n))
        return _sgconv(h, W4, b4, src, dst, n)

    def _L1_gnn_ref(x, edge_index, edge_attr, W, b, eps):
        import jax, jax.numpy as jnp
        import numpy as np
        N_NODES = 100000
        N_EDGES = 15625
        D_IN = 64
        D_OUT = 64
        src = edge_index[0]
        dst = edge_index[1]
        msg = jax.nn.relu(x[src] + edge_attr)
        agg = jax.ops.segment_sum(msg, dst, num_segments=x.shape[0])
        h = (1.0 + eps) * x + agg
        out = h @ W.T + b
        return jax.nn.relu(out)

    def _L2_gnn_ref(x, attn_w, temp, src, dst):
        import jax, jax.numpy as jnp
        import numpy as np
        N, E, D, K = (50000, 12500, 64, 8)
        ALPHA = 0.1

        def _edge_softmax(e, dst, n):
            m = jax.ops.segment_max(e, dst, num_segments=n)
            a = jnp.exp(e - m[dst])
            s = jax.ops.segment_sum(a, dst, num_segments=n)
            return a / s[dst]
        n, d = x.shape
        w_src = attn_w[0, :d]
        w_dst = attn_w[0, d:]
        h = x
        th = x * temp[0]
        for k in range(K):
            s1 = h @ w_src
            s2 = h @ w_dst
            e = jax.nn.leaky_relu(s1[src] + s2[dst])
            a = _edge_softmax(e, dst, n)
            h = jax.ops.segment_sum(h[src] * a[:, None], dst, num_segments=n)
            th = th + h * temp[k + 1]
        return th

    def _L3_gnn_ref(feat, src, dst):
        import jax, jax.numpy as jnp
        import numpy as np
        import math
        K = 10
        BETA = 2.0
        N_NODES = 100000
        N_EDGES = 15625
        HIDDEN = 64
        n = feat.shape[0]
        ones_e = jnp.ones(src.shape, dtype=feat.dtype)
        out_deg = jax.ops.segment_sum(ones_e, src, num_segments=n)
        in_deg = jax.ops.segment_sum(ones_e, dst, num_segments=n)
        src_norm = jnp.maximum(out_deg, 1.0) ** (-0.5)
        dst_norm = jnp.maximum(in_deg, 1.0) ** (-0.5)
        logs = [math.log(BETA + i) for i in range(1, K + 2)]
        denom = sum(logs)
        w = [l / denom for l in logs]
        h = feat
        out = w[0] * feat
        for step in range(K):
            m = (h * src_norm[:, None])[src]
            h = jax.ops.segment_sum(m, dst, num_segments=n)
            h = h * dst_norm[:, None]
            out = out + w[step + 1] * h
        return out
    edge_index = jnp.stack([src, dst])
    h = jnp.maximum(_layernorm(x, axis=-1), 0.0)
    x = x + _L0_gnn_ref(h, edge_index, L0_gnn_W3, L0_gnn_b3, L0_gnn_W4, L0_gnn_b4)
    h = jnp.maximum(_layernorm(x, axis=-1), 0.0)
    x = x + _L1_gnn_ref(h, edge_index, edge_attr_64, L1_gnn_W, L1_gnn_b, L1_gnn_eps)
    h = jnp.maximum(_layernorm(x, axis=-1), 0.0)
    x = x + _L2_gnn_ref(h, L2_gnn_attn_w, L2_gnn_temp, src, dst)
    h = jnp.maximum(_layernorm(x, axis=-1), 0.0)
    x = x + _L3_gnn_ref(h, src, dst)
    return x

_drawn_inputs = setup_inputs


def setup_inputs(seed=0):
    import zlib

    import numpy as np

    out = dict(_drawn_inputs(seed))
    spreads = {}
    factors = {}
    for name, (base, spread) in spreads.items():
        noise = np.random.default_rng([zlib.crc32(name.encode()), seed]).standard_normal(out[name].shape)
        drawn = base * np.exp(spread * noise) if base else spread * noise
        out[name] = jnp.asarray(drawn.astype(out[name].dtype))
    for name, factor in factors.items():
        out[name] = (out[name] * factor).astype(out[name].dtype)
    return out
```

```python
_N, _E, _D = 100000, 50000, 64


def _build(nc, x, src, dst, edge_attr, W3, b3, W4, b4, W1, b1, eps, attn_w, temp, out):
    import math
    from contextlib import ExitStack

    import concourse.bass as bass
    from concourse import mybir

    f32, f16, i32 = mybir.dt.float32, mybir.dt.float16, mybir.dt.int32
    ALU = mybir.AluOpType
    ACT = mybir.ActivationFunctionType
    AXX = mybir.AxisListType.X
    ds = bass.ds

    P = 128
    N, E, D = _N, _E, _D
    HID = W3.shape[0]
    CH = 14
    NCH = 28
    COLS = CH * NCH
    EP = P * COLS
    assert EP >= E and NCH % 2 == 0
    LASTP = E - (P - 1) * COLS
    assert 0 < LASTP <= COLS
    FC = COLS
    XC = COLS + 2
    AW = D + 3
    REG = EP + 1
    ZERO = EP
    TILE = P * CH
    NT = -(-N // TILE)
    assert NT % 2 == 0
    LOB = 1024
    NHI = -(-N // LOB)
    PAD = 1 << 20
    BIG = 1 << 22
    NEG = -1e38
    LN_EPS = 1e-5
    LEAK = 0.01
    K2 = temp.shape[0] - 1
    K3 = 10
    logs = [math.log(2.0 + i) for i in range(1, K3 + 2)]
    mix = [v / sum(logs) for v in logs]

    ctx = ExitStack()
    with ctx:
        def sb(name, shape, dt=f32):
            return ctx.enter_context(nc.sbuf_tensor(name, shape, dt))

        def sem(name):
            return ctx.enter_context(nc.semaphore(name))

        def dram(name, shape, dt=f32):
            return nc.dram_tensor(name, shape, dt, kind="Internal").ap()

        tab_a = dram("tab_a", [N + EP, D])
        tab_b = dram("tab_b", [N + EP, D])
        tab_c = dram("tab_c", [N + EP, D])
        tab_d = dram("tab_d", [N + REG, AW])
        tab_e = dram("tab_e", [N + REG, D])
        alt_d = dram("alt_d", [REG, AW])
        alt_e = dram("alt_e", [REG, D])
        raw = dram("raw", [EP, D])
        lookup = dram("lookup", [NHI * LOB, 4])
        ea_last = dram("ea_last", [COLS, D])

        X = sb("X", [P, XC, D])
        srcI = sb("srcI", [P, COLS], i32)
        dstI = sb("dstI", [P, COLS], i32)
        nextI = sb("nextI", [P, COLS], i32)
        prevI = sb("prevI", [P, COLS], i32)
        dst_gat = sb("dst_gat", [P, COLS], i32)
        dst_tab = sb("dst_tab", [P, COLS], i32)
        dst_out = sb("dst_out", [P, COLS], i32)
        idxA = sb("idxA", [P, COLS], i32)
        idxC = sb("idxC", [P, COLS], i32)
        seatI = nextI
        seatf = sb("seatf", [P, COLS])
        place = sb("place", [P, COLS])
        cont = sb("cont", [P, COLS])
        pen = sb("pen", [P, COLS])
        ends = sb("ends", [P, COLS])
        goes = sb("goes", [P, COLS])
        front = sb("front", [P, COLS])
        after = sb("after", [P, COLS])
        dinv = sb("dinv", [P, XC])
        dnorm = sb("dnorm", [P, XC])
        snE = sb("snE", [P, COLS])
        dnE = sb("dnE", [P, COLS])
        s2V = dst_gat.bitcast(f32)
        s2E = dst_tab.bitcast(f32)
        mx = prevI.bitcast(f32)
        tmpA = sb("tmpA", [P, COLS])
        tmpB = sb("tmpB", [P, COLS])
        c0 = sb("c0", [P, 1])
        allc = sb("allc", [P, 1])
        noend = sb("noend", [P, 1])
        fr = sb("fr", [P, 8])
        fidx = sb("fidx", [P, 8], i32)
        F_DST, F_SEAT, F_TAB, F_SEAT_W, F_TAB_W, F_OUT = range(6)
        allcT = sb("allcT", [P, P])
        c0T = sb("c0T", [P, P])
        noendT = sb("noendT", [1, P])
        ident = sb("ident", [P, P])
        w3 = sb("w3", [P, 2, D])
        w4 = sb("w4", [D, HID])
        w1 = sb("w1", [D, 2, D])
        w3T = sb("w3T", [P, HID])
        w4T = sb("w4T", [HID, D])
        w1T = sb("w1T", [P, D])
        w1Te = sb("w1Te", [P, D])
        b3c = sb("b3c", [HID, 1])
        b4b = sb("b4b", [P, D])
        b1b = sb("b1b", [P, D])
        eps1 = sb("eps1", [P, 1])
        attn = sb("attn", [P, 2 * D])
        tempb = sb("tempb", [P, K2 + 1])
        mixb = sb("mixb", [P, K3 + 1])
        wk = sb("wk", [P, 1])
        lneps = sb("lneps", [P, 1])
        zrow = sb("zrow", [1, AW])
        G = sb("G", [P, 2, CH, AW])
        idxs = sb("idxs", [P, 2, CH], i32)
        vals = sb("vals", [P, 2, CH, 2])
        look = sb("look", [P, 2, CH, 4])
        xin = sb("xin", [P, 2, CH, D])
        own = xin
        SL = 2 * CH * D
        shared = sb("shared", [P, LOB * 4])
        assert 2 * SL + 4 * P <= LOB * 4 and CH * P == SL
        lookI = shared[:, :].rearrange("p (a b) -> p a b", b=4)
        hist = lookI[:, :, 1]
        U = shared[0:HID, 0:SL].rearrange("p (h q n) -> p h q n", h=2, q=CH // 2)
        ea = shared[:, SL:2 * SL].rearrange("p (s j f) -> p s j f", s=2, j=CH)
        DT = shared[:, 2 * SL:2 * SL + 2 * P].rearrange("p (a b) -> p a b", a=2)
        ET = shared[:, 2 * SL + 2 * P:2 * SL + 4 * P].rearrange("p (a b) -> p a b", a=2)
        carry = sb("carry", [P, AW])
        agg = sb("agg", [P, CH, D])
        xm = sb("xm", [P, CH, D])
        st = sb("st", [P, CH, 6])
        lnw = sb("lnw", [P, 6, CH])
        rowsA = sb("rowsA", [P, CH, D])
        rowsB = sb("rowsB", [P, CH, D])
        rowsC = sb("rowsC", [P, CH, D])
        rowsD = sb("rowsD", [P, CH, AW])
        rowsE = sb("rowsE", [P, CH, D])
        hT = sb("hT", [P, CH // 2, P])
        chn = sb("chn", [P, 4, CH])
        sm = sb("sm", [P, 8, CH])
        ms = sb("ms", [P, CH + 1])
        dif = sb("dif", [P, 2 * CH])
        expd = sb("expd", [P, 2 * CH])
        FR = sb("FR", [P, 2, AW])
        fown = sb("fown", [P, 2, D])
        TF = sb("TF", [P, P + 1])
        IT = sb("IT", [P, P])
        MF = sb("MF", [P, P + 1])
        mrep = sb("mrep", [P, AW])
        row = sb("row", [1, 2, P + 1])
        fm = sb("fm", [P, 8])
        half = xin[:, :, :, :].rearrange("p s j f -> p (s j f)").bitcast(f16)
        iota16 = half[:, 0:LOB]
        hot_lo = half[:, LOB:3 * LOB].rearrange("p (a b) -> p a b", a=2)
        hot_hi = half[:, 3 * LOB:3 * LOB + 2 * P].rearrange("p (a b) -> p a b", a=2)
        row_ac = [rowsA, rowsC]
        row_be = [rowsB, rowsE]
        row_d = [rowsD, G[:, 0, :, :]]
        iotaN = lookI[:, :, 3].bitcast(i32)
        placeI = idxC

        TR = ctx.enter_context(nc.psum_tensor("TR", [P, 1024], f32))
        HP = ctx.enter_context(nc.psum_tensor("HP", [P, 4, 512], f32))
        TR1 = ctx.enter_context(nc.psum_tensor("TR1", [P, 1024], f32))
        MI = HP[:, 3, :]
        HI = HP[:, 0:2, :]

        iotas = sem("iotas")
        cleared = sem("cleared")
        loaded = sem("loaded")
        masks = sem("masks")
        weightsT = sem("weightsT")
        wcopied = sem("wcopied")
        dve_step = sem("dve_step")
        pool_step = sem("pool_step")
        hot_ready = sem("hot_ready")
        hot_used = sem("hot_used")
        hist_ready = sem("hist_ready")
        hist_used = sem("hist_used")
        look_ready = sem("look_ready")
        look_stored = sem("look_stored")
        count_ready = sem("count_ready")
        scattered = [sem("scattered0"), sem("scattered1")]
        looked = [sem("looked0"), sem("looked1")]
        look_done = sem("look_done")
        gathered = [sem("gathered0"), sem("gathered1")]
        gathered3 = [sem("gathered3_0"), sem("gathered3_1")]
        used = [sem("used0"), sem("used1")]
        x_kept = [sem("x_kept0"), sem("x_kept1")]
        front_x = sem("front_x")
        raw_ready = sem("raw_ready")
        raw_stored = [sem("raw_stored0"), sem("raw_stored1")]
        own_loaded = [sem("own_loaded0"), sem("own_loaded1")]
        ea_loaded = [sem("ea_loaded0"), sem("ea_loaded1")]
        ea_padded = sem("ea_padded")
        x_loaded = [sem("x_loaded0"), sem("x_loaded1")]
        out_stored = [sem("out_stored0"), sem("out_stored1")]
        rows_ready = sem("rows_ready")
        stored = {k: sem(f"stored_{k}") for k in "abcde"}
        dense_stored = {k: [sem(f"dense_{k}0"), sem(f"dense_{k}1")] for k in "abcde"}
        var_ready = sem("var_ready")
        sd_ready = sem("sd_ready")
        dif_ready = sem("dif_ready")
        exp_ready = sem("exp_ready")
        mixed_ready = sem("mixed_ready")
        rowsT_ready = sem("rowsT_ready")
        rowsT_copied = sem("rowsT_copied")
        hid_ready = sem("hid_ready")
        hid_copied = sem("hid_copied")
        conv_ready = sem("conv_ready")
        conv_copied = sem("conv_copied")
        to_turn = sem("to_turn")
        turned = sem("turned")
        f_gathered = sem("f_gathered")
        f_rows = sem("f_rows")
        f_ready = sem("f_ready")
        f_stored = sem("f_stored")
        step_done = sem("step_done")
        final_ready = [sem("final_ready0"), sem("final_ready1")]
        final_stored = sem("final_stored")
        zeros_ready = sem("zeros_ready")
        zeros_stored = sem("zeros_stored")

        class Reached:

            def __init__(self, eng, name):
                self.eng, self.reg = eng, eng.alloc_register(name)
                eng.reg_mov(self.reg, 0)

            def more(self, n):
                self.eng.reg_add(self.reg, self.reg, n)
                return self.reg

            def skip(self, n):
                self.eng.reg_add(self.reg, self.reg, n)

        sp_waited, pool_waited, pe_waited = sem("sp_waited"), sem("pool_waited"), sem("pe_waited")

        def cols(t, c, n=CH):
            return t[:, ds(c * n, n)]

        def seats(table, first, c):
            return table[first:first + EP, :].rearrange("(p j) f -> p j f", p=P)[:, ds(c * CH, CH), :]

        def nodes(table, first):
            return table[ds(first, TILE), :].rearrange("(p j) f -> p j f", p=P)

        def wide(t, n=D):
            return t.unsqueeze(2).to_broadcast([t.shape[0], t.shape[1], n])

        def flat_rows(t, R):
            return t.unsqueeze(1).to_broadcast([P, R, t.shape[1]])

        TILES = [t * TILE for t in range(NT - 1)] + [N - TILE]
        TR_OF = [TR, TR1]

        block = ctx.enter_context(nc.Block())

        @block.sync
        def _(sp):
            r_used = [Reached(sp, f"sp_used{s}") for s in (0, 1)]
            r_out = [Reached(sp, f"sp_out{s}") for s in (0, 1)]
            r_gat = [Reached(sp, f"sp_gat{s}") for s in (0, 1)]
            sp.dma_start(w3[:, 0, :], W3).then_inc(loaded, 16)
            sp.dma_start(w3[:, 1, :], W3).then_inc(loaded, 16)
            sp.dma_start(w4[:, :], W4).then_inc(loaded, 16)
            sp.dma_start(w1[:, 0, :], W1).then_inc(loaded, 16)
            sp.dma_start(w1[:, 1, :], W1).then_inc(loaded, 16)
            sp.dma_start(b3c[:, :], b3.unsqueeze(1)).then_inc(loaded, 16)
            for t, v in ((b4b, b4), (b1b, b1), (tempb, temp)):
                sp.dma_start(t[:, :], v.unsqueeze(0).to_broadcast([P, t.shape[1]])).then_inc(loaded, 16)
            sp.dma_start(eps1[:, :], eps.unsqueeze(0).to_broadcast([P, 1])).then_inc(loaded, 16)
            sp.dma_start(attn[:, :], attn_w.to_broadcast([P, 2 * D])).then_inc(loaded, 16)
            sp.wait_ge(cleared, 1)
            B = P - 1
            for t, v, sh in ((srcI, src, 0), (dstI, dst, 0), (nextI, dst, 1)):
                sp.dma_start(t[0:B, :], v[sh:sh + B * COLS].rearrange("(p j) -> p j", j=COLS))\
                    .then_inc(loaded, 16)
                sp.dma_start(t[B:P, 0:LASTP - sh], v[B * COLS + sh:E].unsqueeze(0)).then_inc(loaded, 16)
            sp.dma_start(prevI[0:1, 1:COLS], dst[0:COLS - 1].unsqueeze(0)).then_inc(loaded, 16)
            sp.dma_start(prevI[1:B, :], dst[COLS - 1:B * COLS - 1].rearrange("(p j) -> p j", j=COLS))\
                .then_inc(loaded, 16)
            sp.dma_start(prevI[B:P, 0:LASTP + 1], dst[B * COLS - 1:E].unsqueeze(0)).then_inc(loaded, 16)
            sp.dma_start(ea_last[0:LASTP, :], edge_attr[B * COLS:E, :]).then_inc(ea_padded, 16)
            sp.wait_ge(zeros_ready, 1)
            sp.dma_start(ea_last[LASTP:COLS, :].rearrange("(o a) d -> o a d", o=1),
                         zrow[:, 0:D].unsqueeze(1).to_broadcast([1, COLS - LASTP, D])).then_inc(ea_padded, 16)
            for t, z in ((tab_d, N + ZERO), (alt_d, ZERO), (tab_e, N + ZERO), (alt_e, ZERO)):
                sp.dma_start(t[z:z + 1, :], zrow[:, 0:t.shape[1]]).then_inc(zeros_stored, 16)
            with sp.Fori(0, NCH // 2) as i:
                for s in (0, 1):
                    sp.wait_ge(gathered[s], r_gat[s].more(16 * CH))
                    sp.sem_inc(sp_waited, 1)
                    sp.dma_start(X[:, ds((2 * i + s) * CH, CH), :], G[:, s, :, 0:D]).then_inc(x_kept[s], 16)
            sp.wait_ge(look_ready, 1)
            sp.dma_start(lookup.rearrange("(p j) f -> p j f", p=NHI), lookI[0:NHI, :, :])\
                .then_inc(look_stored, 16)
            with sp.Fori(0, NT // 2 - 1) as i:
                for s in (0, 1):
                    sp.wait_ge(out_stored[s], r_out[s].reg)
                    sp.sem_inc(sp_waited, 1)
                    r_out[s].skip(16)
                    sp.dma_start(xin[:, s, :, :], nodes(x, (2 * i + s) * TILE)).then_inc(x_loaded[s], 16)
            for s in (0, 1):
                sp.wait_ge(out_stored[s], r_out[s].reg)
                sp.sem_inc(sp_waited, 1)
                r_out[s].skip(16)
                sp.dma_start(xin[:, s, :, :], nodes(x, TILES[NT - 2 + s])).then_inc(x_loaded[s], 16)
            for s in (0, 1):
                sp.wait_ge(out_stored[s], r_out[s].reg)
                sp.sem_inc(sp_waited, 1)
            r_fs = Reached(sp, "sp_fs")
            r_st = {k: Reached(sp, f"sp_stored_{k}") for k in "abc"}
            for k, t in (("a", tab_a), ("b", tab_b), ("c", tab_c)):
                if k == "c":
                    sp.wait_ge(ea_padded, 32)
                sp.wait_ge(stored[k], r_st[k].more(16 * NCH))
                sp.sem_inc(sp_waited, 1)
                sp.wait_ge(f_stored, r_fs.more(16))
                sp.sem_inc(sp_waited, 1)
                with sp.Fori(0, NCH // 2) as i:
                    for s in (0, 1):
                        c = 2 * i + s
                        sp.wait_ge(used[s], r_used[s].reg)
                        sp.sem_inc(sp_waited, 1)
                        r_used[s].skip(1)
                        sp.dma_start(own[:, s, :, :], seats(t, N, c)).then_inc(own_loaded[s], 16)
                        if k == "c":
                            ev = edge_attr[0:B * COLS, :].rearrange("(p j) f -> p j f", p=B)
                            sp.dma_start(ea[0:112, s, :, :], ev[0:112, ds(c * CH, CH), :])\
                                .then_inc(ea_loaded[s], 16)
                            sp.dma_start(ea[112:B, s, :, :], ev[112:B, ds(c * CH, CH), :])\
                                .then_inc(ea_loaded[s], 16)
                            sp.dma_start(ea[B:P, s, :, :],
                                         ea_last[ds(c * CH, CH), :].rearrange("(o a) d -> o a d", o=1))\
                                .then_inc(ea_loaded[s], 16)

        @block.gpsimd
        def _(pool):
            r_step = Reached(pool, "pool_steps")
            r_used = [Reached(pool, f"pool_used{s}") for s in (0, 1)]
            r_xk = [Reached(pool, f"pool_xk{s}") for s in (0, 1)]
            r_raw = [Reached(pool, f"pool_raw{s}") for s in (0, 1)]
            r_sc = [Reached(pool, f"pool_sc{s}") for s in (0, 1)]
            r_lk = [Reached(pool, f"pool_lk{s}") for s in (0, 1)]
            r_fg = Reached(pool, "pool_fg")
            r_fr = Reached(pool, "pool_fr")
            r_fs = Reached(pool, "pool_fs")
            r_sd = Reached(pool, "pool_sd")
            zero = pool.alloc_register("pool_zero")
            bound = pool.alloc_register("pool_bound")
            pool.reg_mov(zero, 0)

            def last_row(table):
                pool.reg_add(bound, zero, table.shape[0] - 1)

            def gather(to, table, index, s):
                pool.indirect_dma_start(to, None, table, bass.IndirectOffsetOnAxis(ap=index, axis=0),
                                        bounds_check=bound, oob_is_err=False).then_inc(s, 16)

            def scatter(table, index, frm, s):
                pool.indirect_dma_start(table, bass.IndirectOffsetOnAxis(ap=index, axis=0), frm, None,
                                        bounds_check=bound, oob_is_err=False).then_inc(s, 16)

            pool.iota(placeI[:, :], pattern=[[1, COLS]], base=0, channel_multiplier=COLS).then_inc(pool_step, 1)
            pool.wait_ge(pool_step, r_step.more(1))
            pool.sem_inc(pool_waited, 1)
            pool.iota(iotaN, pattern=[[1, LOB]], base=0, channel_multiplier=LOB).then_inc(pool_step, 1)
            pool.wait_ge(pool_step, r_step.more(1))
            pool.sem_inc(pool_waited, 1)
            pool.iota(iota16[:, :], pattern=[[1, LOB]], base=0, channel_multiplier=0,
                      allow_small_or_imprecise_dtypes=True).then_inc(pool_step, 1)
            pool.wait_ge(pool_step, r_step.more(1))
            pool.sem_inc(pool_waited, 1)
            pool.memset(ident[:, :], 0.0).then_inc(pool_step, 1)
            pool.wait_ge(pool_step, r_step.more(1))
            pool.sem_inc(pool_waited, 1)
            pool.affine_select(out=ident[:, :], in_=ident[:, :], compare_op=ALU.not_equal, fill=1.0,
                               base=0, pattern=[[-1, P]], channel_multiplier=1).then_inc(pool_step, 1)
            pool.wait_ge(pool_step, r_step.more(1))
            pool.sem_inc(pool_waited, 1)
            pool.sem_inc(iotas, 1)

            pool.wait_ge(masks, 1)
            last_row(x)
            with pool.Fori(0, NCH // 2) as i:
                for s in (0, 1):
                    pool.wait_ge(x_kept[s], r_xk[s].reg)
                    pool.sem_inc(pool_waited, 1)
                    r_xk[s].skip(16)
                    pool.tensor_copy(idxs[:, s, :], cols(dst_gat, 2 * i + s)).then_inc(pool_step, 1)
                    pool.wait_ge(pool_step, r_step.more(1))
                    pool.sem_inc(pool_waited, 1)
                    last_row(x)
                    for j in range(CH):
                        gather(G[:, s, j, 0:D], x, idxs[:, s, j:j + 1], gathered[s])
            gather(X[:, FC, :], x, fidx[:, F_DST:F_DST + 1], front_x)

            pool.wait_ge(masks, 2)
            pool.wait_ge(look_stored, 16)
            pairs = lookup.rearrange("n (a f) -> (n a) f", f=2)
            last_row(pairs)
            with pool.Fori(0, NCH // 2) as i:
                for s in (0, 1):
                    pool.wait_ge(scattered[s], r_sc[s].reg)
                    pool.sem_inc(pool_waited, 1)
                    r_sc[s].skip(16 * CH)
                    pool.tensor_copy(idxs[:, s, :], cols(dst_tab, 2 * i + s))
                    pool.tensor_copy(vals[:, s, :, 0], cols(place, 2 * i + s))
                    pool.tensor_copy(vals[:, s, :, 1], dnorm[:, ds((2 * i + s) * CH, CH)]).then_inc(pool_step, 1)
                    pool.wait_ge(pool_step, r_step.more(1))
                    pool.sem_inc(pool_waited, 1)
                    last_row(pairs)
                    for j in range(CH):
                        scatter(pairs, idxs[:, s, j:j + 1], vals[:, s, j, :], scattered[s])
            for s in (0, 1):
                pool.wait_ge(scattered[s], r_sc[s].reg)
                pool.sem_inc(pool_waited, 1)

            last_row(lookup)
            with pool.Fori(0, NCH // 2) as i:
                for s in (0, 1):
                    pool.tensor_copy(idxs[:, s, :], cols(srcI, 2 * i + s)).then_inc(pool_step, 1)
                    pool.wait_ge(pool_step, r_step.more(1))
                    pool.sem_inc(pool_waited, 1)
                    last_row(lookup)
                    for j in range(CH):
                        gather(look[:, s, j, :], lookup, idxs[:, s, j:j + 1], looked[s])
                for s in (0, 1):
                    c = 2 * i + s
                    pool.wait_ge(looked[s], r_lk[s].more(16 * CH))
                    pool.sem_inc(pool_waited, 1)
                    pool.tensor_copy(cols(idxA, c), look[:, s, :, 0])
                    pool.tensor_copy(cols(dnE, c), look[:, s, :, 1])
                    pool.tensor_copy(cols(snE, c), look[:, s, :, 2]).then_inc(pool_step, 1)
                    pool.wait_ge(pool_step, r_step.more(1))
                    pool.sem_inc(pool_waited, 1)
            pool.sem_inc(look_done, 1)

            def sweep(table, idx, W, done=gathered):
                with pool.Fori(0, NCH // 2) as i:
                    for s in (0, 1):
                        pool.wait_ge(used[s], r_used[s].reg)
                        pool.sem_inc(pool_waited, 1)
                        r_used[s].skip(1)
                        pool.wait_ge(raw_stored[s], r_raw[s].reg)
                        pool.sem_inc(pool_waited, 1)
                        r_raw[s].skip(16)
                        pool.tensor_copy(idxs[:, s, :], cols(idx, 2 * i + s)).then_inc(pool_step, 1)
                        pool.wait_ge(pool_step, r_step.more(1))
                        pool.sem_inc(pool_waited, 1)
                        last_row(table)
                        for j in range(CH):
                            gather(G[:, s, j, 0:W], table, idxs[:, s, j:j + 1], done[s])

            def front_sums(table, col, W):
                for s in (0, 1):
                    pool.wait_ge(raw_stored[s], r_raw[s].reg)
                    pool.sem_inc(pool_waited, 1)
                last_row(table)
                gather(FR[:, 0, 0:W], table, fidx[:, col:col + 1], f_gathered)

            def front_rows(table, col, frm):
                pool.wait_ge(f_ready, r_fr.more(1))
                pool.sem_inc(pool_waited, 1)
                last_row(table)
                scatter(table, fidx[:, col:col + 1], frm, f_stored)
                pool.wait_ge(f_stored, r_fs.more(16))
                pool.sem_inc(pool_waited, 1)

            r_fs.skip(0)
            r_stored = {k: Reached(pool, f"pool_stored_{k}") for k in "abcde"}
            front_rows(tab_a, F_TAB_W, fown[:, 0, :])
            pool.wait_ge(stored["a"], r_stored["a"].more(16 * NCH))
            pool.sem_inc(pool_waited, 1)
            pool.wait_ge(dense_stored["a"][0], 16 * NT // 2)
            pool.wait_ge(dense_stored["a"][1], 16 * NT // 2)
            pool.sem_inc(pool_waited, 1)
            pool.wait_ge(dense_stored["d"][1], 16 * NT // 2)
            pool.sem_inc(pool_waited, 1)
            sweep(tab_a, idxA, D)
            front_sums(raw, F_SEAT, D)
            front_rows(tab_b, F_TAB_W, rowsB[:, 0, :])
            pool.wait_ge(stored["b"], r_stored["b"].more(16 * NCH))
            pool.sem_inc(pool_waited, 1)
            pool.wait_ge(dense_stored["b"][0], 16 * NT // 2)
            pool.wait_ge(dense_stored["b"][1], 16 * NT // 2)
            pool.sem_inc(pool_waited, 1)
            sweep(tab_b, idxA, D)
            front_sums(raw, F_SEAT, D)
            front_rows(tab_c, F_TAB_W, rowsC[:, 0, :])
            pool.wait_ge(stored["c"], r_stored["c"].more(16 * NCH))
            pool.sem_inc(pool_waited, 1)
            pool.wait_ge(dense_stored["c"][0], 16 * NT // 2)
            pool.wait_ge(dense_stored["c"][1], 16 * NT // 2)
            pool.sem_inc(pool_waited, 1)
            sweep(tab_c, idxA, D)
            front_sums(raw, F_SEAT, D)
            front_rows(tab_d, F_TAB_W, rowsD[:, 0, :])
            pool.wait_ge(stored["d"], r_stored["d"].more(16 * NCH))
            pool.sem_inc(pool_waited, 1)
            pool.wait_ge(dense_stored["d"][0], 16 * NT // 2)
            pool.wait_ge(dense_stored["d"][1], 16 * NT // 2)
            pool.sem_inc(pool_waited, 1)
            pool.wait_ge(zeros_stored, 64)
            pool.wait_ge(step_done, r_sd.more(1))
            pool.sem_inc(pool_waited, 1)
            with pool.Fori(0, K2 // 2):
                sweep(tab_d, idxC, AW)
                pool.wait_ge(step_done, r_sd.more(1))
                pool.sem_inc(pool_waited, 1)
                front_sums(alt_d, F_SEAT, AW)
                front_rows(alt_d, F_SEAT_W, FR[:, 0, :])
                sweep(alt_d, seatI, AW)
                front_sums(tab_d, F_TAB, AW)
                front_rows(tab_d, F_TAB_W, FR[:, 0, :])
            front_rows(tab_e, F_TAB_W, rowsE[:, 0, :])
            pool.wait_ge(stored["e"], r_stored["e"].more(16 * NCH))
            pool.sem_inc(pool_waited, 1)
            pool.wait_ge(dense_stored["e"][0], 16 * NT // 2)
            pool.wait_ge(dense_stored["e"][1], 16 * NT // 2)
            pool.sem_inc(pool_waited, 1)
            pool.wait_ge(step_done, r_sd.more(1))
            pool.sem_inc(pool_waited, 1)
            with pool.Fori(0, K3 // 2):
                sweep(tab_e, idxC, D, gathered3)
                pool.wait_ge(step_done, r_sd.more(1))
                pool.sem_inc(pool_waited, 1)
                front_sums(alt_e, F_SEAT, D)
                front_rows(alt_e, F_SEAT_W, FR[:, 0, 0:D])
                sweep(alt_e, seatI, D, gathered3)
                front_sums(tab_e, F_TAB, D)
                front_rows(tab_e, F_TAB_W, FR[:, 0, 0:D])

            for s in (0, 1):
                pool.wait_ge(out_stored[s], 16 * NT // 2)
            r_fin = [Reached(pool, f"pool_fin{s}") for s in (0, 1)]
            last_row(out)
            with pool.Fori(0, NCH // 2) as i:
                for s in (0, 1):
                    pool.wait_ge(final_ready[s], r_fin[s].more(1))
                    pool.sem_inc(pool_waited, 1)
                    pool.wait_ge(scattered[s], r_sc[s].reg)
                    pool.sem_inc(pool_waited, 1)
                    r_sc[s].skip(16 * CH)
                    pool.tensor_copy(idxs[:, s, :], cols(dst_out, 2 * i + s)).then_inc(pool_step, 1)
                    pool.wait_ge(pool_step, r_step.more(1))
                    pool.sem_inc(pool_waited, 1)
                    last_row(out)
                    for j in range(CH):
                        scatter(out, idxs[:, s, j:j + 1], G[:, s, j, 0:D], scattered[s])
            scatter(out, fidx[:, F_OUT:F_OUT + 1], X[:, FC, :], final_stored)
            for s in (0, 1):
                pool.wait_ge(scattered[s], r_sc[s].reg)
                pool.sem_inc(pool_waited, 1)
            pool.wait_ge(final_stored, 16)
            pool.wait_ge(look_stored, 16)

        @block.scalar
        def _(act):
            r_var = Reached(act, "act_var")
            r_rows = Reached(act, "act_rows")
            r_raw = Reached(act, "act_raw")
            r_rt = Reached(act, "act_rt")
            r_hid = Reached(act, "act_hid")
            r_dif = Reached(act, "act_dif")

            def root(R):
                act.wait_ge(var_ready, r_var.more(1))
                nc.scalar.activation(lnw[:, 4, 0:R], lnw[:, 3, 0:R], ACT.Sqrt, bias=lneps[:, 0:1],
                                     scale=1.0 / D).then_inc(sd_ready, 1)

            def turn_copy(R, T=TR):
                act.wait_ge(rowsT_ready, r_rt.more(1))
                q = R // 2
                for a, b in ((0, min(q, 4)), (4, q)):
                    if b > a:
                        last = nc.scalar.activation(hT[:, a:b, :].rearrange("p a b -> p (a b)"),
                                                    T[:, a * P:b * P], ACT.Copy)
                last.then_inc(rowsT_copied, 1)

            def hidden_relu(R):
                act.wait_ge(hid_ready, r_hid.more(1))
                q = R // 2
                for h in (0, 1):
                    for g, (a, b) in enumerate(((0, min(q, 4)), (4, q))):
                        if b > a:
                            last = nc.scalar.activation(U[:, h, a:b, :].rearrange("p a b -> p (a b)"),
                                                        HP[:, 2 * h + g, 0:(b - a) * P], ACT.Relu,
                                                        bias=b3c[:, 0:1])
                last.then_inc(hid_copied, 1)

            def hidden(R):
                turn_copy(R)
                hidden_relu(R)

            def store_rows(to, frm, s):
                act.wait_ge(rows_ready, r_rows.more(1))
                act.dma_start(to, frm).then_inc(s, 16)

            def store_raw(to, s, W):
                act.wait_ge(raw_ready, r_raw.more(1))
                act.dma_start(to, G[:, s, :, 0:W]).then_inc(raw_stored[s], 16)

            def exps():
                act.wait_ge(dif_ready, r_dif.more(1))
                nc.scalar.activation(expd[:, :], dif[:, :], ACT.Exp).then_inc(exp_ready, 1)

            act.wait_ge(var_ready, r_var.more(1))
            nc.scalar.activation(tmpB[:, :], tmpA[:, :], ACT.Sqrt).then_inc(sd_ready, 1)
            act.wait_ge(var_ready, r_var.more(1))
            nc.scalar.activation(tmpB[:, :], tmpA[:, :], ACT.Sqrt, bias=1.0).then_inc(sd_ready, 1)
            act.wait_ge(var_ready, r_var.more(1))
            nc.scalar.activation(hist[0:NHI, :], hist[0:NHI, :], ACT.Sqrt).then_inc(sd_ready, 1)
            act.wait_ge(look_stored, 16)
            with act.Fori(0, NCH) as c:
                root(CH)
                store_rows(seats(tab_a, N, c), rowsA[:, :, :], stored["a"])
            root(2)

            r_be = [Reached(act, f"act_be{s}") for s in (0, 1)]
            r_conv = Reached(act, "act_conv")
            r_cc = Reached(act, "act_cc")

            def conv_rows(s):
                act.wait_ge(dense_stored["e"][s], r_be[s].reg)
                r_be[s].skip(16)
                act.wait_ge(conv_ready, r_conv.more(1))
                nc.scalar.activation(row_be[s][:, :, :].rearrange("p a b -> p (a b)"),
                                     TR_OF[s][:, 0:CH * D], ACT.Copy).then_inc(conv_copied, 1)
                act.wait_ge(conv_copied, r_cc.more(1))

            def dense_a(s, first):
                root(CH)
                store_rows(nodes(tab_a, first), row_ac[s][:, :, :], dense_stored["a"][s])
                turn_copy(CH, TR_OF[s])

            def dense_c(s, first):
                root(CH)
                store_rows(nodes(tab_c, first), row_ac[s][:, :, :], dense_stored["c"][s])
                turn_copy(CH, TR_OF[s])
                r_conv.skip(1)

            def dense_de(s, first, o, first_o):
                root(CH)
                if o is not None:
                    hidden_relu(CH)
                store_rows(nodes(tab_d, first), row_d[s][:, :, :], dense_stored["d"][s])
                root(CH)
                if o is not None:
                    conv_rows(o)
                    act.dma_start(nodes(tab_b, first_o), row_be[o][:, :, :]).then_inc(dense_stored["b"][o], 16)
                store_rows(nodes(tab_e, first), row_be[s][:, :, :], dense_stored["e"][s])
                act.dma_start(nodes(out, first), xin[:, s, :, :]).then_inc(out_stored[s], 16)

            dense_a(0, TILES[0])
            hidden_relu(CH)
            conv_rows(0)
            act.dma_start(nodes(tab_b, TILES[0]), row_be[0][:, :, :]).then_inc(dense_stored["b"][0], 16)
            dense_c(0, TILES[0])
            dense_a(1, TILES[1])
            dense_de(0, TILES[0], 1, TILES[1])
            dense_c(1, TILES[1])
            with act.Fori(1, NT // 2 - 1) as i:
                dense_a(0, 2 * i * TILE)
                dense_de(1, (2 * i - 1) * TILE, 0, 2 * i * TILE)
                dense_c(0, 2 * i * TILE)
                dense_a(1, (2 * i + 1) * TILE)
                dense_de(0, 2 * i * TILE, 1, (2 * i + 1) * TILE)
                dense_c(1, (2 * i + 1) * TILE)
            dense_a(0, TILES[NT - 2])
            dense_de(1, TILES[NT - 3], 0, TILES[NT - 2])
            dense_c(0, TILES[NT - 2])
            act.wait_ge(dense_stored["a"][0], 16 * NT // 2)
            act.wait_ge(dense_stored["b"][0], 16 * NT // 2)
            dense_a(1, TILES[NT - 1])
            dense_de(0, TILES[NT - 2], 1, TILES[NT - 1])
            act.wait_ge(dense_stored["c"][0], 16 * NT // 2)
            dense_c(1, TILES[NT - 1])
            act.wait_ge(dense_stored["d"][0], 16 * NT // 2)
            act.wait_ge(dense_stored["e"][0], 16 * NT // 2)
            act.wait_ge(out_stored[0], 16 * NT // 2)
            dense_de(1, TILES[NT - 1], None, None)

            with act.Fori(0, NCH // 2) as i:
                for s in (0, 1):
                    store_raw(seats(raw, 0, 2 * i + s), s, D)
                    hidden(CH)
                    store_rows(seats(tab_b, N, 2 * i + s), rowsB[:, :, :], stored["b"])
            hidden(2)
            with act.Fori(0, NCH // 2) as i:
                for s in (0, 1):
                    store_raw(seats(raw, 0, 2 * i + s), s, D)
                    root(CH)
                    store_rows(seats(tab_c, N, 2 * i + s), rowsC[:, :, :], stored["c"])
            root(2)
            with act.Fori(0, NCH // 2) as i:
                for s in (0, 1):
                    store_raw(seats(raw, 0, 2 * i + s), s, D)
                    turn_copy(CH)
                    root(CH)
                    store_rows(seats(tab_d, N, 2 * i + s), rowsD[:, :, :], stored["d"])
            turn_copy(2)
            root(2)

            with act.Fori(0, K2 // 2):
                for table, first in ((alt_d, 0), (tab_d, N)):
                    with act.Fori(0, NCH // 2) as i:
                        for s in (0, 1):
                            exps()
                            store_raw(seats(table, first, 2 * i + s), s, AW)
                    act.wait_ge(dif_ready, r_dif.more(1))
                    nc.scalar.activation(ET[0:AW, :, :], DT[0:AW, :, :], ACT.Exp).then_inc(exp_ready, 1)
                    act.wait_ge(dif_ready, r_dif.more(1))
                    nc.scalar.activation(fm[:, 6:8], fm[:, 4:6], ACT.Exp).then_inc(exp_ready, 1)
            with act.Fori(0, NCH) as c:
                root(CH)
                store_rows(seats(tab_e, N, c), rowsE[:, :, :], stored["e"])
            root(2)
            with act.Fori(0, K3 // 2):
                for table, first in ((alt_e, 0), (tab_e, N)):
                    with act.Fori(0, NCH // 2) as i:
                        for s in (0, 1):
                            store_raw(seats(table, first, 2 * i + s), s, D)

        @block.tensor
        def _(pe):
            r_rows = Reached(pe, "pe_rows")
            r_mix = Reached(pe, "pe_mix")
            r_rt = Reached(pe, "pe_rt")
            r_hid = Reached(pe, "pe_hid")
            r_turn = Reached(pe, "pe_turn")
            r_hot = Reached(pe, "pe_hot")
            r_hu = Reached(pe, "pe_hu")

            def turn(rows, R, T=TR):
                for q in range(R // 2):
                    last = nc.tensor.transpose(T[:, q * P:(q + 1) * P],
                                               rows[:, 2 * q:2 * q + 2, :].rearrange("p a b -> p (a b)"),
                                               ident[:, :])
                last.then_inc(rowsT_ready, 1)
                pe.wait_ge(rowsT_copied, r_rt.more(1))
                pe.sem_inc(pe_waited, 1)

            def hidden(rows, R, T=TR):
                turn(rows, R, T)
                q = R // 2
                for h in (0, 1):
                    for g, (a, b) in enumerate(((0, min(q, 4)), (4, q))):
                        if b > a:
                            last = nc.tensor.matmul(HP[:, 2 * h + g, 0:(b - a) * P],
                                                    w3T[h * D:(h + 1) * D, :],
                                                    hT[h * D:(h + 1) * D, a:b, :].rearrange("p a b -> p (a b)"),
                                                    start=True, stop=True)
                last.then_inc(hid_ready, 1)
                pe.wait_ge(hid_copied, r_hid.more(1))
                pe.sem_inc(pe_waited, 1)
                for r in range(R):
                    last = nc.tensor.matmul(T[:, r * D:(r + 1) * D], U[:, r % 2, r // 2, :], w4T[:, :],
                                            start=True, stop=True)
                last.then_inc(conv_ready, 1)

            def linear(rows, R, T=TR, w=w1T):
                turn(rows, R, T)
                for r in range(R):
                    h = r % 2
                    at = h * 512 + r // 2 * D
                    last = nc.tensor.matmul(T[:, at:at + D], hT[h * D:(h + 1) * D, r // 2, :],
                                            w[h * D:(h + 1) * D, :], start=True, stop=True)
                last.then_inc(conv_ready, 1)

            def turn_one(to, frm, n):
                pe.wait_ge(to_turn, r_turn.more(1))
                pe.sem_inc(pe_waited, 1)
                nc.tensor.transpose(to, frm, ident[0:n, 0:n]).then_inc(turned, 1)

            pe.wait_ge(iotas, 1)
            pe.wait_ge(loaded, 16 * 20)
            nc.tensor.transpose(TR[:, 0:P], w3[:, :, :].rearrange("p a b -> p (a b)"), ident[:, :])
            nc.tensor.transpose(TR[:, P:P + D], w4[:, :], ident[0:D, 0:D])
            nc.tensor.transpose(TR[:, 2 * P:2 * P + D], w1[:, :, :].rearrange("p a b -> p (a b)"),
                                ident[0:D, 0:D]).then_inc(weightsT, 1)
            for _ in range(2):
                turn_one(MI[:, 0:P], allcT[:, :], P)
            turn_one(MI[0:1, 0:P], noend[:, :], P)
            turn_one(MI[0:1, 0:P], fm[:, 0:1], P)
            turn_one(MI[:, 128:129], row[:, 1, 0:P], 1)
            with pe.Fori(0, NCH):
                pe.wait_ge(hist_used, r_hu.reg)
                pe.sem_inc(pe_waited, 1)
                r_hu.skip(1)
                for j in range(CH):
                    pe.wait_ge(hot_ready, r_hot.more(1))
                    pe.sem_inc(pe_waited, 1)
                    for h in (0, 1):
                        last = nc.tensor.matmul(HI[0:NHI, h, :], hot_hi[:, j % 2, 0:NHI],
                                                hot_lo[:, j % 2, h * 512:(h + 1) * 512],
                                                start=(j == 0), stop=(j == CH - 1))
                    last.then_inc(hot_used, 1)
            pe.wait_ge(wcopied, 1)
            r_rows.skip(NCH)
            def dense_products(s):
                pe.wait_ge(rows_ready, r_rows.more(1))
                pe.sem_inc(pe_waited, 1)
                hidden(row_ac[s], CH, TR_OF[s])

            def dense_linear(s):
                pe.wait_ge(rows_ready, r_rows.more(1))
                pe.sem_inc(pe_waited, 1)
                linear(row_ac[s], CH, TR_OF[s], w1Te)

            dense_products(0)
            dense_linear(0)
            dense_products(1)
            r_rows.skip(2)
            dense_linear(1)
            with pe.Fori(0, NT // 2 - 1):
                dense_products(0)
                r_rows.skip(2)
                dense_linear(0)
                dense_products(1)
                r_rows.skip(2)
                dense_linear(1)

            def carry_turns(W):
                turn_one(MI[0:W, 0:P], carry[:, 0:W], P)
                turn_one(MI[:, 128:128 + W], IT[0:W, :], W)

            with pe.Fori(0, NCH):
                pe.wait_ge(mixed_ready, r_mix.more(1))
                pe.sem_inc(pe_waited, 1)
                hidden(agg, CH)
            carry_turns(D)
            pe.wait_ge(mixed_ready, r_mix.more(1))
            pe.sem_inc(pe_waited, 1)
            hidden(agg, 2)
            carry_turns(D)
            with pe.Fori(0, NCH):
                pe.wait_ge(mixed_ready, r_mix.more(1))
                pe.sem_inc(pe_waited, 1)
                linear(agg, CH)
            carry_turns(D)
            pe.wait_ge(mixed_ready, r_mix.more(1))
            pe.sem_inc(pe_waited, 1)
            linear(agg, 2)

            def spread_turns():
                turn_one(MI[0:1, 0:P], fm[:, 0:1], P)
                turn_one(MI[:, 128:129], row[:, 1, 0:P], 1)

            spread_turns()
            with pe.Fori(0, K2):
                turn_one(MI[0:AW, 0:P], mrep[:, :], P)
                turn_one(MI[0:AW, 0:P], carry[:, :], P)
                turn_one(MI[:, 128:128 + AW], IT[0:AW, :], AW)
                turn_one(MI[:, 256:256 + AW], TF[0:AW, 0:P], AW)
                spread_turns()
            with pe.Fori(0, K3):
                carry_turns(D)

        @block.vector
        def _(dve):
            v = nc.vector
            r_sd = Reached(dve, "dve_sd")
            r_exp = Reached(dve, "dve_exp")
            r_conv = Reached(dve, "dve_conv")
            r_turned = Reached(dve, "dve_turned")
            r_stored = {k: Reached(dve, f"dve_st_{k}") for k in "abcde"}
            r_gat = [Reached(dve, f"dve_gat{s}") for s in (0, 1)]
            r_gat3 = [Reached(dve, f"dve_gat3_{s}") for s in (0, 1)]
            r_own = [Reached(dve, f"dve_own{s}") for s in (0, 1)]
            r_ea = [Reached(dve, f"dve_ea{s}") for s in (0, 1)]
            r_xl = [Reached(dve, f"dve_xl{s}") for s in (0, 1)]
            r_fg = Reached(dve, "dve_fg")
            r_hot = Reached(dve, "dve_hot")
            r_fs = Reached(dve, "dve_fs")
            steps = [0]

            def nth():
                steps[0] += 1
                return steps[0]

            def fresh():
                dve.sem_clear(dve_step)
                steps[0] = 0

            v.memset(srcI[:, :], -1)
            v.memset(dstI[:, :], PAD)
            v.memset(nextI[:, :], PAD)
            v.memset(prevI[:, :], PAD).then_inc(dve_step, 1)
            dve.wait_ge(dve_step, nth())
            dve.sem_inc(cleared, 1)
            v.memset(zrow[:, :], 0.0).then_inc(dve_step, 1)
            dve.wait_ge(dve_step, nth())
            v.memset(zrow[:, AW - 1:AW], 1.0).then_inc(dve_step, 1)
            dve.wait_ge(dve_step, nth())
            dve.sem_inc(zeros_ready, 1)
            for k, w in enumerate(mix):
                v.memset(mixb[:, k:k + 1], w)
            v.memset(lneps[:, :], LN_EPS)
            v.memset(rowsD[:, :, AW - 1:AW], 1.0)
            v.memset(FR[:, :, :], 0.0)
            v.memset(X[:, FC + 1:XC, :], 0.0)
            v.memset(dinv[:, :], 0.0)
            v.memset(dnorm[:, :], 0.0)
            v.memset(fm[:, :], 0.0)
            v.memset(hist[:, :], 0.0).then_inc(dve_step, 1)
            dve.wait_ge(dve_step, nth())
            dve.wait_ge(loaded, 16 * 20)
            dve.wait_ge(iotas, 1)

            v.tensor_tensor(cont[:, :], dstI[:, :], prevI[:, :], ALU.is_equal)
            v.tensor_tensor(goes[:, :], dstI[:, :], nextI[:, :], ALU.is_equal)
            v.tensor_scalar(dst_gat[:, :], dstI[:, :], N - 1, None, ALU.min)
            v.tensor_scalar(eps1[:, :], eps1[:, :], 1.0, None, ALU.add)
            v.tensor_copy(place[:, :], placeI[:, :]).then_inc(dve_step, 1)
            dve.wait_ge(dve_step, nth())
            v.tensor_copy(c0[:, :], cont[:, 0:1]).then_inc(dve_step, 1)
            dve.wait_ge(dve_step, nth())
            v.memset(cont[:, 0:1], 0.0)
            v.tensor_scalar(ends[:, :], goes[:, :], -1.0, 1.0, ALU.mult, ALU.add)
            v.memset(tmpB[:, :], 0.0).then_inc(dve_step, 1)
            dve.wait_ge(dve_step, nth())
            v.tensor_tensor_scan(tmpA[:, :], goes[:, :], tmpB[:, :], 1.0, ALU.mult, ALU.add)
            v.tensor_tensor_scan(after[:, ::-1], goes[:, ::-1], tmpB[:, ::-1], 1.0, ALU.mult, ALU.add)
            v.tensor_scalar(pen[:, :], cont[:, :], -NEG, NEG, ALU.mult, ALU.add).then_inc(dve_step, 1)
            dve.wait_ge(dve_step, nth())
            v.tensor_scalar(front[:, 0:1], tmpA[:, 0:1], -1.0, 1.0, ALU.mult, ALU.add)
            v.tensor_tensor(front[:, 1:COLS], tmpA[:, 0:COLS - 1], tmpA[:, 1:COLS], ALU.subtract)
            v.tensor_tensor(allc[:, :], tmpA[:, COLS - 2:COLS - 1], c0[:, :], ALU.mult)
            v.tensor_copy(noend[:, :], tmpA[:, COLS - 1:COLS]).then_inc(dve_step, 1)
            dve.wait_ge(dve_step, nth())
            v.tensor_scalar(front[:, :], front[:, :], c0[:, 0:1], None, ALU.mult).then_inc(dve_step, 1)
            dve.wait_ge(dve_step, nth())

            def at_front(to, arr):
                v.tensor_tensor(tmpA[:, :], front[:, :], arr, ALU.mult).then_inc(dve_step, 1)
                dve.wait_ge(dve_step, nth())
                v.tensor_reduce(to, tmpA[:, :], AXX, ALU.add).then_inc(dve_step, 1)
                dve.wait_ge(dve_step, nth())

            v.tensor_reduce(fr[:, 0:1], front[:, :], AXX, ALU.add).then_inc(dve_step, 1)
            dve.wait_ge(dve_step, nth())
            at_front(fr[:, 1:2], place[:, :])
            at_front(fr[:, 2:3], dstI[:, :])
            v.tensor_scalar(fr[:, 3:4], fr[:, 0:1], -1.0, 1.0, ALU.mult, ALU.add).then_inc(dve_step, 1)
            dve.wait_ge(dve_step, nth())
            v.scalar_tensor_tensor(fr[:, 4:5], fr[:, 3:4], place[:, 0:1], fr[:, 1:2], ALU.mult, ALU.add).then_inc(dve_step, 1)
            dve.wait_ge(dve_step, nth())
            v.scalar_tensor_tensor(fr[:, 5:6], fr[:, 3:4], float(BIG), fr[:, 4:5], ALU.mult, ALU.add).then_inc(dve_step, 1)
            dve.wait_ge(dve_step, nth())
            v.tensor_copy(fidx[:, F_DST:F_DST + 1], fr[:, 2:3])
            v.tensor_copy(fidx[:, F_SEAT:F_SEAT + 1], fr[:, 4:5])
            v.tensor_copy(fidx[:, F_SEAT_W:F_SEAT_W + 1], fr[:, 5:6])
            v.tensor_scalar(fidx[:, F_TAB:F_TAB + 1], fr[:, 4:5], float(N), None, ALU.add)
            v.tensor_scalar(fidx[:, F_TAB_W:F_TAB_W + 1], fr[:, 5:6], float(N), None, ALU.add)
            v.scalar_tensor_tensor(fidx[:, F_OUT:F_OUT + 1], fr[:, 3:4], float(BIG), fr[:, 2:3],
                                   ALU.mult, ALU.add).then_inc(dve_step, 1)
            dve.wait_ge(dve_step, nth())
            v.tensor_scalar(tmpA[:, :], goes[:, :], float(BIG), None, ALU.mult).then_inc(dve_step, 1)
            dve.wait_ge(dve_step, nth())
            v.scalar_tensor_tensor(dst_tab[:, :], dstI[:, :], 2.0, tmpA[:, :], ALU.mult, ALU.add).then_inc(dve_step, 1)
            dve.wait_ge(dve_step, nth())
            v.scalar_tensor_tensor(tmpA[:, :], front[:, :], float(BIG), tmpA[:, :], ALU.mult, ALU.add).then_inc(dve_step, 1)
            dve.wait_ge(dve_step, nth())
            v.tensor_tensor(dst_out[:, :], dstI[:, :], tmpA[:, :], ALU.add).then_inc(dve_step, 1)
            dve.wait_ge(dve_step, nth())
            dve.sem_inc(masks, 1)

            dve.wait_ge(weightsT, 1)
            v.tensor_copy(w3T[:, :], TR[:, 0:P])
            v.tensor_copy(w4T[:, :], TR[:, P:P + D])
            v.tensor_copy(w1T[:, :], TR[:, 2 * P:2 * P + D])
            v.tensor_scalar(w1Te[:, :], TR[:, 2 * P:2 * P + D], eps1[:, 0:1], None, ALU.mult).then_inc(dve_step, 1)
            dve.wait_ge(dve_step, nth())
            dve.sem_inc(wcopied, 1)

            def to_pe():
                dve.sem_inc(to_turn, 1)
                dve.wait_ge(turned, r_turned.more(1))

            v.tensor_copy(allcT[:, :], c0[:, 0:1].to_broadcast([P, P])).then_inc(dve_step, 1)
            dve.wait_ge(dve_step, nth())
            to_pe()
            v.tensor_copy(c0T[:, :], MI[:, 0:P])
            v.tensor_copy(allcT[:, :], allc[:, 0:1].to_broadcast([P, P])).then_inc(dve_step, 1)
            dve.wait_ge(dve_step, nth())
            to_pe()
            v.tensor_copy(allcT[:, :], MI[:, 0:P]).then_inc(dve_step, 1)
            dve.wait_ge(dve_step, nth())
            to_pe()
            v.tensor_copy(noendT[:, :], MI[0:1, 0:P]).then_inc(dve_step, 1)
            dve.wait_ge(dve_step, nth())

            v.memset(row[:, :, :], 0.0)
            v.memset(tmpB[:, :], 1.0).then_inc(dve_step, 1)
            dve.wait_ge(dve_step, nth())
            v.tensor_tensor_scan(tmpA[:, :], cont[:, :], tmpB[:, :], 0.0, ALU.mult, ALU.add).then_inc(dve_step, 1)
            dve.wait_ge(dve_step, nth())
            v.tensor_copy(fm[:, 0:1], tmpA[:, COLS - 1:COLS]).then_inc(dve_step, 1)
            dve.wait_ge(dve_step, nth())
            to_pe()
            v.tensor_tensor_scan(row[:, 0, 1:P + 1], allcT[0:1, :], MI[0:1, 0:P], 0.0, ALU.mult, ALU.add).then_inc(dve_step, 1)
            dve.wait_ge(dve_step, nth())
            v.tensor_tensor(row[:, 1, 0:P], row[:, 0, 0:P], c0T[0:1, :], ALU.mult).then_inc(dve_step, 1)
            dve.wait_ge(dve_step, nth())
            to_pe()
            v.tensor_copy(fm[:, 1:2], MI[:, 128:129]).then_inc(dve_step, 1)
            dve.wait_ge(dve_step, nth())
            v.scalar_tensor_tensor(tmpA[:, :], front[:, :], fm[:, 1:2], tmpA[:, :], ALU.mult, ALU.add).then_inc(dve_step, 1)
            dve.wait_ge(dve_step, nth())
            dve.sem_inc(var_ready, 1)
            dve.wait_ge(sd_ready, r_sd.more(1))
            v.reciprocal(dnorm[:, 0:COLS], tmpB[:, :]).then_inc(dve_step, 1)
            dve.wait_ge(dve_step, nth())
            dve.sem_inc(var_ready, 1)
            dve.wait_ge(sd_ready, r_sd.more(1))
            v.reciprocal(dinv[:, 0:COLS], tmpB[:, :]).then_inc(dve_step, 1)
            dve.wait_ge(dve_step, nth())
            at_front(dnorm[:, FC:FC + 1], dnorm[:, 0:COLS])
            at_front(dinv[:, FC:FC + 1], dinv[:, 0:COLS])
            v.tensor_scalar(place[:, :], place[:, :], float(N), None, ALU.add).then_inc(dve_step, 1)
            dve.wait_ge(dve_step, nth())

            v.tensor_single_scalar(nextI[:, :], srcI[:, :], LOB.bit_length() - 1,
                                   op=ALU.arith_shift_right).then_inc(dve_step, 1)
            dve.wait_ge(dve_step, nth())
            v.tensor_single_scalar(prevI[:, :], srcI[:, :], LOB - 1, op=ALU.bitwise_and).then_inc(dve_step, 1)
            dve.wait_ge(dve_step, nth())
            r_hist = Reached(dve, "dve_hist")
            r_hot_at = [None]
            with dve.Fori(0, NCH) as c:
                fresh()
                v.tensor_copy(chn[:, 0, :], cols(nextI, c))
                v.tensor_copy(chn[:, 1, :], cols(prevI, c)).then_inc(dve_step, 1)
                dve.wait_ge(dve_step, nth())
                for j in range(CH):
                    if j >= 2:
                        dve.wait_ge(hot_used, r_hot.more(1))
                    v.tensor_scalar(hot_hi[:, j % 2, 0:P], iota16[:, 0:P], chn[:, 0, j:j + 1], None,
                                    ALU.is_equal)
                    v.tensor_scalar(hot_lo[:, j % 2, :], iota16[:, :], chn[:, 1, j:j + 1], None,
                                    ALU.is_equal).then_inc(dve_step, 1)
                    dve.wait_ge(dve_step, nth())
                    dve.sem_inc(hot_ready, 1)
                dve.wait_ge(hot_used, r_hot.more(2))
                v.tensor_tensor(hist[0:NHI, :], hist[0:NHI, :],
                                HI[0:NHI, :, :].rearrange("p a b -> p (a b)"), ALU.add).then_inc(dve_step, 1)
                dve.wait_ge(dve_step, nth())
                dve.sem_inc(hist_used, 1)
            v.tensor_scalar(srcI[:, :], srcI[:, :], 0, None, ALU.max)
            v.tensor_copy(lookI[:, :, 0], iotaN)
            v.tensor_scalar(hist[:, :], hist[:, :], 1.0, None, ALU.max).then_inc(dve_step, 1)
            dve.wait_ge(dve_step, nth())
            dve.sem_inc(var_ready, 1)
            v.memset(lookI[:, :, 3], 0.0)
            dve.wait_ge(sd_ready, r_sd.more(1))
            v.reciprocal(lookI[0:NHI, :, 2], hist[0:NHI, :]).then_inc(dve_step, 1)
            dve.wait_ge(dve_step, nth())
            v.memset(hist[:, :], 1.0).then_inc(dve_step, 1)
            dve.wait_ge(dve_step, nth())
            dve.sem_inc(look_ready, 1)
            dve.sem_inc(masks, 1)

            def norm(xr, to, R):
                m_sum, m_dif, m2, var, sd, rs = (lnw[:, k, 0:R] for k in range(6))
                for r in range(R):
                    last = v.bn_stats(st[:, r, :], xr[:, r, :])
                last.then_inc(dve_step, 1)
                dve.wait_ge(dve_step, nth())
                v.tensor_tensor(m_sum, st[:, 0:R, 1], st[:, 0:R, 4], ALU.add)
                v.tensor_tensor(m2, st[:, 0:R, 2], st[:, 0:R, 5], ALU.add)
                v.tensor_tensor(m_dif, st[:, 0:R, 1], st[:, 0:R, 4], ALU.subtract).then_inc(dve_step, 1)
                dve.wait_ge(dve_step, nth())
                v.tensor_tensor(m_dif, m_dif, m_dif, ALU.mult).then_inc(dve_step, 1)
                dve.wait_ge(dve_step, nth())
                v.scalar_tensor_tensor(var, m_dif, D / 4.0, m2, ALU.mult, ALU.add).then_inc(dve_step, 1)
                dve.wait_ge(dve_step, nth())
                dve.sem_inc(var_ready, 1)
                v.scalar_tensor_tensor(xm[:, 0:R, :], wide(m_sum), -0.5, xr, ALU.mult, ALU.add)
                dve.wait_ge(sd_ready, r_sd.more(1))
                v.reciprocal(rs, sd).then_inc(dve_step, 1)
                dve.wait_ge(dve_step, nth())
                v.scalar_tensor_tensor(to, xm[:, 0:R, :], 0.0, wide(rs), ALU.max, ALU.mult).then_inc(dve_step, 1)
                dve.wait_ge(dve_step, nth())

            def xcols(c):
                return X[:, ds(c * CH, CH), :]

            def attention_row(to, xr, R):
                for k in (0, 1):
                    v.tensor_tensor(xm[:, 0:R, :], to[:, :, 0:D], flat_rows(attn[:, k * D:(k + 1) * D], R),
                                    ALU.mult).then_inc(dve_step, 1)
                    dve.wait_ge(dve_step, nth())
                    v.tensor_reduce(to[:, :, D + k:D + k + 1], xm[:, 0:R, :], AXX, ALU.add).then_inc(dve_step, 1)
                    dve.wait_ge(dve_step, nth())
                v.scalar_tensor_tensor(xr, to[:, :, 0:D], tempb[:, 0:1], xr, ALU.mult, ALU.add).then_inc(dve_step, 1)
                dve.wait_ge(dve_step, nth())

            def stage_a(xr, dv, R, ready):
                norm(xr, rowsA[:, 0:R, :], R)
                v.tensor_tensor(rowsA[:, 0:R, :], rowsA[:, 0:R, :], wide(dv), ALU.mult).then_inc(dve_step, 1)
                dve.wait_ge(dve_step, nth())
                dve.sem_inc(ready, 1)

            for s in (0, 1):
                dve.wait_ge(x_kept[s], 16 * NCH // 2)
                r_gat[s].skip(16 * CH * (NCH // 2))
            dve.wait_ge(front_x, 16)
            with dve.Fori(0, NCH) as c:
                fresh()
                v.tensor_copy(chn[:, 0, :], dinv[:, ds(c * CH, CH)]).then_inc(dve_step, 1)
                dve.wait_ge(dve_step, nth())
                dve.wait_ge(stored["a"], r_stored["a"].reg)
                r_stored["a"].skip(16)
                stage_a(xcols(c), chn[:, 0, :], CH, rows_ready)
            dve.wait_ge(stored["a"], r_stored["a"].reg)
            stage_a(X[:, FC:XC, :], dinv[:, FC:XC], 2, f_rows)
            v.tensor_copy(fown[:, :, :], rowsA[:, 0:2, :]).then_inc(dve_step, 1)
            dve.wait_ge(dve_step, nth())
            dve.sem_inc(f_ready, 1)

            r_cc = Reached(dve, "dve_cc")

            def dense_a(s):
                dve.wait_ge(x_loaded[s], r_xl[s].more(16))
                dve.wait_ge(dense_stored["c"][s], r_dc[s].reg)
                r_dc[s].skip(16)
                norm(xin[:, s, :, :], row_ac[s][:, :, :], CH)
                dve.sem_inc(rows_ready, 1)

            def dense_c(s):
                xs = xin[:, s, :, :]
                r_conv.skip(1)
                dve.wait_ge(conv_copied, r_cc.more(1))
                v.tensor_tensor(agg[:, :, :], row_be[s][:, :, :], flat_rows(b4b[:, :], CH), ALU.add).then_inc(dve_step, 1)
                dve.wait_ge(dve_step, nth())
                v.tensor_tensor(xs, xs, agg[:, :, :], ALU.add).then_inc(dve_step, 1)
                dve.wait_ge(dve_step, nth())
                dve.wait_ge(dense_stored["a"][s], r_da[s].more(16))
                norm(xs, row_ac[s][:, :, :], CH)
                dve.sem_inc(rows_ready, 1)

            def dense_de(s):
                xs = xin[:, s, :, :]
                after_linear(xs, CH, TR_OF[s])
                dve.wait_ge(dense_stored["d"][s], r_dd[s].reg)
                r_dd[s].skip(16)
                norm(xs, row_d[s][:, :, 0:D], CH)
                attention_row(row_d[s][:, :, :], xs, CH)
                dve.sem_inc(rows_ready, 1)
                dve.wait_ge(dense_stored["b"][s], r_db[s].more(16))
                norm(xs, row_be[s][:, :, :], CH)
                v.scalar_tensor_tensor(xs, row_be[s][:, :, :], mixb[:, 0:1], xs, ALU.mult, ALU.add).then_inc(dve_step, 1)
                dve.wait_ge(dve_step, nth())
                dve.sem_inc(rows_ready, 1)

            def after_linear(xr, R, T=TR):
                q = R // 2
                conv = T[:, :].rearrange("p (h q f) -> p q h f", h=2, f=D)[:, 0:q, :, :]
                bias = b1b[:, :].unsqueeze(1).unsqueeze(1).to_broadcast([P, q, 2, D])
                dve.wait_ge(conv_ready, r_conv.more(1))
                v.tensor_tensor(agg[:, 0:R, :].rearrange("p (q h) f -> p q h f", h=2), conv, bias,
                                ALU.add).then_inc(dve_step, 1)
                dve.wait_ge(dve_step, nth())
                v.scalar_tensor_tensor(xr, agg[:, 0:R, :], 0.0, xr, ALU.max, ALU.add).then_inc(dve_step, 1)
                dve.wait_ge(dve_step, nth())

            def stage_d(xr, R, ready):
                after_linear(xr, R)
                dve.wait_ge(stored["d"], r_stored["d"].reg)
                if ready is rows_ready:
                    r_stored["d"].skip(16)
                norm(xr, rowsD[:, 0:R, 0:D], R)
                attention_row(rowsD[:, 0:R, :], xr, R)
                dve.sem_inc(ready, 1)

            def stage_e(xr, R, ready):
                norm(xr, rowsE[:, 0:R, :], R)
                v.scalar_tensor_tensor(xr, rowsE[:, 0:R, :], mixb[:, 0:1], xr, ALU.mult, ALU.add).then_inc(dve_step, 1)
                dve.wait_ge(dve_step, nth())
                dve.sem_inc(ready, 1)

            r_da, r_db, r_dc, r_dd = ([Reached(dve, f"dve_dense_{k}{s}") for s in (0, 1)] for k in "abcd")
            v.memset(row_d[1][:, :, AW - 1:AW], 1.0).then_inc(dve_step, 1)
            dve.wait_ge(dve_step, nth())
            dense_a(0)
            dense_c(0)
            dense_a(1)
            dense_de(0)
            dense_c(1)
            with dve.Fori(0, NT // 2 - 1):
                fresh()
                dense_a(0)
                dense_de(1)
                dense_c(0)
                dense_a(1)
                dense_de(0)
                dense_c(1)
            dense_de(1)
            dve.wait_ge(f_stored, r_fs.more(16))

            dve.wait_ge(look_done, 1)
            v.tensor_scalar(tmpA[:, :], idxA[:, :], float(N), None, ALU.is_ge).then_inc(dve_step, 1)
            dve.wait_ge(dve_step, nth())
            v.tensor_scalar(seatf[:, :], idxA[:, :], float(-N - ZERO), None, ALU.add).then_inc(dve_step, 1)
            dve.wait_ge(dve_step, nth())
            v.tensor_tensor(seatf[:, :], seatf[:, :], tmpA[:, :], ALU.mult).then_inc(dve_step, 1)
            dve.wait_ge(dve_step, nth())
            v.tensor_scalar(seatf[:, :], seatf[:, :], float(ZERO), None, ALU.add).then_inc(dve_step, 1)
            dve.wait_ge(dve_step, nth())
            v.tensor_copy(seatI[:, :], seatf[:, :]).then_inc(dve_step, 1)
            dve.wait_ge(dve_step, nth())

            def begin():
                v.memset(carry[:, :], 0.0).then_inc(dve_step, 1)
                dve.wait_ge(dve_step, nth())

            def chain(s, W, go):
                for j in range(CH):
                    before = carry[:, 0:W] if j == 0 else G[:, s, j - 1, 0:W]
                    v.scalar_tensor_tensor(G[:, s, j, 0:W], before, go[:, j:j + 1], G[:, s, j, 0:W],
                                           ALU.mult, ALU.add).then_inc(dve_step, 1)
                    dve.wait_ge(dve_step, nth())
                dve.sem_inc(raw_ready, 1)
                v.tensor_copy(carry[:, 0:W], G[:, s, CH - 1, 0:W]).then_inc(dve_step, 1)
                dve.wait_ge(dve_step, nth())

            def carry_in(W):
                to_pe()
                v.memset(TF[0:W, 0:1], 0.0)
                v.tensor_tensor_scan(TF[0:W, 1:P + 1], allcT[0:W, :], MI[0:W, 0:P], 0.0,
                                     ALU.mult, ALU.add).then_inc(dve_step, 1)
                dve.wait_ge(dve_step, nth())
                v.tensor_tensor(IT[0:W, :], TF[0:W, 0:P], c0T[0:W, :], ALU.mult).then_inc(dve_step, 1)
                dve.wait_ge(dve_step, nth())
                to_pe()
                dve.wait_ge(f_gathered, r_fg.more(16))
                v.tensor_tensor(FR[:, 0, 0:W], FR[:, 0, 0:W], MI[:, 128:128 + W], ALU.add).then_inc(dve_step, 1)
                dve.wait_ge(dve_step, nth())

            def stage_b(m, o, dv, R, ready, s=None):
                v.tensor_tensor(agg[:, 0:R, :], m, o, ALU.add).then_inc(dve_step, 1)
                dve.wait_ge(dve_step, nth())
                if s is not None:
                    dve.sem_inc(used[s], 1)
                v.tensor_tensor(agg[:, 0:R, :], agg[:, 0:R, :], wide(dv), ALU.mult).then_inc(dve_step, 1)
                dve.wait_ge(dve_step, nth())
                dve.sem_inc(mixed_ready, 1)
                dve.wait_ge(stored["b"], r_stored["b"].reg)
                if s is not None:
                    r_stored["b"].skip(16)
                dve.wait_ge(conv_ready, r_conv.more(1))
                v.tensor_tensor(rowsB[:, 0:R, :], TR[:, 0:R * D].rearrange("p (a b) -> p a b", b=D),
                                wide(dv), ALU.mult).then_inc(dve_step, 1)
                dve.wait_ge(dve_step, nth())
                dve.sem_inc(ready, 1)

            begin()
            with dve.Fori(0, NCH // 2) as i:
                fresh()
                for s in (0, 1):
                    c = 2 * i + s
                    v.tensor_copy(chn[:, 0, :], cols(cont, c))
                    v.tensor_copy(chn[:, 1, :], dinv[:, ds(c * CH, CH)]).then_inc(dve_step, 1)
                    dve.wait_ge(dve_step, nth())
                    dve.wait_ge(gathered[s], r_gat[s].more(16 * CH * (1)))
                    chain(s, D, chn[:, 0, :])
                    dve.wait_ge(own_loaded[s], r_own[s].more(16))
                    stage_b(G[:, s, :, 0:D], own[:, s, :, :], chn[:, 1, :], CH,
                            rows_ready, s)
            carry_in(D)
            stage_b(FR[:, :, 0:D], fown[:, :, :], dinv[:, FC:XC], 2, f_ready)
            v.tensor_copy(fown[:, :, :], rowsB[:, 0:2, :]).then_inc(dve_step, 1)
            dve.wait_ge(dve_step, nth())
            dve.wait_ge(f_stored, r_fs.more(16))

            def stage_c(m, o, dv, xr, R, ready, s=None):
                v.tensor_tensor(agg[:, 0:R, :], m, o, ALU.add).then_inc(dve_step, 1)
                dve.wait_ge(dve_step, nth())
                if s is not None:
                    dve.sem_inc(used[s], 1)
                v.tensor_tensor(agg[:, 0:R, :], agg[:, 0:R, :], wide(dv), ALU.mult).then_inc(dve_step, 1)
                dve.wait_ge(dve_step, nth())
                v.tensor_tensor(agg[:, 0:R, :], agg[:, 0:R, :], flat_rows(b4b[:, :], R), ALU.add).then_inc(dve_step, 1)
                dve.wait_ge(dve_step, nth())
                v.tensor_tensor(xr, xr, agg[:, 0:R, :], ALU.add).then_inc(dve_step, 1)
                dve.wait_ge(dve_step, nth())
                dve.wait_ge(stored["c"], r_stored["c"].reg)
                if s is not None:
                    r_stored["c"].skip(16)
                norm(xr, rowsC[:, 0:R, :], R)
                dve.sem_inc(ready, 1)

            begin()
            with dve.Fori(0, NCH // 2) as i:
                fresh()
                for s in (0, 1):
                    c = 2 * i + s
                    v.tensor_copy(chn[:, 0, :], cols(cont, c))
                    v.tensor_copy(chn[:, 1, :], dinv[:, ds(c * CH, CH)]).then_inc(dve_step, 1)
                    dve.wait_ge(dve_step, nth())
                    dve.wait_ge(gathered[s], r_gat[s].more(16 * CH))
                    chain(s, D, chn[:, 0, :])
                    dve.wait_ge(own_loaded[s], r_own[s].more(16))
                    stage_c(G[:, s, :, 0:D], own[:, s, :, :], chn[:, 1, :], xcols(c), CH,
                            rows_ready, s)
            carry_in(D)
            stage_c(FR[:, :, 0:D], fown[:, :, :], dinv[:, FC:XC], X[:, FC:XC, :], 2, f_ready)
            v.tensor_copy(fown[:, :, :], rowsC[:, 0:2, :]).then_inc(dve_step, 1)
            dve.wait_ge(dve_step, nth())
            dve.wait_ge(f_stored, r_fs.more(16))

            begin()
            with dve.Fori(0, NCH // 2) as i:
                fresh()
                for s in (0, 1):
                    c = 2 * i + s
                    g = G[:, s, :, 0:D]
                    v.tensor_copy(chn[:, 0, :], cols(cont, c)).then_inc(dve_step, 1)
                    dve.wait_ge(dve_step, nth())
                    dve.wait_ge(ea_loaded[s], r_ea[s].more(48))
                    dve.wait_ge(gathered[s], r_gat[s].more(16 * CH))
                    v.tensor_tensor(g, g, ea[:, s, :, :], ALU.add).then_inc(dve_step, 1)
                    dve.wait_ge(dve_step, nth())
                    v.tensor_scalar(g, g, 0.0, None, ALU.max).then_inc(dve_step, 1)
                    dve.wait_ge(dve_step, nth())
                    chain(s, D, chn[:, 0, :])
                    dve.wait_ge(own_loaded[s], r_own[s].more(16))
                    v.scalar_tensor_tensor(agg[:, :, :], own[:, s, :, :], eps1[:, 0:1], g,
                                           ALU.mult, ALU.add).then_inc(dve_step, 1)
                    dve.wait_ge(dve_step, nth())
                    dve.sem_inc(mixed_ready, 1)
                    dve.sem_inc(used[s], 1)
                    stage_d(xcols(c), CH, rows_ready)
                    v.tensor_copy(cols(s2V, c), rowsD[:, :, D + 1]).then_inc(dve_step, 1)
                    dve.wait_ge(dve_step, nth())
            carry_in(D)
            v.scalar_tensor_tensor(agg[:, 0:2, :], fown[:, :, :], eps1[:, 0:1], FR[:, :, 0:D],
                                   ALU.mult, ALU.add).then_inc(dve_step, 1)
            dve.wait_ge(dve_step, nth())
            dve.sem_inc(mixed_ready, 1)
            stage_d(X[:, FC:XC, :], 2, f_ready)
            v.tensor_copy(fm[:, 2:3], rowsD[:, 0, D + 1:D + 2]).then_inc(dve_step, 1)
            dve.wait_ge(dve_step, nth())

            def spread():
                v.copy_predicated(s2V[:, :], front[:, :].bitcast(i32),
                                  fm[:, 2:3].to_broadcast([P, COLS])).then_inc(dve_step, 1)
                dve.wait_ge(dve_step, nth())
                v.tensor_tensor(tmpA[:, :], s2V[:, :], ends[:, :], ALU.mult).then_inc(dve_step, 1)
                dve.wait_ge(dve_step, nth())
                v.tensor_tensor_scan(s2E[:, ::-1], goes[:, ::-1], tmpA[:, ::-1], 0.0, ALU.mult, ALU.add).then_inc(dve_step, 1)
                dve.wait_ge(dve_step, nth())
                v.tensor_copy(fm[:, 0:1], s2E[:, 0:1]).then_inc(dve_step, 1)
                dve.wait_ge(dve_step, nth())
                to_pe()
                v.memset(row[:, 0, P:P + 1], 0.0)
                v.tensor_tensor_scan(row[:, 0, 0:P][:, ::-1], noendT[:, ::-1], MI[0:1, 0:P][:, ::-1], 0.0,
                                     ALU.mult, ALU.add).then_inc(dve_step, 1)
                dve.wait_ge(dve_step, nth())
                v.tensor_copy(row[:, 1, 0:P], row[:, 0, 1:P + 1]).then_inc(dve_step, 1)
                dve.wait_ge(dve_step, nth())
                to_pe()
                v.tensor_copy(fm[:, 1:2], MI[:, 128:129]).then_inc(dve_step, 1)
                dve.wait_ge(dve_step, nth())
                v.scalar_tensor_tensor(s2E[:, :], after[:, :], fm[:, 1:2], s2E[:, :], ALU.mult, ALU.add).then_inc(dve_step, 1)
                dve.wait_ge(dve_step, nth())

            def seats_only():
                v.tensor_scalar(idxC[:, :], seatf[:, :], float(N), None, ALU.add).then_inc(dve_step, 1)
                dve.wait_ge(dve_step, nth())
                dve.sem_inc(step_done, 1)

            spread()
            dve.wait_ge(f_stored, r_fs.more(16))
            v.tensor_copy(idxC[:, :], idxA[:, :]).then_inc(dve_step, 1)
            dve.wait_ge(dve_step, nth())
            dve.sem_inc(step_done, 1)
            def step_d(k, first):
                v.tensor_copy(wk[:, :], tempb[:, ds(k + 1, 1)]).then_inc(dve_step, 1)
                dve.wait_ge(dve_step, nth())
                v.memset(ms[:, 0:1], NEG).then_inc(dve_step, 1)
                dve.wait_ge(dve_step, nth())
                begin()
                with dve.Fori(0, NCH // 2) as i:
                    fresh()
                    for s in (0, 1):
                        c = 2 * i + s
                        g = G[:, s, :, :]
                        r1, s1, e0, e1, a, p, rd, rw = (sm[:, n, :] for n in range(8))
                        v.tensor_copy(chn[:, 0, :], cols(cont, c))
                        v.tensor_copy(chn[:, 1, :], cols(s2E, c))
                        v.tensor_copy(chn[:, 2, :], cols(pen, c)).then_inc(dve_step, 1)
                        dve.wait_ge(dve_step, nth())
                        dve.wait_ge(gathered[s], r_gat[s].more(16 * CH))
                        v.reciprocal(r1, g[:, :, D + 2]).then_inc(dve_step, 1)
                        dve.wait_ge(dve_step, nth())
                        v.tensor_tensor(s1, g[:, :, D], r1, ALU.mult).then_inc(dve_step, 1)
                        dve.wait_ge(dve_step, nth())
                        v.tensor_tensor(e0, s1, chn[:, 1, :], ALU.add).then_inc(dve_step, 1)
                        dve.wait_ge(dve_step, nth())
                        v.scalar_tensor_tensor(e1, e0, LEAK, e0, ALU.mult, ALU.max).then_inc(dve_step, 1)
                        dve.wait_ge(dve_step, nth())
                        v.tensor_tensor_scan(ms[:, 1:CH + 1], chn[:, 2, :], e1, ms[:, 0:1],
                                             ALU.add, ALU.max).then_inc(dve_step, 1)
                        dve.wait_ge(dve_step, nth())
                        v.tensor_tensor(dif[:, 0:CH], ms[:, 0:CH], ms[:, 1:CH + 1], ALU.subtract)
                        v.tensor_tensor(dif[:, CH:2 * CH], e1, ms[:, 1:CH + 1], ALU.subtract).then_inc(dve_step, 1)
                        dve.wait_ge(dve_step, nth())
                        v.tensor_scalar(dif[:, :], dif[:, :], 0.0, None, ALU.min).then_inc(dve_step, 1)
                        dve.wait_ge(dve_step, nth())
                        dve.sem_inc(dif_ready, 1)
                        v.tensor_copy(cols(mx, c), ms[:, 1:CH + 1])
                        v.tensor_copy(ms[:, 0:1], ms[:, CH:CH + 1]).then_inc(dve_step, 1)
                        dve.wait_ge(dve_step, nth())
                        dve.wait_ge(exp_ready, r_exp.more(1))
                        v.tensor_tensor(a, expd[:, 0:CH], chn[:, 0, :], ALU.mult)
                        v.tensor_tensor(p, expd[:, CH:2 * CH], r1, ALU.mult).then_inc(dve_step, 1)
                        dve.wait_ge(dve_step, nth())
                        v.tensor_tensor(g, g, wide(p, AW), ALU.mult).then_inc(dve_step, 1)
                        dve.wait_ge(dve_step, nth())
                        chain(s, AW, a)
                        v.reciprocal(rd, g[:, :, D + 2]).then_inc(dve_step, 1)
                        dve.wait_ge(dve_step, nth())
                        v.tensor_tensor(cols(s2V, c), g[:, :, D + 1], rd, ALU.mult)
                        v.tensor_scalar(rw, rd, wk[:, 0:1], None, ALU.mult).then_inc(dve_step, 1)
                        dve.wait_ge(dve_step, nth())
                        v.tensor_tensor(agg[:, :, :], g[:, :, 0:D], wide(rw), ALU.mult).then_inc(dve_step, 1)
                        dve.wait_ge(dve_step, nth())
                        dve.sem_inc(used[s], 1)
                        v.tensor_tensor(xcols(c), xcols(c), agg[:, :, :], ALU.add).then_inc(dve_step, 1)
                        dve.wait_ge(dve_step, nth())
                if first:
                    seats_only()
                v.tensor_copy(mrep[:, :], mx[:, COLS - 1:COLS].to_broadcast([P, AW])).then_inc(dve_step, 1)
                dve.wait_ge(dve_step, nth())
                to_pe()
                v.memset(MF[0:AW, 0:1], NEG)
                v.tensor_scalar(IT[0:AW, :], allcT[0:AW, :], -NEG, NEG, ALU.mult, ALU.add).then_inc(dve_step, 1)
                dve.wait_ge(dve_step, nth())
                v.tensor_tensor_scan(MF[0:AW, 1:P + 1], IT[0:AW, :], MI[0:AW, 0:P], NEG,
                                     ALU.add, ALU.max).then_inc(dve_step, 1)
                dve.wait_ge(dve_step, nth())
                v.tensor_tensor(DT[0:AW, 0, :], MF[0:AW, 0:P], MF[0:AW, 1:P + 1], ALU.subtract)
                v.tensor_tensor(DT[0:AW, 1, :], MI[0:AW, 0:P], MF[0:AW, 1:P + 1], ALU.subtract).then_inc(dve_step, 1)
                dve.wait_ge(dve_step, nth())
                v.tensor_scalar(DT[0:AW, :, :], DT[0:AW, :, :], 0.0, None, ALU.min).then_inc(dve_step, 1)
                dve.wait_ge(dve_step, nth())
                dve.sem_inc(dif_ready, 1)
                to_pe()
                dve.wait_ge(exp_ready, r_exp.more(1))
                v.memset(TF[0:AW, 0:1], 0.0)
                v.tensor_tensor(ET[0:AW, 0, :], ET[0:AW, 0, :], allcT[0:AW, :], ALU.mult)
                v.tensor_tensor(ET[0:AW, 1, :], ET[0:AW, 1, :], MI[0:AW, 0:P], ALU.mult).then_inc(dve_step, 1)
                dve.wait_ge(dve_step, nth())
                v.tensor_tensor_scan(TF[0:AW, 1:P + 1], ET[0:AW, 0, :], ET[0:AW, 1, :], 0.0,
                                     ALU.mult, ALU.add).then_inc(dve_step, 1)
                dve.wait_ge(dve_step, nth())
                v.tensor_tensor(IT[0:AW, :], TF[0:AW, 0:P], c0T[0:AW, :], ALU.mult).then_inc(dve_step, 1)
                dve.wait_ge(dve_step, nth())
                to_pe()
                v.tensor_scalar(DT[0:AW, 0, :], c0T[0:AW, :], -NEG, NEG, ALU.mult, ALU.add).then_inc(dve_step, 1)
                dve.wait_ge(dve_step, nth())
                v.tensor_tensor(TF[0:AW, 0:P], MF[0:AW, 0:P], c0T[0:AW, :], ALU.mult).then_inc(dve_step, 1)
                dve.wait_ge(dve_step, nth())
                v.tensor_tensor(TF[0:AW, 0:P], TF[0:AW, 0:P], DT[0:AW, 0, :], ALU.add).then_inc(dve_step, 1)
                dve.wait_ge(dve_step, nth())
                to_pe()
                v.tensor_copy(fm[:, 1:2], MI[:, 256:257]).then_inc(dve_step, 1)
                dve.wait_ge(dve_step, nth())
                at_front(fm[:, 0:1], mx[:, :])
                v.tensor_tensor(fm[:, 3:4], fm[:, 0:1], fm[:, 1:2], ALU.max).then_inc(dve_step, 1)
                dve.wait_ge(dve_step, nth())
                v.tensor_scalar(fm[:, 4:6], fm[:, 0:2], fm[:, 3:4], None, ALU.subtract).then_inc(dve_step, 1)
                dve.wait_ge(dve_step, nth())
                dve.sem_inc(dif_ready, 1)
                dve.wait_ge(exp_ready, r_exp.more(1))
                dve.wait_ge(f_gathered, r_fg.more(16))
                v.tensor_scalar(FR[:, 0, :], FR[:, 0, :], fm[:, 6:7], None, ALU.mult).then_inc(dve_step, 1)
                dve.wait_ge(dve_step, nth())
                v.scalar_tensor_tensor(FR[:, 0, :], MI[:, 128:128 + AW], fm[:, 7:8], FR[:, 0, :],
                                       ALU.mult, ALU.add).then_inc(dve_step, 1)
                dve.wait_ge(dve_step, nth())
                dve.sem_inc(f_ready, 1)
                v.reciprocal(fm[:, 4:5], FR[:, 0, D + 2:D + 3]).then_inc(dve_step, 1)
                dve.wait_ge(dve_step, nth())
                v.tensor_tensor(fm[:, 2:3], fm[:, 4:5], FR[:, 0, D + 1:D + 2], ALU.mult).then_inc(dve_step, 1)
                dve.wait_ge(dve_step, nth())
                v.tensor_tensor(fm[:, 4:5], fm[:, 4:5], wk[:, :], ALU.mult).then_inc(dve_step, 1)
                dve.wait_ge(dve_step, nth())
                v.scalar_tensor_tensor(X[:, FC, :], FR[:, 0, 0:D], fm[:, 4:5], X[:, FC, :],
                                       ALU.mult, ALU.add).then_inc(dve_step, 1)
                dve.wait_ge(dve_step, nth())
                spread()
                dve.wait_ge(f_stored, r_fs.more(16))

            with dve.Fori(0, K2 // 2) as i:
                fresh()
                step_d(2 * i, True)
                step_d(2 * i + 1, False)

            with dve.Fori(0, NCH) as c:
                fresh()
                dve.wait_ge(stored["e"], r_stored["e"].reg)
                r_stored["e"].skip(16)
                stage_e(xcols(c), CH, rows_ready)
            dve.wait_ge(stored["e"], r_stored["e"].reg)
            stage_e(X[:, FC:XC, :], 2, f_ready)
            dve.wait_ge(f_stored, r_fs.more(16))

            v.tensor_copy(mx[:, :], snE[:, :])
            v.tensor_copy(idxC[:, :], idxA[:, :]).then_inc(dve_step, 1)
            dve.wait_ge(dve_step, nth())
            v.tensor_tensor(snE[:, :], snE[:, :], dnE[:, :], ALU.mult).then_inc(dve_step, 1)
            dve.wait_ge(dve_step, nth())
            dve.sem_inc(step_done, 1)
            def step_e(k, first):
                v.tensor_copy(wk[:, :], mixb[:, ds(k + 1, 1)]).then_inc(dve_step, 1)
                dve.wait_ge(dve_step, nth())
                begin()
                with dve.Fori(0, NCH // 2) as i:
                    fresh()
                    for s in (0, 1):
                        c = 2 * i + s
                        g = G[:, s, :, 0:D]
                        v.tensor_copy(chn[:, 0, :], cols(cont, c))
                        v.tensor_copy(chn[:, 2, :], dnorm[:, ds(c * CH, CH)])
                        v.tensor_copy(chn[:, 1, :], cols(mx, c)).then_inc(dve_step, 1)
                        dve.wait_ge(dve_step, nth())
                        v.tensor_scalar(chn[:, 3, :], chn[:, 2, :], wk[:, 0:1], None, ALU.mult).then_inc(dve_step, 1)
                        dve.wait_ge(dve_step, nth())
                        dve.wait_ge(gathered3[s], r_gat3[s].more(16 * CH))
                        v.tensor_tensor(g, g, wide(chn[:, 1, :]), ALU.mult).then_inc(dve_step, 1)
                        dve.wait_ge(dve_step, nth())
                        chain(s, D, chn[:, 0, :])
                        v.tensor_tensor(agg[:, :, :], g, wide(chn[:, 3, :]), ALU.mult).then_inc(dve_step, 1)
                        dve.wait_ge(dve_step, nth())
                        dve.sem_inc(used[s], 1)
                        v.tensor_tensor(xcols(c), xcols(c), agg[:, :, :], ALU.add).then_inc(dve_step, 1)
                        dve.wait_ge(dve_step, nth())
                if first:
                    seats_only()
                v.tensor_copy(mx[:, :], snE[:, :]).then_inc(dve_step, 1)
                dve.wait_ge(dve_step, nth())
                carry_in(D)
                dve.sem_inc(f_ready, 1)
                v.tensor_tensor(fm[:, 4:5], dnorm[:, FC:FC + 1], wk[:, :], ALU.mult).then_inc(dve_step, 1)
                dve.wait_ge(dve_step, nth())
                v.scalar_tensor_tensor(X[:, FC, :], FR[:, 0, 0:D], fm[:, 4:5], X[:, FC, :],
                                       ALU.mult, ALU.add).then_inc(dve_step, 1)
                dve.wait_ge(dve_step, nth())
                dve.wait_ge(f_stored, r_fs.more(16))

            with dve.Fori(0, K3 // 2) as i:
                fresh()
                step_e(2 * i, True)
                step_e(2 * i + 1, False)

            r_sc = [Reached(dve, f"dve_sc{s}") for s in (0, 1)]
            for s in (0, 1):
                r_sc[s].skip(16 * CH * (NCH // 2))
            with dve.Fori(0, NCH // 2) as i:
                fresh()
                for s in (0, 1):
                    dve.wait_ge(scattered[s], r_sc[s].reg)
                    r_sc[s].skip(16 * CH)
                    v.tensor_copy(G[:, s, :, 0:D], xcols(2 * i + s)).then_inc(dve_step, 1)
                    dve.wait_ge(dve_step, nth())
                    dve.sem_inc(final_ready[s], 1)


_ARGS = ["x", "src", "dst", "edge_attr_64", "L0_gnn_W3", "L0_gnn_b3", "L0_gnn_W4", "L0_gnn_b4",
         "L1_gnn_W", "L1_gnn_b", "L1_gnn_eps", "L2_gnn_attn_w", "L2_gnn_temp"]


def kernel(**inputs):
    import numpy as np
    import concourse.bacc as bacc
    from concourse import mybir
    from concourse.bass_utils import run_bass_kernel_spmd

    nc = bacc.Bacc("TRN2", target_bir_lowering=False, num_devices=1)
    arrays, args = {}, []
    for name in _ARGS:
        a = np.ascontiguousarray(inputs[name])
        if a.ndim == 0:
            a = a.reshape(1)
        arrays[f"in_{name}"] = a
        args.append(nc.dram_tensor(f"in_{name}", a.shape, mybir.dt.from_np(a.dtype), kind="ExternalInput").ap())
    out = nc.dram_tensor("out", [_N, _D], mybir.dt.float32, kind="ExternalOutput").ap()
    _build(nc, *args, out)
    r = run_bass_kernel_spmd(nc, [arrays], core_ids=[0])
    return r.results[0]["out"]
```

```python
_N, _E, _D = 100000, 50000, 64


def _build(nc, x, src, dst, edge_attr, W3, b3, W4, b4, W1, b1, eps, attn_w, temp, out):
    import math
    from contextlib import ExitStack

    import concourse.bass as bass
    from concourse import mybir

    f32, f16, i32 = mybir.dt.float32, mybir.dt.float16, mybir.dt.int32
    ALU = mybir.AluOpType
    ACT = mybir.ActivationFunctionType
    AXX = mybir.AxisListType.X
    ds = bass.ds

    P = 128
    N, E, D = _N, _E, _D
    HID = W3.shape[0]
    CH = 14
    NCH = 28
    COLS = CH * NCH
    EP = P * COLS
    assert EP >= E and NCH % 2 == 0
    LASTP = E - (P - 1) * COLS
    assert 0 < LASTP <= COLS
    FC = COLS
    XC = COLS + 2
    AW = D + 3
    REG = EP + 1
    ZERO = EP
    TILE = P * CH
    NT = -(-N // TILE)
    assert NT % 2 == 0
    LOB = 1024
    NHI = -(-N // LOB)
    PAD = 1 << 20
    BIG = 1 << 22
    NEG = -1e38
    LN_EPS = 1e-5
    LEAK = 0.01
    K2 = temp.shape[0] - 1
    K3 = 10
    logs = [math.log(2.0 + i) for i in range(1, K3 + 2)]
    mix = [v / sum(logs) for v in logs]

    ctx = ExitStack()
    with ctx:
        def sb(name, shape, dt=f32):
            return ctx.enter_context(nc.sbuf_tensor(name, shape, dt))

        def sem(name):
            return ctx.enter_context(nc.semaphore(name))

        def dram(name, shape, dt=f32):
            return nc.dram_tensor(name, shape, dt, kind="Internal").ap()

        tab_a = dram("tab_a", [N + EP, D])
        tab_b = dram("tab_b", [N + EP, D])
        tab_c = dram("tab_c", [N + EP, D])
        tab_d = dram("tab_d", [N + REG, AW])
        tab_e = dram("tab_e", [N + REG, D])
        alt_d = dram("alt_d", [REG, AW])
        alt_e = dram("alt_e", [REG, D])
        raw = dram("raw", [EP, D])
        lookup = dram("lookup", [NHI * LOB, 4])
        short = dram("short", [EP, 2])
        kept = dram("kept", [7, P, COLS])
        KEPT = K_CONT, K_FRONT, K_OUT, K_FACTOR, K_DNORM, K_SEAT, K_SHORT = range(7)
        counts = dram("counts", [P, 1])
        ea_last = dram("ea_last", [COLS, D])

        X = sb("X", [P, XC, D])
        srcI = sb("srcI", [P, COLS], i32)
        dstI = sb("dstI", [P, COLS], i32)
        nextI = sb("nextI", [P, COLS], i32)
        prevI = sb("prevI", [P, COLS], i32)
        dst_gat = sb("dst_gat", [P, COLS], i32)
        dst_tab = sb("dst_tab", [P, COLS], i32)
        dst_out = sb("dst_out", [P, COLS], i32)
        idxA = sb("idxA", [P, COLS], i32)
        idxC = sb("idxC", [P, COLS], i32)
        seatI = nextI
        seatf = sb("seatf", [P, COLS])
        place = sb("place", [P, COLS])
        cont = sb("cont", [P, COLS])
        pen = sb("pen", [P, COLS])
        ends = sb("ends", [P, COLS])
        goes = sb("goes", [P, COLS])
        front = sb("front", [P, COLS])
        after = sb("after", [P, COLS])
        dinv = sb("dinv", [P, XC])
        dnorm = sb("dnorm", [P, XC])
        snE = sb("snE", [P, COLS])
        s2V = dst_gat.bitcast(f32)
        s2E = dst_tab.bitcast(f32)
        mx = prevI.bitcast(f32)
        tmpA = sb("tmpA", [P, COLS])
        tmpB = sb("tmpB", [P, COLS])
        c0 = sb("c0", [P, 1])
        allc = sb("allc", [P, 1])
        noend = sb("noend", [P, 1])
        fr = sb("fr", [P, 8])
        fidx = sb("fidx", [P, 8], i32)
        F_DST, F_SEAT, F_TAB, F_SEAT_W, F_TAB_W, F_OUT = range(6)
        allcT = sb("allcT", [P, P])
        c0T = sb("c0T", [P, P])
        noendT = sb("noendT", [1, P])
        ident = sb("ident", [P, P])
        w3 = sb("w3", [P, 2, D])
        w4 = sb("w4", [D, HID])
        w1 = sb("w1", [D, 2, D])
        w3T = sb("w3T", [P, HID])
        w4T = sb("w4T", [HID, D])
        w1T = sb("w1T", [P, D])
        w1Te = sb("w1Te", [P, D])
        b3c = sb("b3c", [HID, 1])
        b4b = sb("b4b", [P, D])
        b1b = sb("b1b", [P, D])
        eps1 = sb("eps1", [P, 1])
        attn = sb("attn", [P, 2 * D])
        tempb = sb("tempb", [P, K2 + 1])
        mixb = sb("mixb", [P, K3 + 1])
        wk = sb("wk", [P, 1])
        lneps = sb("lneps", [P, 1])
        zrow = sb("zrow", [1, AW])
        G = sb("G", [P, 2, CH, AW])
        idxs = sb("idxs", [P, 2, CH], i32)
        vals = sb("vals", [P, 2, CH, 2])
        look = sb("look", [P, 2, CH, 4])
        xin = sb("xin", [P, 2, CH, D])
        own = xin
        SL = 2 * CH * D
        shared = sb("shared", [P, LOB * 4])
        assert 2 * SL + 4 * P <= LOB * 4 and CH * P == SL
        lookI = shared[:, :].rearrange("p (a b) -> p a b", b=4)
        hist = lookI[:, :, 1]
        U = shared[0:HID, 0:SL].rearrange("p (h q n) -> p h q n", h=2, q=CH // 2)
        ea = shared[:, SL:2 * SL].rearrange("p (s j f) -> p s j f", s=2, j=CH)
        DT = shared[:, 2 * SL:2 * SL + 2 * P].rearrange("p (a b) -> p a b", a=2)
        ET = shared[:, 2 * SL + 2 * P:2 * SL + 4 * P].rearrange("p (a b) -> p a b", a=2)
        carry = sb("carry", [P, AW])
        agg = sb("agg", [P, CH, D])
        xm = sb("xm", [P, CH, D])
        st = sb("st", [P, CH, 6])
        lnw = sb("lnw", [P, 6, CH])
        rowsA = sb("rowsA", [P, CH, D])
        rowsB = sb("rowsB", [P, CH, D])
        rowsC = sb("rowsC", [P, CH, D])
        rowsD = sb("rowsD", [P, CH, AW])
        rowsE = sb("rowsE", [P, CH, D])
        hT = sb("hT", [P, CH // 2, P])
        chn = sb("chn", [P, 4, CH])
        sm = sb("sm", [P, 8, CH])
        ms = sb("ms", [P, CH + 1])
        dif = sb("dif", [P, 2 * CH])
        expd = sb("expd", [P, 2 * CH])
        FR = sb("FR", [P, 2, AW])
        fown = sb("fown", [P, 2, D])
        TF = sb("TF", [P, P + 1])
        IT = sb("IT", [P, P])
        MF = sb("MF", [P, P + 1])
        mrep = sb("mrep", [P, AW])
        row = sb("row", [1, 2, P + 1])
        fm = sb("fm", [P, 8])
        sl = sb("sl", [P, 10])
        S_N, S_LAST, S_C0, S_ALLC, S_ON, S_NEXT, S_PREV, S_M, S_NOTON, S_DN = range(10)
        fidx2 = sb("fidx2", [P, 3], i32)
        shortI = sb("shortI", [1, 1], i32)
        zeros = sb("zeros", [P, D])
        rec = G[:, 1, :, :].rearrange("p a b -> p (a b)")[:, 0:2 * COLS].rearrange("p (a b) -> p a b", b=2)
        to_short = dst_gat
        map_at = dst_gat
        dst2 = dst_tab.bitcast(f32)[:, :]
        src2I, dst2I = prevI, idxC
        scrA, scrB = seatf, nextI.bitcast(f32)[:, :]
        cont2 = srcI.bitcast(f32)[:, :]
        row2 = nextI.bitcast(f32)[:, :]
        dn2, sn2 = seatf, tmpB
        seat2, dnd2 = dst_gat.bitcast(f32)[:, :], dst_tab.bitcast(f32)[:, :]
        half = xin[:, :, :, :].rearrange("p s j f -> p (s j f)").bitcast(f16)
        iota16 = half[:, 0:LOB]
        hot_lo = half[:, LOB:3 * LOB].rearrange("p (a b) -> p a b", a=2)
        hot_hi = half[:, 3 * LOB:3 * LOB + 2 * P].rearrange("p (a b) -> p a b", a=2)
        row_ac = [rowsA, rowsC]
        row_be = [rowsB, rowsE]
        row_d = [rowsD, G[:, 0, :, :]]
        xout = ea
        iotaN = lookI[:, :, 3].bitcast(i32)
        placeI = idxC

        TR = ctx.enter_context(nc.psum_tensor("TR", [P, 1024], f32))
        HP = ctx.enter_context(nc.psum_tensor("HP", [P, 4, 512], f32))
        TR1 = ctx.enter_context(nc.psum_tensor("TR1", [P, 1024], f32))
        MI = HP[:, 3, :]
        HI = HP[:, 0:2, :]

        iotas = sem("iotas")
        cleared = sem("cleared")
        loaded = sem("loaded")
        masks = sem("masks")
        weightsT = sem("weightsT")
        wcopied = sem("wcopied")
        dve_step = sem("dve_step")
        pool_step = sem("pool_step")
        hot_ready = sem("hot_ready")
        hot_used = sem("hot_used")
        hist_ready = sem("hist_ready")
        hist_used = sem("hist_used")
        look_ready = sem("look_ready")
        look_stored = sem("look_stored")
        count_ready = sem("count_ready")
        scattered = [sem("scattered0"), sem("scattered1")]
        mapped = [sem("mapped0"), sem("mapped1")]
        looked = [sem("looked0"), sem("looked1")]
        look_done = sem("look_done")
        gathered = [sem("gathered0"), sem("gathered1")]
        gathered3 = [sem("gathered3_0"), sem("gathered3_1")]
        used = [sem("used0"), sem("used1")]
        x_kept = [sem("x_kept0"), sem("x_kept1")]
        front_x = sem("front_x")
        raw_ready = sem("raw_ready")
        raw_stored = [sem("raw_stored0"), sem("raw_stored1")]
        own_loaded = [sem("own_loaded0"), sem("own_loaded1")]
        ea_loaded = [sem("ea_loaded0"), sem("ea_loaded1")]
        ea_padded = sem("ea_padded")
        x_loaded = [sem("x_loaded0"), sem("x_loaded1")]
        x_free = [sem("x_free0"), sem("x_free1")]
        out_stored = [sem("out_stored0"), sem("out_stored1")]
        rows_ready = sem("rows_ready")
        stored = {k: sem(f"stored_{k}") for k in "abcde"}
        dense_stored = {k: [sem(f"dense_{k}0"), sem(f"dense_{k}1")] for k in "abcde"}
        var_ready = sem("var_ready")
        sd_ready = sem("sd_ready")
        dif_ready = sem("dif_ready")
        exp_ready = sem("exp_ready")
        mixed_ready = sem("mixed_ready")
        rowsT_ready = sem("rowsT_ready")
        rowsT_copied = sem("rowsT_copied")
        hid_ready = sem("hid_ready")
        hid_copied = sem("hid_copied")
        conv_ready = sem("conv_ready")
        conv_copied = sem("conv_copied")
        to_turn = sem("to_turn")
        turned = sem("turned")
        f_gathered = sem("f_gathered")
        f_rows = sem("f_rows")
        f_ready = sem("f_ready")
        f_stored = sem("f_stored")
        short_to = sem("short_to")
        counts_stored = sem("counts_stored")
        short_zero = sem("short_zero")
        short_done = sem("short_done")
        short_loaded = sem("short_loaded")
        ends_ready = sem("ends_ready")
        ends_moved = sem("ends_moved")
        kept_ready = sem("kept_ready")
        kept_stored = sem("kept_stored")
        map_ready = sem("map_ready")
        src2_ready = sem("src2_ready")
        looked_up = sem("looked_up")
        arrays_free = sem("arrays_free")
        kept_loaded = sem("kept_loaded")
        step_done = sem("step_done")
        final_ready = [sem("final_ready0"), sem("final_ready1")]
        final_stored = sem("final_stored")
        zeros_ready = sem("zeros_ready")
        short_zeros = sem("short_zeros")
        zeros_stored = sem("zeros_stored")

        class Reached:

            def __init__(self, eng, name, start=0):
                self.eng, self.reg = eng, eng.alloc_register(name)
                eng.reg_mov(self.reg, start)

            def more(self, n):
                self.eng.reg_add(self.reg, self.reg, n)
                return self.reg

            def skip(self, n):
                self.eng.reg_add(self.reg, self.reg, n)

        FIRST = 1

        sp_waited, pool_waited, pe_waited = sem("sp_waited"), sem("pool_waited"), sem("pe_waited")

        def cols(t, c, n=CH):
            return t[:, ds(c * n, n)]

        def seats(table, first, c):
            return table[first:first + EP, :].rearrange("(p j) f -> p j f", p=P)[:, ds(c * CH, CH), :]

        def nodes(table, first):
            return table[ds(first, TILE), :].rearrange("(p j) f -> p j f", p=P)

        def wide(t, n=D):
            return t.unsqueeze(2).to_broadcast([t.shape[0], t.shape[1], n])

        def flat_rows(t, R):
            return t.unsqueeze(1).to_broadcast([P, R, t.shape[1]])

        TILES = [t * TILE for t in range(NT - 1)] + [N - TILE]
        TR_OF = [TR, TR1]
        PAIR1, PAIR2 = NT // 6, NT // 4 + 2

        block = ctx.enter_context(nc.Block())

        @block.sync
        def _(sp):
            r_used = [Reached(sp, f"sp_used{s}", FIRST) for s in (0, 1)]
            r_xf = [Reached(sp, f"sp_xf{s}", FIRST) for s in (0, 1)]
            r_gat = [Reached(sp, f"sp_gat{s}") for s in (0, 1)]
            sp.sem_inc(x_kept[0], FIRST)
            sp.sem_inc(x_kept[1], FIRST)
            sp.dma_start(w3[:, 0, :], W3).then_inc(loaded, 16)
            sp.dma_start(w3[:, 1, :], W3).then_inc(loaded, 16)
            sp.dma_start(w4[:, :], W4).then_inc(loaded, 16)
            sp.dma_start(w1[:, 0, :], W1).then_inc(loaded, 16)
            sp.dma_start(w1[:, 1, :], W1).then_inc(loaded, 16)
            sp.dma_start(b3c[:, :], b3.unsqueeze(1)).then_inc(loaded, 16)
            for t, v in ((b4b, b4), (b1b, b1), (tempb, temp)):
                sp.dma_start(t[:, :], v.unsqueeze(0).to_broadcast([P, t.shape[1]])).then_inc(loaded, 16)
            sp.dma_start(eps1[:, :], eps.unsqueeze(0).to_broadcast([P, 1])).then_inc(loaded, 16)
            sp.dma_start(attn[:, :], attn_w.to_broadcast([P, 2 * D])).then_inc(loaded, 16)
            sp.wait_ge(cleared, 1)
            B = P - 1
            for t, v, sh in ((srcI, src, 0), (dstI, dst, 0), (nextI, dst, 1)):
                sp.dma_start(t[0:B, :], v[sh:sh + B * COLS].rearrange("(p j) -> p j", j=COLS))\
                    .then_inc(loaded, 16)
                sp.dma_start(t[B:P, 0:LASTP - sh], v[B * COLS + sh:E].unsqueeze(0)).then_inc(loaded, 16)
            sp.dma_start(prevI[0:1, 1:COLS], dst[0:COLS - 1].unsqueeze(0)).then_inc(loaded, 16)
            sp.dma_start(prevI[1:B, :], dst[COLS - 1:B * COLS - 1].rearrange("(p j) -> p j", j=COLS))\
                .then_inc(loaded, 16)
            sp.dma_start(prevI[B:P, 0:LASTP + 1], dst[B * COLS - 1:E].unsqueeze(0)).then_inc(loaded, 16)
            sp.dma_start(ea_last[0:LASTP, :], edge_attr[B * COLS:E, :]).then_inc(ea_padded, 16)
            sp.wait_ge(zeros_ready, 1)
            sp.dma_start(ea_last[LASTP:COLS, :].rearrange("(o a) d -> o a d", o=1),
                         zrow[:, 0:D].unsqueeze(1).to_broadcast([1, COLS - LASTP, D])).then_inc(ea_padded, 16)
            sp.dma_start(short.rearrange("(p j) f -> p j f", p=P).rearrange("p j f -> p (j f)")
                         .rearrange("p (a b) -> p a b", b=16),
                         zeros[:, 0:16].unsqueeze(1).to_broadcast([P, COLS // 8, 16])).then_inc(short_zero, 16)
            for t, z in ((tab_d, N + ZERO), (alt_d, ZERO), (tab_e, N + ZERO), (alt_e, ZERO)):
                sp.dma_start(t[z:z + 1, :], zrow[:, 0:t.shape[1]]).then_inc(zeros_stored, 16)
            with sp.Fori(0, NCH // 2) as i:
                for s in (0, 1):
                    sp.wait_ge(gathered[s], r_gat[s].more(16 * CH))
                    sp.sem_inc(sp_waited, 1)
                    sp.dma_start(X[:, ds((2 * i + s) * CH, CH), :], G[:, s, :, 0:D]).then_inc(x_kept[s], 16)
            sp.wait_ge(look_ready, 1)
            sp.dma_start(lookup.rearrange("(p j) f -> p j f", p=NHI), lookI[0:NHI, :, :])\
                .then_inc(look_stored, 16)
            def keep(k, t):
                sp.dma_start(kept[k], t[:, :]).then_inc(kept_stored, 16)

            def load_tiles(first, last):
                with sp.Fori(first, last) as i:
                    for s in (0, 1):
                        sp.wait_ge(x_free[s], r_xf[s].reg)
                        sp.sem_inc(sp_waited, 1)
                        r_xf[s].skip(1)
                        sp.dma_start(xin[:, s, :, :], nodes(x, (2 * i + s) * TILE)).then_inc(x_loaded[s], 16)

            load_tiles(0, PAIR2 + 1)
            sp.wait_ge(short_to, 1)
            sp.dma_start(counts, sl[:, S_N:S_N + 1]).then_inc(counts_stored, 16)
            sp.wait_ge(counts_stored, 16)
            sp.dma_start(row[:, 1, 0:P], counts.rearrange("p o -> o p")).then_inc(short_loaded, 16)
            sp.wait_ge(short_done, 1)
            sp.dma_start(rec, short.rearrange("(p j) f -> p j f", p=P)).then_inc(short_loaded, 16)
            sp.wait_ge(ends_ready, 1)
            sp.dma_start(sl[0:P - 1, S_NEXT:S_NEXT + 1], dst2[1:P, 0:1]).then_inc(ends_moved, 16)
            sp.dma_start(sl[1:P, S_PREV:S_PREV + 1], sl[0:P - 1, S_LAST:S_LAST + 1]).then_inc(ends_moved, 16)
            sp.wait_ge(kept_ready, 1)
            keep(K_CONT, cont2)
            keep(K_FRONT, tmpB[:, :])
            keep(K_OUT, scrB)
            load_tiles(PAIR2 + 1, NT // 2 - 1)
            for s in (0, 1):
                sp.wait_ge(x_free[s], r_xf[s].reg)
                sp.sem_inc(sp_waited, 1)
                r_xf[s].skip(1)
                sp.dma_start(xin[:, s, :, :], nodes(x, TILES[NT - 2 + s])).then_inc(x_loaded[s], 16)
            for s in (0, 1):
                sp.wait_ge(x_free[s], r_xf[s].reg)
                sp.sem_inc(sp_waited, 1)
                sp.wait_ge(out_stored[s], FIRST + 16 * NT // 2)
                sp.sem_inc(sp_waited, 1)
            sp.wait_ge(kept_ready, 2)
            keep(K_FACTOR, dn2[:, :])
            keep(K_DNORM, dnd2)
            keep(K_SEAT, row2)
            keep(K_SHORT, seat2)
            r_fs = Reached(sp, "sp_fs")
            r_st = {k: Reached(sp, f"sp_stored_{k}", FIRST) for k in "abc"}
            for k, t in (("a", tab_a), ("b", tab_b), ("c", tab_c)):
                if k == "c":
                    sp.wait_ge(ea_padded, 32)
                sp.wait_ge(stored[k], r_st[k].more(16 * NCH))
                sp.sem_inc(sp_waited, 1)
                sp.wait_ge(f_stored, r_fs.more(16))
                sp.sem_inc(sp_waited, 1)
                with sp.Fori(0, NCH // 2) as i:
                    for s in (0, 1):
                        c = 2 * i + s
                        sp.wait_ge(used[s], r_used[s].reg)
                        sp.sem_inc(sp_waited, 1)
                        r_used[s].skip(1)
                        sp.dma_start(own[:, s, :, :], seats(t, N, c)).then_inc(own_loaded[s], 16)
                        if k == "c":
                            ev = edge_attr[0:B * COLS, :].rearrange("(p j) f -> p j f", p=B)
                            sp.dma_start(ea[0:112, s, :, :], ev[0:112, ds(c * CH, CH), :])\
                                .then_inc(ea_loaded[s], 16)
                            sp.dma_start(ea[112:B, s, :, :], ev[112:B, ds(c * CH, CH), :])\
                                .then_inc(ea_loaded[s], 16)
                            sp.dma_start(ea[B:P, s, :, :],
                                         ea_last[ds(c * CH, CH), :].rearrange("(o a) d -> o a d", o=1))\
                                .then_inc(ea_loaded[s], 16)

            sp.wait_ge(arrays_free, 1)
            sp.wait_ge(kept_stored, 16 * len(KEPT))
            for k, t in ((K_CONT, after[:, :]), (K_FRONT, front[:, :]), (K_OUT, idxA.bitcast(f32)),
                         (K_FACTOR, mx), (K_DNORM, seatf[:, :]), (K_SEAT, idxC.bitcast(f32)),
                         (K_SHORT, seatI.bitcast(f32))):
                sp.dma_start(t[:, :], kept[k]).then_inc(kept_loaded, 16)

        @block.gpsimd
        def _(pool):
            r_step = Reached(pool, "pool_steps")
            r_used = [Reached(pool, f"pool_used{s}", FIRST) for s in (0, 1)]
            r_xk = [Reached(pool, f"pool_xk{s}", FIRST) for s in (0, 1)]
            r_raw = [Reached(pool, f"pool_raw{s}", FIRST) for s in (0, 1)]
            r_sc = [Reached(pool, f"pool_sc{s}") for s in (0, 1)]
            r_lk = [Reached(pool, f"pool_lk{s}") for s in (0, 1)]
            r_fg = Reached(pool, "pool_fg")
            r_fr = Reached(pool, "pool_fr")
            r_fs = Reached(pool, "pool_fs")
            r_sd = Reached(pool, "pool_sd")
            zero = pool.alloc_register("pool_zero")
            bound = pool.alloc_register("pool_bound")
            pool.reg_mov(zero, 0)

            def last_row(table):
                pool.reg_add(bound, zero, table.shape[0] - 1)

            def gather(to, table, index, s):
                pool.indirect_dma_start(to, None, table, bass.IndirectOffsetOnAxis(ap=index, axis=0),
                                        bounds_check=bound, oob_is_err=False).then_inc(s, 16)

            def scatter(table, index, frm, s):
                pool.indirect_dma_start(table, bass.IndirectOffsetOnAxis(ap=index, axis=0), frm, None,
                                        bounds_check=bound, oob_is_err=False).then_inc(s, 16)

            def scatter_add(table, index, frm, s):
                pool.indirect_dma_start(table, bass.IndirectOffsetOnAxis(ap=index, axis=0), frm, None,
                                        bounds_check=bound, oob_is_err=False,
                                        compute_op=ALU.add).then_inc(s, 16)

            pool.iota(placeI[:, :], pattern=[[1, COLS]], base=0, channel_multiplier=COLS).then_inc(pool_step, 1)
            pool.wait_ge(pool_step, r_step.more(1))
            pool.sem_inc(pool_waited, 1)
            pool.iota(iotaN, pattern=[[1, LOB]], base=0, channel_multiplier=LOB).then_inc(pool_step, 1)
            pool.wait_ge(pool_step, r_step.more(1))
            pool.sem_inc(pool_waited, 1)
            pool.iota(iota16[:, :], pattern=[[1, LOB]], base=0, channel_multiplier=0,
                      allow_small_or_imprecise_dtypes=True).then_inc(pool_step, 1)
            pool.wait_ge(pool_step, r_step.more(1))
            pool.sem_inc(pool_waited, 1)
            pool.memset(ident[:, :], 0.0).then_inc(pool_step, 1)
            pool.wait_ge(pool_step, r_step.more(1))
            pool.sem_inc(pool_waited, 1)
            pool.affine_select(out=ident[:, :], in_=ident[:, :], compare_op=ALU.not_equal, fill=1.0,
                               base=0, pattern=[[-1, P]], channel_multiplier=1).then_inc(pool_step, 1)
            pool.wait_ge(pool_step, r_step.more(1))
            pool.sem_inc(pool_waited, 1)
            pool.sem_inc(iotas, 1)

            pool.wait_ge(masks, 1)
            last_row(x)
            with pool.Fori(0, NCH // 2) as i:
                for s in (0, 1):
                    pool.wait_ge(x_kept[s], r_xk[s].reg)
                    pool.sem_inc(pool_waited, 1)
                    r_xk[s].skip(16)
                    pool.tensor_copy(idxs[:, s, :], cols(dst_gat, 2 * i + s)).then_inc(pool_step, 1)
                    pool.wait_ge(pool_step, r_step.more(1))
                    pool.sem_inc(pool_waited, 1)
                    last_row(x)
                    for j in range(CH):
                        gather(G[:, s, j, 0:D], x, idxs[:, s, j:j + 1], gathered[s])
            gather(X[:, FC, :], x, fidx[:, F_DST:F_DST + 1], front_x)

            pool.wait_ge(masks, 2)
            pool.wait_ge(look_stored, 16)
            pairs = lookup.rearrange("n (a f) -> (n a) f", f=2)
            last_row(pairs)
            with pool.Fori(0, NCH // 2) as i:
                for s in (0, 1):
                    pool.tensor_copy(idxs[:, s, :], cols(dst_tab, 2 * i + s))
                    pool.tensor_copy(vals[:, s, :, 0], cols(place, 2 * i + s))
                    pool.tensor_copy(vals[:, s, :, 1], dnorm[:, ds((2 * i + s) * CH, CH)]).then_inc(pool_step, 1)
                    pool.wait_ge(pool_step, r_step.more(1))
                    pool.sem_inc(pool_waited, 1)
                    last_row(pairs)
                    for j in range(CH):
                        scatter(pairs, idxs[:, s, j:j + 1], vals[:, s, j, :], scattered[s])
                for s in (0, 1):
                    pool.wait_ge(scattered[s], r_sc[s].more(16 * CH))
                    pool.sem_inc(pool_waited, 1)

            last_row(lookup)
            with pool.Fori(0, NCH // 2) as i:
                for s in (0, 1):
                    pool.tensor_copy(idxs[:, s, :], cols(srcI, 2 * i + s)).then_inc(pool_step, 1)
                    pool.wait_ge(pool_step, r_step.more(1))
                    pool.sem_inc(pool_waited, 1)
                    last_row(lookup)
                    for j in range(CH):
                        gather(look[:, s, j, :], lookup, idxs[:, s, j:j + 1], looked[s])
                for s in (0, 1):
                    c = 2 * i + s
                    pool.wait_ge(looked[s], r_lk[s].more(16 * CH))
                    pool.sem_inc(pool_waited, 1)
                    pool.tensor_copy(cols(idxA, c), look[:, s, :, 0])
                    pool.tensor_copy(cols(snE, c), look[:, s, :, 2]).then_inc(pool_step, 1)
                    pool.wait_ge(pool_step, r_step.more(1))
                    pool.sem_inc(pool_waited, 1)
            pool.sem_inc(look_done, 1)

            pool.wait_ge(short_to, 1)
            pool.wait_ge(short_zero, 16)
            last_row(short)
            with pool.Fori(0, NCH // 2) as i:
                for s in (0, 1):
                    pool.tensor_copy(idxs[:, s, :], cols(to_short, 2 * i + s))
                    pool.tensor_copy(vals[:, s, :, 0], cols(srcI, 2 * i + s))
                    pool.tensor_copy(vals[:, s, :, 1], cols(dstI, 2 * i + s)).then_inc(pool_step, 1)
                    pool.wait_ge(pool_step, r_step.more(1))
                    pool.sem_inc(pool_waited, 1)
                    last_row(short)
                    for j in range(CH):
                        scatter(short, idxs[:, s, j:j + 1], vals[:, s, j, :], scattered[s])
                for s in (0, 1):
                    pool.wait_ge(scattered[s], r_sc[s].more(16 * CH))
                    pool.sem_inc(pool_waited, 1)
            pool.sem_inc(short_done, 1)
            r_map = [Reached(pool, f"pool_map{s}") for s in (0, 1)]
            ones = lookup.rearrange("n (a f) -> (n a) f", f=1)
            pool.wait_ge(map_ready, 1)
            last_row(ones)
            short_cols = pool.value_load(shortI[0:1, 0:1], min_val=0, max_val=COLS)
            with pool.Fori(0, NCH // 2) as i:
                with pool.If(i * (2 * CH) < short_cols):
                    for s in (0, 1):
                        pool.tensor_copy(idxs[:, s, :], cols(map_at, 2 * i + s))
                        pool.tensor_copy(vals[:, s, :, 0], cols(scrA, 2 * i + s)).then_inc(pool_step, 1)
                        pool.wait_ge(pool_step, r_step.more(1))
                        pool.sem_inc(pool_waited, 1)
                        last_row(ones)
                        for j in range(CH):
                            scatter(ones, idxs[:, s, j:j + 1], vals[:, s, j, 0:1], mapped[s])
                    for s in (0, 1):
                        pool.wait_ge(mapped[s], r_map[s].more(16 * CH))
                        pool.sem_inc(pool_waited, 1)

            def look_up(index, parts):
                with pool.Fori(0, NCH // 2) as i:
                    with pool.If(i * (2 * CH) < short_cols):
                        for s in (0, 1):
                            pool.tensor_copy(idxs[:, s, :], cols(index, 2 * i + s)).then_inc(pool_step, 1)
                            pool.wait_ge(pool_step, r_step.more(1))
                            pool.sem_inc(pool_waited, 1)
                            last_row(lookup)
                            for j in range(CH):
                                gather(look[:, s, j, :], lookup, idxs[:, s, j:j + 1], looked[s])
                        for s in (0, 1):
                            c = 2 * i + s
                            pool.wait_ge(looked[s], r_lk[s].more(16 * CH))
                            pool.sem_inc(pool_waited, 1)
                            for k, to in parts:
                                last = pool.tensor_copy(cols(to, c), look[:, s, :, k])
                            last.then_inc(pool_step, 1)
                            pool.wait_ge(pool_step, r_step.more(1))
                            pool.sem_inc(pool_waited, 1)

            look_up(dst2I, [(1, dnd2)])
            pool.wait_ge(kept_stored, 48)
            look_up(src2I, [(0, row2), (1, dn2), (2, sn2), (3, seat2)])
            pool.sem_inc(looked_up, 1)

            def sweep(table, idx, W, done=gathered):
                with pool.Fori(0, NCH // 2) as i:
                    for s in (0, 1):
                        pool.wait_ge(used[s], r_used[s].reg)
                        pool.sem_inc(pool_waited, 1)
                        r_used[s].skip(1)
                        pool.wait_ge(raw_stored[s], r_raw[s].reg)
                        pool.sem_inc(pool_waited, 1)
                        r_raw[s].skip(16)
                        pool.tensor_copy(idxs[:, s, :], cols(idx, 2 * i + s)).then_inc(pool_step, 1)
                        pool.wait_ge(pool_step, r_step.more(1))
                        pool.sem_inc(pool_waited, 1)
                        last_row(table)
                        for j in range(CH):
                            gather(G[:, s, j, 0:W], table, idxs[:, s, j:j + 1], done[s])

            def front_sums(table, col, W):
                for s in (0, 1):
                    pool.wait_ge(raw_stored[s], r_raw[s].reg)
                    pool.sem_inc(pool_waited, 1)
                last_row(table)
                gather(FR[:, 0, 0:W], table, fidx[:, col:col + 1], f_gathered)

            def front_rows(table, col, frm):
                pool.wait_ge(f_ready, r_fr.more(1))
                pool.sem_inc(pool_waited, 1)
                last_row(table)
                scatter(table, fidx[:, col:col + 1], frm, f_stored)
                pool.wait_ge(f_stored, r_fs.more(16))
                pool.sem_inc(pool_waited, 1)

            r_stored = {k: Reached(pool, f"pool_stored_{k}", FIRST) for k in "abcde"}
            front_rows(tab_a, F_TAB_W, fown[:, 0, :])
            pool.wait_ge(stored["a"], r_stored["a"].more(16 * NCH))
            pool.sem_inc(pool_waited, 1)
            pool.wait_ge(dense_stored["a"][0], FIRST + 16 * NT // 2)
            pool.wait_ge(dense_stored["a"][1], FIRST + 16 * NT // 2)
            pool.sem_inc(pool_waited, 1)
            pool.wait_ge(dense_stored["d"][1], FIRST + 16 * NT // 2)
            pool.sem_inc(pool_waited, 1)
            sweep(tab_a, idxA, D)
            front_sums(raw, F_SEAT, D)
            front_rows(tab_b, F_TAB_W, rowsB[:, 0, :])
            pool.wait_ge(stored["b"], r_stored["b"].more(16 * NCH))
            pool.sem_inc(pool_waited, 1)
            pool.wait_ge(dense_stored["b"][0], FIRST + 16 * NT // 2)
            pool.wait_ge(dense_stored["b"][1], FIRST + 16 * NT // 2)
            pool.sem_inc(pool_waited, 1)
            sweep(tab_b, idxA, D)
            front_sums(raw, F_SEAT, D)
            front_rows(tab_c, F_TAB_W, rowsC[:, 0, :])
            pool.wait_ge(stored["c"], r_stored["c"].more(16 * NCH))
            pool.sem_inc(pool_waited, 1)
            pool.wait_ge(dense_stored["c"][0], FIRST + 16 * NT // 2)
            pool.wait_ge(dense_stored["c"][1], FIRST + 16 * NT // 2)
            pool.sem_inc(pool_waited, 1)
            sweep(tab_c, idxA, D)
            front_sums(raw, F_SEAT, D)
            front_rows(tab_d, F_TAB_W, rowsD[:, 0, :])
            pool.wait_ge(stored["d"], r_stored["d"].more(16 * NCH))
            pool.sem_inc(pool_waited, 1)
            pool.wait_ge(dense_stored["d"][0], FIRST + 16 * NT // 2)
            pool.wait_ge(dense_stored["d"][1], FIRST + 16 * NT // 2)
            pool.sem_inc(pool_waited, 1)
            pool.wait_ge(zeros_stored, 64)
            pool.wait_ge(step_done, r_sd.more(1))
            pool.sem_inc(pool_waited, 1)
            with pool.Fori(0, K2 // 2):
                sweep(tab_d, idxC, AW)
                pool.wait_ge(step_done, r_sd.more(1))
                pool.sem_inc(pool_waited, 1)
                front_sums(alt_d, F_SEAT, AW)
                front_rows(alt_d, F_SEAT_W, FR[:, 0, :])
                sweep(alt_d, seatI, AW)
                front_sums(tab_d, F_TAB, AW)
                front_rows(tab_d, F_TAB_W, FR[:, 0, :])
            front_rows(tab_e, F_TAB_W, rowsE[:, 0, :])
            pool.wait_ge(stored["e"], r_stored["e"].more(16 * NCH))
            pool.sem_inc(pool_waited, 1)
            pool.wait_ge(dense_stored["e"][0], FIRST + 16 * NT // 2)
            pool.wait_ge(dense_stored["e"][1], FIRST + 16 * NT // 2)
            pool.sem_inc(pool_waited, 1)
            pool.wait_ge(step_done, r_sd.more(1))
            pool.sem_inc(pool_waited, 1)
            sweep(tab_e, idxC, D, gathered3)
            front_sums(alt_e, F_SEAT, D)
            front_rows(alt_e, F_SEAT_W, FR[:, 0, 0:D])

            for s in (0, 1):
                pool.wait_ge(out_stored[s], FIRST + 16 * NT // 2)
            r_fin = [Reached(pool, f"pool_fin{s}") for s in (0, 1)]
            last_row(out)
            with pool.Fori(0, NCH // 2) as i:
                for s in (0, 1):
                    pool.wait_ge(final_ready[s], r_fin[s].more(1))
                    pool.sem_inc(pool_waited, 1)
                    pool.wait_ge(scattered[s], r_sc[s].reg)
                    pool.sem_inc(pool_waited, 1)
                    r_sc[s].skip(16 * CH)
                    pool.tensor_copy(idxs[:, s, :], cols(dst_out, 2 * i + s)).then_inc(pool_step, 1)
                    pool.wait_ge(pool_step, r_step.more(1))
                    pool.sem_inc(pool_waited, 1)
                    last_row(out)
                    for j in range(CH):
                        scatter(out, idxs[:, s, j:j + 1], G[:, s, j, 0:D], scattered[s])
            scatter(out, fidx[:, F_OUT:F_OUT + 1], X[:, FC, :], final_stored)
            for s in (0, 1):
                pool.wait_ge(scattered[s], r_sc[s].reg)
                pool.sem_inc(pool_waited, 1)
            pool.wait_ge(final_stored, 16)
            pool.wait_ge(kept_loaded, 16 * len(KEPT))

            def short_sweep(table, idx):
                with pool.Fori(0, NCH // 2) as i:
                    with pool.If(i * (2 * CH) < short_cols):
                        for s in (0, 1):
                            pool.wait_ge(used[s], r_used[s].reg)
                            pool.sem_inc(pool_waited, 1)
                            r_used[s].skip(1)
                            pool.wait_ge(raw_stored[s], r_raw[s].reg)
                            pool.sem_inc(pool_waited, 1)
                            r_raw[s].skip(16)
                            pool.tensor_copy(idxs[:, s, :], cols(idx, 2 * i + s)).then_inc(pool_step, 1)
                            pool.wait_ge(pool_step, r_step.more(1))
                            pool.sem_inc(pool_waited, 1)
                            last_row(table)
                            for j in range(CH):
                                gather(G[:, s, j, 0:D], table, idxs[:, s, j:j + 1], gathered3[s])

            def short_front(table):
                for s in (0, 1):
                    pool.wait_ge(raw_stored[s], r_raw[s].reg)
                    pool.sem_inc(pool_waited, 1)
                last_row(table)
                gather(FR[:, 0, 0:D], table, fidx2[:, 0:1], f_gathered)
                pool.wait_ge(f_ready, r_fr.more(1))
                pool.sem_inc(pool_waited, 1)
                last_row(table)
                scatter(table, fidx2[:, 1:2], FR[:, 0, 0:D], f_stored)
                pool.wait_ge(f_stored, r_fs.more(16))
                pool.sem_inc(pool_waited, 1)

            pool.wait_ge(short_zeros, 32)
            short_sweep(alt_e, idxC)
            short_front(tab_b)
            with pool.Fori(0, (K3 - 2) // 2):
                short_sweep(tab_b, seatI)
                short_front(tab_c)
                short_sweep(tab_c, seatI)
                short_front(tab_b)
            last_row(out)
            with pool.Fori(0, NCH // 2) as i:
                with pool.If(i * (2 * CH) < short_cols):
                    for s in (0, 1):
                        pool.wait_ge(final_ready[s], r_fin[s].more(1))
                        pool.sem_inc(pool_waited, 1)
                        pool.wait_ge(scattered[s], r_sc[s].reg)
                        pool.sem_inc(pool_waited, 1)
                        r_sc[s].skip(16 * CH)
                        pool.tensor_copy(idxs[:, s, :], cols(idxA, 2 * i + s)).then_inc(pool_step, 1)
                        pool.wait_ge(pool_step, r_step.more(1))
                        pool.sem_inc(pool_waited, 1)
                        last_row(out)
                        for j in range(CH):
                            scatter_add(out, idxs[:, s, j:j + 1], G[:, s, j, 0:D], scattered[s])
            scatter_add(out, fidx2[:, 2:3], X[:, FC, :], final_stored)
            for s in (0, 1):
                pool.wait_ge(scattered[s], r_sc[s].reg)
                pool.sem_inc(pool_waited, 1)
            pool.wait_ge(final_stored, 32)
            pool.wait_ge(look_stored, 16)

        @block.scalar
        def _(act):
            r_var = Reached(act, "act_var")
            r_rows = Reached(act, "act_rows")
            r_raw = Reached(act, "act_raw")
            r_rt = Reached(act, "act_rt")
            r_hid = Reached(act, "act_hid")
            r_dif = Reached(act, "act_dif")

            def root(R):
                act.wait_ge(var_ready, r_var.more(1))
                nc.scalar.activation(lnw[:, 4, 0:R], lnw[:, 3, 0:R], ACT.Sqrt, bias=lneps[:, 0:1],
                                     scale=1.0 / D).then_inc(sd_ready, 1)

            def turn_copy(R, T=TR):
                q = R // 2
                for a, b in ((0, min(q, 4)), (4, q)):
                    if b > a:
                        act.wait_ge(rowsT_ready, r_rt.more(1))
                        last = nc.scalar.activation(hT[:, a:b, :].rearrange("p a b -> p (a b)"),
                                                    T[:, a * P:b * P], ACT.Copy)
                last.then_inc(rowsT_copied, 1)

            def hidden_relu(R):
                q = R // 2
                for g, (a, b) in enumerate(((0, min(q, 4)), (4, q))):
                    if b > a:
                        act.wait_ge(hid_ready, r_hid.more(1))
                        for h in (0, 1):
                            last = nc.scalar.activation(U[:, h, a:b, :].rearrange("p a b -> p (a b)"),
                                                        HP[:, 2 * h + g, 0:(b - a) * P], ACT.Relu,
                                                        bias=b3c[:, 0:1])
                last.then_inc(hid_copied, 1)

            def hidden(R):
                turn_copy(R)
                hidden_relu(R)

            def store_rows(to, frm, s):
                act.wait_ge(rows_ready, r_rows.more(1))
                act.dma_start(to, frm).then_inc(s, 16)

            def store_raw(to, s, W):
                act.wait_ge(raw_ready, r_raw.more(1))
                act.dma_start(to, G[:, s, :, 0:W]).then_inc(raw_stored[s], 16)

            def exps():
                act.wait_ge(dif_ready, r_dif.more(1))
                nc.scalar.activation(expd[:, :], dif[:, :], ACT.Exp).then_inc(exp_ready, 1)

            for s in (0, 1):
                act.sem_inc(raw_stored[s], FIRST)
                act.sem_inc(out_stored[s], FIRST)
                for k in "abcde":
                    act.sem_inc(dense_stored[k][s], FIRST)
            for k in "abcde":
                act.sem_inc(stored[k], FIRST)
            act.wait_ge(var_ready, r_var.more(1))
            nc.scalar.activation(tmpB[:, :], tmpA[:, :], ACT.Sqrt).then_inc(sd_ready, 1)
            act.wait_ge(var_ready, r_var.more(1))
            nc.scalar.activation(tmpB[:, :], tmpA[:, :], ACT.Sqrt, bias=1.0).then_inc(sd_ready, 1)
            act.wait_ge(var_ready, r_var.more(1))
            nc.scalar.activation(hist[0:NHI, :], hist[0:NHI, :], ACT.Sqrt).then_inc(sd_ready, 1)
            act.wait_ge(look_stored, 16)
            with act.Fori(0, NCH) as c:
                root(CH)
                store_rows(seats(tab_a, N, c), rowsA[:, :, :], stored["a"])
            root(2)

            r_be = [Reached(act, f"act_be{s}", FIRST) for s in (0, 1)]
            r_conv = Reached(act, "act_conv")
            r_cc = Reached(act, "act_cc")

            def conv_rows(s):
                act.wait_ge(dense_stored["e"][s], r_be[s].reg)
                r_be[s].skip(16)
                act.wait_ge(conv_ready, r_conv.more(1))
                nc.scalar.activation(row_be[s][:, :, :].rearrange("p a b -> p (a b)"),
                                     TR_OF[s][:, 0:CH * D], ACT.Copy).then_inc(conv_copied, 1)
                act.wait_ge(conv_copied, r_cc.more(1))

            def store_a(s, first):
                store_rows(nodes(tab_a, first), row_ac[s][:, :, :], dense_stored["a"][s])

            def store_d(s, first):
                store_rows(nodes(tab_d, first), row_d[s][:, :, :], dense_stored["d"][s])

            def rows_b(s, first):
                conv_rows(s)
                act.dma_start(nodes(tab_b, first), row_be[s][:, :, :]).then_inc(dense_stored["b"][s], 16)

            def store_e(s, first):
                act.wait_ge(rows_ready, r_rows.more(1))
                act.dma_start(nodes(out, first), xout[:, s, :, :]).then_inc(out_stored[s], 16)
                act.dma_start(nodes(tab_e, first), row_be[s][:, :, :]).then_inc(dense_stored["e"][s], 16)

            def rows_c(s, first):
                root(CH)
                store_rows(nodes(tab_c, first), row_ac[s][:, :, :], dense_stored["c"][s])

            def dense_half(s, now, before, o, other):
                root(CH)
                turn_copy(CH, TR_OF[o])
                r_conv.skip(1)
                store_a(s, now)
                if before is not None:
                    store_d(s, before)
                turn_copy(CH, TR_OF[s])
                root(CH)
                hidden_relu(CH)
                root(CH)
                rows_b(s, now)
                store_e(o, other)
                rows_c(s, now)

            root(CH)
            store_a(0, TILES[0])
            hidden(CH)
            rows_b(0, TILES[0])
            rows_c(0, TILES[0])
            dense_half(1, TILES[1], None, 0, TILES[0])
            with act.Fori(1, NT // 2 - 1) as i:
                dense_half(0, 2 * i * TILE, (2 * i - 2) * TILE, 1, (2 * i - 1) * TILE)
                dense_half(1, (2 * i + 1) * TILE, (2 * i - 1) * TILE, 0, 2 * i * TILE)
            dense_half(0, TILES[NT - 2], TILES[NT - 4], 1, TILES[NT - 3])
            act.wait_ge(dense_stored["a"][0], FIRST + 16 * NT // 2)
            act.wait_ge(dense_stored["b"][0], FIRST + 16 * NT // 2)
            act.wait_ge(dense_stored["c"][0], FIRST + 16 * NT // 2)
            dense_half(1, TILES[NT - 1], TILES[NT - 3], 0, TILES[NT - 2])
            turn_copy(CH, TR_OF[1])
            store_d(0, TILES[NT - 2])
            root(CH)
            root(CH)
            act.wait_ge(dense_stored["e"][0], FIRST + 16 * NT // 2)
            act.wait_ge(out_stored[0], FIRST + 16 * NT // 2)
            store_e(1, TILES[NT - 1])
            act.wait_ge(dense_stored["d"][0], FIRST + 16 * NT // 2)
            store_d(1, TILES[NT - 1])

            with act.Fori(0, NCH // 2) as i:
                for s in (0, 1):
                    store_raw(seats(raw, 0, 2 * i + s), s, D)
                    hidden(CH)
                    store_rows(seats(tab_b, N, 2 * i + s), rowsB[:, :, :], stored["b"])
            hidden(2)
            with act.Fori(0, NCH // 2) as i:
                for s in (0, 1):
                    store_raw(seats(raw, 0, 2 * i + s), s, D)
                    root(CH)
                    store_rows(seats(tab_c, N, 2 * i + s), rowsC[:, :, :], stored["c"])
            root(2)
            with act.Fori(0, NCH // 2) as i:
                for s in (0, 1):
                    store_raw(seats(raw, 0, 2 * i + s), s, D)
                    turn_copy(CH)
                    root(CH)
                    store_rows(seats(tab_d, N, 2 * i + s), rowsD[:, :, :], stored["d"])
            turn_copy(2)
            root(2)

            def step_d(table, first, last=False):
                with act.Fori(0, NCH // 2) as i:
                    for s in (0, 1):
                        exps()
                        store_raw(seats(table, first, 2 * i + s), s, AW)
                        if last:
                            root(CH)
                            store_rows(seats(tab_e, N, 2 * i + s), rowsE[:, :, :], stored["e"])
                act.wait_ge(dif_ready, r_dif.more(1))
                nc.scalar.activation(ET[0:AW, :, :], DT[0:AW, :, :], ACT.Exp).then_inc(exp_ready, 1)
                act.wait_ge(dif_ready, r_dif.more(1))
                nc.scalar.activation(fm[:, 6:8], fm[:, 4:6], ACT.Exp).then_inc(exp_ready, 1)

            with act.Fori(0, K2 // 2 - 1):
                step_d(alt_d, 0)
                step_d(tab_d, N)
            step_d(alt_d, 0)
            step_d(tab_d, N, True)
            root(2)
            with act.Fori(0, NCH // 2) as i:
                for s in (0, 1):
                    store_raw(seats(alt_e, 0, 2 * i + s), s, D)
            act.dma_start(tab_b[ZERO:ZERO + 1, :], zrow[:, 0:D]).then_inc(short_zeros, 16)
            act.dma_start(tab_c[ZERO:ZERO + 1, :], zrow[:, 0:D]).then_inc(short_zeros, 16)
            short_cols = act.value_load(shortI[0:1, 0:1], min_val=0, max_val=COLS)

            def short_stores(table):
                with act.Fori(0, NCH // 2) as i:
                    with act.If(i * (2 * CH) < short_cols):
                        for s in (0, 1):
                            store_raw(seats(table, 0, 2 * i + s), s, D)

            short_stores(tab_b)
            with act.Fori(0, (K3 - 2) // 2):
                short_stores(tab_c)
                short_stores(tab_b)

        @block.tensor
        def _(pe):
            r_rows = Reached(pe, "pe_rows")
            r_mix = Reached(pe, "pe_mix")
            r_rt = Reached(pe, "pe_rt")
            r_hid = Reached(pe, "pe_hid")
            r_turn = Reached(pe, "pe_turn")
            r_hot = Reached(pe, "pe_hot")
            r_hu = Reached(pe, "pe_hu", FIRST)

            def turn(rows, R, T=TR):
                for q in range(R // 2):
                    last = nc.tensor.transpose(T[:, q * P:(q + 1) * P],
                                               rows[:, 2 * q:2 * q + 2, :].rearrange("p a b -> p (a b)"),
                                               ident[:, :])
                    if q == 3 or q == R // 2 - 1:
                        last.then_inc(rowsT_ready, 1)
                pe.wait_ge(rowsT_copied, r_rt.more(1))
                pe.sem_inc(pe_waited, 1)

            def hidden(rows, R, T=TR):
                turn(rows, R, T)
                q = R // 2
                for g, (a, b) in enumerate(((0, min(q, 4)), (4, q))):
                    if b > a:
                        for h in (0, 1):
                            last = nc.tensor.matmul(HP[:, 2 * h + g, 0:(b - a) * P],
                                                    w3T[h * D:(h + 1) * D, :],
                                                    hT[h * D:(h + 1) * D, a:b, :].rearrange("p a b -> p (a b)"),
                                                    start=True, stop=True)
                        last.then_inc(hid_ready, 1)
                pe.wait_ge(hid_copied, r_hid.more(1))
                pe.sem_inc(pe_waited, 1)
                for r in range(R):
                    last = nc.tensor.matmul(T[:, r * D:(r + 1) * D], U[:, r % 2, r // 2, :], w4T[:, :],
                                            start=True, stop=True)
                last.then_inc(conv_ready, 1)

            def linear(rows, R, T=TR, w=w1T):
                turn(rows, R, T)
                for r in range(R):
                    h = r % 2
                    at = h * 512 + r // 2 * D
                    last = nc.tensor.matmul(T[:, at:at + D], hT[h * D:(h + 1) * D, r // 2, :],
                                            w[h * D:(h + 1) * D, :], start=True, stop=True)
                last.then_inc(conv_ready, 1)

            def turn_one(to, frm, n):
                pe.wait_ge(to_turn, r_turn.more(1))
                pe.sem_inc(pe_waited, 1)
                nc.tensor.transpose(to, frm, ident[0:n, 0:n]).then_inc(turned, 1)

            pe.wait_ge(iotas, 1)
            pe.wait_ge(loaded, 16 * 20)
            nc.tensor.transpose(TR[:, 0:P], w3[:, :, :].rearrange("p a b -> p (a b)"), ident[:, :])
            nc.tensor.transpose(TR[:, P:P + D], w4[:, :], ident[0:D, 0:D])
            nc.tensor.transpose(TR[:, 2 * P:2 * P + D], w1[:, :, :].rearrange("p a b -> p (a b)"),
                                ident[0:D, 0:D]).then_inc(weightsT, 1)
            for _ in range(2):
                turn_one(MI[:, 0:P], allcT[:, :], P)
            turn_one(MI[0:1, 0:P], noend[:, :], P)
            turn_one(MI[0:1, 0:P], fm[:, 0:1], P)
            turn_one(MI[:, 128:129], row[:, 1, 0:P], 1)
            with pe.Fori(0, NCH):
                pe.wait_ge(hist_used, r_hu.reg)
                pe.sem_inc(pe_waited, 1)
                r_hu.skip(1)
                for j in range(CH):
                    pe.wait_ge(hot_ready, r_hot.more(1))
                    pe.sem_inc(pe_waited, 1)
                    for h in (0, 1):
                        last = nc.tensor.matmul(HI[0:NHI, h, :], hot_hi[:, j % 2, 0:NHI],
                                                hot_lo[:, j % 2, h * 512:(h + 1) * 512],
                                                start=(j == 0), stop=(j == CH - 1))
                    last.then_inc(hot_used, 1)
            pe.wait_ge(wcopied, 1)
            r_rows.skip(NCH)
            def dense_products(s):
                pe.wait_ge(rows_ready, r_rows.more(1))
                pe.sem_inc(pe_waited, 1)
                hidden(row_ac[s], CH, TR_OF[s])

            def dense_linear(s):
                pe.wait_ge(rows_ready, r_rows.more(1))
                pe.sem_inc(pe_waited, 1)
                linear(row_ac[s], CH, TR_OF[s], w1Te)

            dense_products(0)
            dense_linear(0)
            dense_products(1)
            r_rows.skip(1)
            dense_linear(1)
            with pe.Fori(0, NT // 2 - 1):
                dense_products(0)
                r_rows.skip(2)
                dense_linear(0)
                dense_products(1)
                r_rows.skip(2)
                dense_linear(1)


            def carry_turns(W):
                turn_one(MI[0:W, 0:P], carry[:, 0:W], P)
                turn_one(MI[:, 128:128 + W], IT[0:W, :], W)

            with pe.Fori(0, NCH):
                pe.wait_ge(mixed_ready, r_mix.more(1))
                pe.sem_inc(pe_waited, 1)
                hidden(agg, CH)
            carry_turns(D)
            pe.wait_ge(mixed_ready, r_mix.more(1))
            pe.sem_inc(pe_waited, 1)
            hidden(agg, 2)
            carry_turns(D)
            with pe.Fori(0, NCH):
                pe.wait_ge(mixed_ready, r_mix.more(1))
                pe.sem_inc(pe_waited, 1)
                linear(agg, CH)
            carry_turns(D)
            pe.wait_ge(mixed_ready, r_mix.more(1))
            pe.sem_inc(pe_waited, 1)
            linear(agg, 2)

            def spread_turns():
                turn_one(MI[0:1, 0:P], fm[:, 0:1], P)
                turn_one(MI[:, 128:129], row[:, 1, 0:P], 1)

            spread_turns()
            with pe.Fori(0, K2):
                turn_one(MI[0:AW, 0:P], mrep[:, :], P)
                turn_one(MI[0:AW, 0:P], carry[:, :], P)
                turn_one(MI[:, 128:128 + AW], IT[0:AW, :], AW)
                turn_one(MI[:, 256:256 + AW], TF[0:AW, 0:P], AW)
                spread_turns()
            carry_turns(D)
            turn_one(MI[:, 0:P], allcT[:, :], P)
            turn_one(MI[:, 0:P], allcT[:, :], P)
            with pe.Fori(0, K3 - 1):
                carry_turns(D)

        @block.vector
        def _(dve):
            v = nc.vector
            r_sd = Reached(dve, "dve_sd")
            r_exp = Reached(dve, "dve_exp")
            r_conv = Reached(dve, "dve_conv")
            r_turned = Reached(dve, "dve_turned")
            r_stored = {k: Reached(dve, f"dve_st_{k}", FIRST) for k in "abcde"}
            r_gat = [Reached(dve, f"dve_gat{s}") for s in (0, 1)]
            r_gat3 = [Reached(dve, f"dve_gat3_{s}") for s in (0, 1)]
            r_own = [Reached(dve, f"dve_own{s}") for s in (0, 1)]
            r_ea = [Reached(dve, f"dve_ea{s}") for s in (0, 1)]
            r_xl = [Reached(dve, f"dve_xl{s}") for s in (0, 1)]
            r_fg = Reached(dve, "dve_fg")
            r_hot = Reached(dve, "dve_hot")
            r_fs = Reached(dve, "dve_fs")
            steps = [0]

            def nth():
                steps[0] += 1
                return steps[0]

            def fresh():
                dve.sem_clear(dve_step)
                steps[0] = 0

            for s in (0, 1):
                dve.sem_inc(used[s], FIRST)
                dve.sem_inc(x_free[s], FIRST)
            dve.sem_inc(hist_used, FIRST)
            v.memset(srcI[:, :], -1)
            v.memset(dstI[:, :], PAD)
            v.memset(nextI[:, :], PAD)
            v.memset(prevI[:, :], PAD).then_inc(dve_step, 1)
            dve.wait_ge(dve_step, nth())
            dve.sem_inc(cleared, 1)
            v.memset(zeros[:, :], 0.0)
            v.memset(zrow[:, :], 0.0).then_inc(dve_step, 1)
            dve.wait_ge(dve_step, nth())
            v.memset(zrow[:, AW - 1:AW], 1.0).then_inc(dve_step, 1)
            dve.wait_ge(dve_step, nth())
            dve.sem_inc(zeros_ready, 1)
            for k, w in enumerate(mix):
                v.memset(mixb[:, k:k + 1], w)
            v.memset(lneps[:, :], LN_EPS)
            v.memset(rowsD[:, :, AW - 1:AW], 1.0)
            v.memset(sl[:, :], -1.0)
            v.memset(FR[:, :, :], 0.0)
            v.memset(X[:, FC + 1:XC, :], 0.0)
            v.memset(dinv[:, :], 0.0)
            v.memset(dnorm[:, :], 0.0)
            v.memset(fm[:, :], 0.0)
            v.memset(hist[:, :], 0.0).then_inc(dve_step, 1)
            dve.wait_ge(dve_step, nth())
            dve.wait_ge(loaded, 16 * 20)
            dve.wait_ge(iotas, 1)

            v.tensor_tensor(cont[:, :], dstI[:, :], prevI[:, :], ALU.is_equal)
            v.tensor_tensor(goes[:, :], dstI[:, :], nextI[:, :], ALU.is_equal)
            v.tensor_scalar(dst_gat[:, :], dstI[:, :], N - 1, None, ALU.min)
            v.tensor_scalar(eps1[:, :], eps1[:, :], 1.0, None, ALU.add)
            v.tensor_copy(place[:, :], placeI[:, :]).then_inc(dve_step, 1)
            dve.wait_ge(dve_step, nth())
            v.tensor_copy(c0[:, :], cont[:, 0:1]).then_inc(dve_step, 1)
            dve.wait_ge(dve_step, nth())
            v.memset(cont[:, 0:1], 0.0)
            v.tensor_scalar(ends[:, :], goes[:, :], -1.0, 1.0, ALU.mult, ALU.add)
            v.memset(tmpB[:, :], 0.0).then_inc(dve_step, 1)
            dve.wait_ge(dve_step, nth())
            v.tensor_tensor_scan(tmpA[:, :], goes[:, :], tmpB[:, :], 1.0, ALU.mult, ALU.add)
            v.tensor_tensor_scan(after[:, ::-1], goes[:, ::-1], tmpB[:, ::-1], 1.0, ALU.mult, ALU.add)
            v.tensor_scalar(pen[:, :], cont[:, :], -NEG, NEG, ALU.mult, ALU.add).then_inc(dve_step, 1)
            dve.wait_ge(dve_step, nth())
            v.tensor_scalar(front[:, 0:1], tmpA[:, 0:1], -1.0, 1.0, ALU.mult, ALU.add)
            v.tensor_tensor(front[:, 1:COLS], tmpA[:, 0:COLS - 1], tmpA[:, 1:COLS], ALU.subtract)
            v.tensor_tensor(allc[:, :], tmpA[:, COLS - 2:COLS - 1], c0[:, :], ALU.mult)
            v.tensor_copy(noend[:, :], tmpA[:, COLS - 1:COLS]).then_inc(dve_step, 1)
            dve.wait_ge(dve_step, nth())
            v.tensor_scalar(front[:, :], front[:, :], c0[:, 0:1], None, ALU.mult).then_inc(dve_step, 1)
            dve.wait_ge(dve_step, nth())

            def at_front(to, arr):
                v.tensor_tensor(tmpA[:, :], front[:, :], arr, ALU.mult).then_inc(dve_step, 1)
                dve.wait_ge(dve_step, nth())
                v.tensor_reduce(to, tmpA[:, :], AXX, ALU.add).then_inc(dve_step, 1)
                dve.wait_ge(dve_step, nth())

            v.tensor_reduce(fr[:, 0:1], front[:, :], AXX, ALU.add).then_inc(dve_step, 1)
            dve.wait_ge(dve_step, nth())
            at_front(fr[:, 1:2], place[:, :])
            at_front(fr[:, 2:3], dstI[:, :])
            v.tensor_scalar(fr[:, 3:4], fr[:, 0:1], -1.0, 1.0, ALU.mult, ALU.add).then_inc(dve_step, 1)
            dve.wait_ge(dve_step, nth())
            v.scalar_tensor_tensor(fr[:, 4:5], fr[:, 3:4], place[:, 0:1], fr[:, 1:2], ALU.mult, ALU.add).then_inc(dve_step, 1)
            dve.wait_ge(dve_step, nth())
            v.scalar_tensor_tensor(fr[:, 5:6], fr[:, 3:4], float(BIG), fr[:, 4:5], ALU.mult, ALU.add).then_inc(dve_step, 1)
            dve.wait_ge(dve_step, nth())
            v.tensor_copy(fidx[:, F_DST:F_DST + 1], fr[:, 2:3])
            v.tensor_copy(fidx[:, F_SEAT:F_SEAT + 1], fr[:, 4:5])
            v.tensor_copy(fidx[:, F_SEAT_W:F_SEAT_W + 1], fr[:, 5:6])
            v.tensor_scalar(fidx[:, F_TAB:F_TAB + 1], fr[:, 4:5], float(N), None, ALU.add)
            v.tensor_scalar(fidx[:, F_TAB_W:F_TAB_W + 1], fr[:, 5:6], float(N), None, ALU.add)
            v.scalar_tensor_tensor(fidx[:, F_OUT:F_OUT + 1], fr[:, 3:4], float(BIG), fr[:, 2:3],
                                   ALU.mult, ALU.add).then_inc(dve_step, 1)
            dve.wait_ge(dve_step, nth())
            v.tensor_scalar(tmpA[:, :], goes[:, :], float(BIG), None, ALU.mult).then_inc(dve_step, 1)
            dve.wait_ge(dve_step, nth())
            v.scalar_tensor_tensor(dst_tab[:, :], dstI[:, :], 2.0, tmpA[:, :], ALU.mult, ALU.add).then_inc(dve_step, 1)
            dve.wait_ge(dve_step, nth())
            v.scalar_tensor_tensor(tmpA[:, :], front[:, :], float(BIG), tmpA[:, :], ALU.mult, ALU.add).then_inc(dve_step, 1)
            dve.wait_ge(dve_step, nth())
            v.tensor_tensor(dst_out[:, :], dstI[:, :], tmpA[:, :], ALU.add).then_inc(dve_step, 1)
            dve.wait_ge(dve_step, nth())
            dve.sem_inc(masks, 1)

            dve.wait_ge(weightsT, 1)
            v.tensor_copy(w3T[:, :], TR[:, 0:P])
            v.tensor_copy(w4T[:, :], TR[:, P:P + D])
            v.tensor_copy(w1T[:, :], TR[:, 2 * P:2 * P + D])
            v.tensor_scalar(w1Te[:, :], TR[:, 2 * P:2 * P + D], eps1[:, 0:1], None, ALU.mult).then_inc(dve_step, 1)
            dve.wait_ge(dve_step, nth())
            dve.sem_inc(wcopied, 1)

            def to_pe():
                dve.sem_inc(to_turn, 1)
                dve.wait_ge(turned, r_turned.more(1))

            v.tensor_copy(allcT[:, :], c0[:, 0:1].to_broadcast([P, P])).then_inc(dve_step, 1)
            dve.wait_ge(dve_step, nth())
            to_pe()
            v.tensor_copy(c0T[:, :], MI[:, 0:P])
            v.tensor_copy(allcT[:, :], allc[:, 0:1].to_broadcast([P, P])).then_inc(dve_step, 1)
            dve.wait_ge(dve_step, nth())
            to_pe()
            v.tensor_copy(allcT[:, :], MI[:, 0:P]).then_inc(dve_step, 1)
            dve.wait_ge(dve_step, nth())
            to_pe()
            v.tensor_copy(noendT[:, :], MI[0:1, 0:P]).then_inc(dve_step, 1)
            dve.wait_ge(dve_step, nth())

            v.memset(row[:, :, :], 0.0)
            v.memset(tmpB[:, :], 1.0).then_inc(dve_step, 1)
            dve.wait_ge(dve_step, nth())
            v.tensor_tensor_scan(tmpA[:, :], cont[:, :], tmpB[:, :], 0.0, ALU.mult, ALU.add).then_inc(dve_step, 1)
            dve.wait_ge(dve_step, nth())
            v.tensor_copy(fm[:, 0:1], tmpA[:, COLS - 1:COLS]).then_inc(dve_step, 1)
            dve.wait_ge(dve_step, nth())
            to_pe()
            v.tensor_tensor_scan(row[:, 0, 1:P + 1], allcT[0:1, :], MI[0:1, 0:P], 0.0, ALU.mult, ALU.add).then_inc(dve_step, 1)
            dve.wait_ge(dve_step, nth())
            v.tensor_tensor(row[:, 1, 0:P], row[:, 0, 0:P], c0T[0:1, :], ALU.mult).then_inc(dve_step, 1)
            dve.wait_ge(dve_step, nth())
            to_pe()
            v.tensor_copy(fm[:, 1:2], MI[:, 128:129]).then_inc(dve_step, 1)
            dve.wait_ge(dve_step, nth())
            v.scalar_tensor_tensor(tmpA[:, :], front[:, :], fm[:, 1:2], tmpA[:, :], ALU.mult, ALU.add).then_inc(dve_step, 1)
            dve.wait_ge(dve_step, nth())
            dve.sem_inc(var_ready, 1)
            dve.wait_ge(sd_ready, r_sd.more(1))
            v.reciprocal(dnorm[:, 0:COLS], tmpB[:, :]).then_inc(dve_step, 1)
            dve.wait_ge(dve_step, nth())
            dve.sem_inc(var_ready, 1)
            dve.wait_ge(sd_ready, r_sd.more(1))
            v.reciprocal(dinv[:, 0:COLS], tmpB[:, :]).then_inc(dve_step, 1)
            dve.wait_ge(dve_step, nth())
            at_front(dnorm[:, FC:FC + 1], dnorm[:, 0:COLS])
            at_front(dinv[:, FC:FC + 1], dinv[:, 0:COLS])
            v.tensor_scalar(place[:, :], place[:, :], float(N), None, ALU.add).then_inc(dve_step, 1)
            dve.wait_ge(dve_step, nth())

            v.tensor_single_scalar(nextI[:, :], srcI[:, :], LOB.bit_length() - 1,
                                   op=ALU.arith_shift_right).then_inc(dve_step, 1)
            dve.wait_ge(dve_step, nth())
            v.tensor_single_scalar(prevI[:, :], srcI[:, :], LOB - 1, op=ALU.bitwise_and).then_inc(dve_step, 1)
            dve.wait_ge(dve_step, nth())
            r_hist = Reached(dve, "dve_hist")
            r_hot_at = [None]
            with dve.Fori(0, NCH) as c:
                fresh()
                v.tensor_copy(chn[:, 0, :], cols(nextI, c))
                v.tensor_copy(chn[:, 1, :], cols(prevI, c)).then_inc(dve_step, 1)
                dve.wait_ge(dve_step, nth())
                for j in range(CH):
                    if j >= 2:
                        dve.wait_ge(hot_used, r_hot.more(1))
                    v.tensor_scalar(hot_hi[:, j % 2, 0:P], iota16[:, 0:P], chn[:, 0, j:j + 1], None,
                                    ALU.is_equal)
                    v.tensor_scalar(hot_lo[:, j % 2, :], iota16[:, :], chn[:, 1, j:j + 1], None,
                                    ALU.is_equal).then_inc(dve_step, 1)
                    dve.wait_ge(dve_step, nth())
                    dve.sem_inc(hot_ready, 1)
                dve.wait_ge(hot_used, r_hot.more(2))
                v.tensor_tensor(hist[0:NHI, :], hist[0:NHI, :],
                                HI[0:NHI, :, :].rearrange("p a b -> p (a b)"), ALU.add).then_inc(dve_step, 1)
                dve.wait_ge(dve_step, nth())
                dve.sem_inc(hist_used, 1)
            v.tensor_scalar(srcI[:, :], srcI[:, :], 0, None, ALU.max)
            v.tensor_copy(lookI[:, :, 0], iotaN)
            v.tensor_scalar(hist[:, :], hist[:, :], 1.0, None, ALU.max).then_inc(dve_step, 1)
            dve.wait_ge(dve_step, nth())
            dve.sem_inc(var_ready, 1)
            v.memset(lookI[:, :, 3], 0.0)
            dve.wait_ge(sd_ready, r_sd.more(1))
            v.reciprocal(lookI[0:NHI, :, 2], hist[0:NHI, :]).then_inc(dve_step, 1)
            dve.wait_ge(dve_step, nth())
            v.memset(hist[:, :], 1.0).then_inc(dve_step, 1)
            dve.wait_ge(dve_step, nth())
            dve.sem_inc(look_ready, 1)
            dve.sem_inc(masks, 1)

            def norm(xr, to, R):
                m_sum, m_dif, m2, var, sd, rs = (lnw[:, k, 0:R] for k in range(6))
                for r in range(R):
                    last = v.bn_stats(st[:, r, :], xr[:, r, :])
                last.then_inc(dve_step, 1)
                dve.wait_ge(dve_step, nth())
                v.tensor_tensor(m_sum, st[:, 0:R, 1], st[:, 0:R, 4], ALU.add)
                v.tensor_tensor(m2, st[:, 0:R, 2], st[:, 0:R, 5], ALU.add)
                v.tensor_tensor(m_dif, st[:, 0:R, 1], st[:, 0:R, 4], ALU.subtract).then_inc(dve_step, 1)
                dve.wait_ge(dve_step, nth())
                v.tensor_tensor(m_dif, m_dif, m_dif, ALU.mult).then_inc(dve_step, 1)
                dve.wait_ge(dve_step, nth())
                v.scalar_tensor_tensor(var, m_dif, D / 4.0, m2, ALU.mult, ALU.add).then_inc(dve_step, 1)
                dve.wait_ge(dve_step, nth())
                dve.sem_inc(var_ready, 1)
                v.scalar_tensor_tensor(xm[:, 0:R, :], wide(m_sum), -0.5, xr, ALU.mult, ALU.add)
                dve.wait_ge(sd_ready, r_sd.more(1))
                v.reciprocal(rs, sd).then_inc(dve_step, 1)
                dve.wait_ge(dve_step, nth())
                v.scalar_tensor_tensor(to, xm[:, 0:R, :], 0.0, wide(rs), ALU.max, ALU.mult).then_inc(dve_step, 1)
                dve.wait_ge(dve_step, nth())

            def xcols(c):
                return X[:, ds(c * CH, CH), :]

            def dots(to, R):
                for k in (0, 1):
                    v.tensor_tensor(xm[:, 0:R, :], to[:, :, 0:D], flat_rows(attn[:, k * D:(k + 1) * D], R),
                                    ALU.mult).then_inc(dve_step, 1)
                    dve.wait_ge(dve_step, nth())
                    v.tensor_reduce(to[:, :, D + k:D + k + 1], xm[:, 0:R, :], AXX, ALU.add).then_inc(dve_step, 1)
                    dve.wait_ge(dve_step, nth())

            def attention_row(to, xr, R):
                dots(to, R)
                v.scalar_tensor_tensor(xr, to[:, :, 0:D], tempb[:, 0:1], xr, ALU.mult, ALU.add).then_inc(dve_step, 1)
                dve.wait_ge(dve_step, nth())

            def stage_a(xr, dv, R, ready):
                norm(xr, rowsA[:, 0:R, :], R)
                v.tensor_tensor(rowsA[:, 0:R, :], rowsA[:, 0:R, :], wide(dv), ALU.mult).then_inc(dve_step, 1)
                dve.wait_ge(dve_step, nth())
                dve.sem_inc(ready, 1)

            for s in (0, 1):
                dve.wait_ge(x_kept[s], FIRST + 16 * NCH // 2)
                r_gat[s].skip(16 * CH * (NCH // 2))
            dve.wait_ge(front_x, 16)
            with dve.Fori(0, NCH) as c:
                fresh()
                v.tensor_copy(chn[:, 0, :], dinv[:, ds(c * CH, CH)]).then_inc(dve_step, 1)
                dve.wait_ge(dve_step, nth())
                dve.wait_ge(stored["a"], r_stored["a"].reg)
                r_stored["a"].skip(16)
                stage_a(xcols(c), chn[:, 0, :], CH, rows_ready)
            dve.wait_ge(stored["a"], r_stored["a"].reg)
            stage_a(X[:, FC:XC, :], dinv[:, FC:XC], 2, f_rows)
            v.tensor_copy(fown[:, :, :], rowsA[:, 0:2, :]).then_inc(dve_step, 1)
            dve.wait_ge(dve_step, nth())
            dve.sem_inc(f_ready, 1)

            r_cc = Reached(dve, "dve_cc")

            def dense_a(s):
                dve.wait_ge(x_loaded[s], r_xl[s].more(16))
                dve.wait_ge(dense_stored["c"][s], r_dc[s].reg)
                r_dc[s].skip(16)
                norm(xin[:, s, :, :], row_ac[s][:, :, :], CH)
                dve.sem_inc(rows_ready, 1)
                v.tensor_tensor(xin[:, s, :, :], xin[:, s, :, :], flat_rows(b4b[:, :], CH), ALU.add).then_inc(dve_step, 1)
                dve.wait_ge(dve_step, nth())

            def dense_c(s):
                xs = xin[:, s, :, :]
                r_conv.skip(1)
                dve.wait_ge(conv_copied, r_cc.more(1))
                v.tensor_tensor(xs, xs, row_be[s][:, :, :], ALU.add).then_inc(dve_step, 1)
                dve.wait_ge(dve_step, nth())
                dve.wait_ge(dense_stored["a"][s], r_da[s].more(16))
                norm(xs, row_ac[s][:, :, :], CH)
                dve.sem_inc(rows_ready, 1)

            def dense_d(s):
                xs = xin[:, s, :, :]
                after_linear(xs, CH, TR_OF[s])
                dve.wait_ge(dense_stored["d"][s], r_dd[s].reg)
                r_dd[s].skip(16)
                norm(xs, row_d[s][:, :, 0:D], CH)
                v.scalar_tensor_tensor(xs, row_d[s][:, :, 0:D], tempb[:, 0:1], xs, ALU.mult, ALU.add).then_inc(dve_step, 1)
                dve.wait_ge(dve_step, nth())

            def dense_e(s):
                xs = xin[:, s, :, :]
                dve.wait_ge(dense_stored["b"][s], r_db[s].more(16))
                norm(xs, row_be[s][:, :, :], CH)
                dve.wait_ge(out_stored[s], r_do[s].reg)
                r_do[s].skip(16)
                v.scalar_tensor_tensor(xout[:, s, :, :], row_be[s][:, :, :], mixb[:, 0:1], xs, ALU.mult, ALU.add).then_inc(dve_step, 1)
                dve.wait_ge(dve_step, nth())
                dve.sem_inc(rows_ready, 1)
                dve.sem_inc(x_free[s], 1)

            def dense_dots(s):
                dots(row_d[s][:, :, :], CH)
                dve.sem_inc(rows_ready, 1)

            def after_linear(xr, R, T=TR):
                q = R // 2
                conv = T[:, :].rearrange("p (h q f) -> p q h f", h=2, f=D)[:, 0:q, :, :]
                bias = b1b[:, :].unsqueeze(1).unsqueeze(1).to_broadcast([P, q, 2, D])
                dve.wait_ge(conv_ready, r_conv.more(1))
                v.tensor_tensor(agg[:, 0:R, :].rearrange("p (q h) f -> p q h f", h=2), conv, bias,
                                ALU.add).then_inc(dve_step, 1)
                dve.wait_ge(dve_step, nth())
                v.scalar_tensor_tensor(xr, agg[:, 0:R, :], 0.0, xr, ALU.max, ALU.add).then_inc(dve_step, 1)
                dve.wait_ge(dve_step, nth())

            def stage_d(xr, R, ready):
                after_linear(xr, R)
                dve.wait_ge(stored["d"], r_stored["d"].reg)
                if ready is rows_ready:
                    r_stored["d"].skip(16)
                norm(xr, rowsD[:, 0:R, 0:D], R)
                attention_row(rowsD[:, 0:R, :], xr, R)
                dve.sem_inc(ready, 1)

            def stage_e(xr, R, ready):
                norm(xr, rowsE[:, 0:R, :], R)
                v.scalar_tensor_tensor(xr, rowsE[:, 0:R, :], mixb[:, 0:1], xr, ALU.mult, ALU.add).then_inc(dve_step, 1)
                dve.wait_ge(dve_step, nth())
                dve.sem_inc(ready, 1)

            r_da, r_db, r_dc, r_dd = ([Reached(dve, f"dve_dense_{k}{s}", FIRST) for s in (0, 1)] for k in "abcd")
            r_do = [Reached(dve, f"dve_dense_out{s}", FIRST) for s in (0, 1)]
            v.memset(row_d[1][:, :, AW - 1:AW], 1.0).then_inc(dve_step, 1)
            dve.wait_ge(dve_step, nth())
            dense_a(0)
            dense_c(0)
            dense_a(1)
            dense_d(0)
            dense_e(0)
            dense_c(1)
            def dense_pairs(n):
                with dve.Fori(0, n):
                    fresh()
                    for s in (0, 1):
                        dense_a(s)
                        dense_dots(s)
                        dense_d(1 - s)
                        dense_e(1 - s)
                        dense_c(s)

            dense_pairs(PAIR1)
            dve.wait_ge(look_done, 1)
            cn, dl = sl[:, S_N:S_N + 1], sl[:, S_LAST:S_LAST + 1]
            v.tensor_scalar(tmpA[:, :], idxA[:, :], float(N), None, ALU.is_ge)
            v.tensor_scalar(tmpB[:, :], dstI[:, :], float(N), None, ALU.is_lt)
            v.tensor_scalar(fm[:, 0:1], place[:, 0:1], float(-N - 1), None, ALU.add)
            v.tensor_copy(dl, dstI[:, COLS - 1:COLS]).then_inc(dve_step, 1)
            dve.wait_ge(dve_step, nth())
            v.tensor_tensor(tmpA[:, :], tmpA[:, :], tmpB[:, :], ALU.mult).then_inc(dve_step, 1)
            dve.wait_ge(dve_step, nth())
            v.tensor_tensor_scan(tmpB[:, :], tmpA[:, :], tmpA[:, :], 0.0, ALU.add, ALU.max).then_inc(dve_step, 1)
            dve.wait_ge(dve_step, nth())
            v.tensor_copy(cn, tmpB[:, COLS - 1:COLS]).then_inc(dve_step, 1)
            dve.wait_ge(dve_step, nth())
            v.scalar_tensor_tensor(tmpB[:, :], tmpB[:, :], fm[:, 0:1], tmpA[:, :], ALU.add, ALU.mult).then_inc(dve_step, 1)
            dve.wait_ge(dve_step, nth())
            v.tensor_scalar(tmpA[:, :], tmpA[:, :], float(-BIG), float(BIG), ALU.mult, ALU.add).then_inc(dve_step, 1)
            dve.wait_ge(dve_step, nth())
            v.tensor_tensor(to_short[:, :], tmpA[:, :], tmpB[:, :], ALU.add).then_inc(dve_step, 1)
            dve.wait_ge(dve_step, nth())
            dve.sem_inc(short_to, 1)
            dense_pairs(PAIR2 - PAIR1)

            dve.wait_ge(short_loaded, 32)
            v.tensor_reduce(row[:, 0, 0:1], row[:, 1, 0:P], AXX, ALU.max).then_inc(dve_step, 1)
            dve.wait_ge(dve_step, nth())
            v.tensor_scalar(row[:, 0, 0:1], row[:, 0, 0:1], 1.0, float(COLS), ALU.add, ALU.min).then_inc(dve_step, 1)
            dve.wait_ge(dve_step, nth())
            v.tensor_copy(shortI[:, :], row[:, 0, 0:1])

            def live_columns():
                v.tensor_scalar(tmpA[:, :], place[:, :], place[:, 0:1], None, ALU.subtract).then_inc(dve_step, 1)
                dve.wait_ge(dve_step, nth())
                v.tensor_scalar(tmpB[:, :], tmpA[:, :], cn, None, ALU.is_lt).then_inc(dve_step, 1)
                dve.wait_ge(dve_step, nth())

            live_columns()
            v.tensor_copy(src2I[:, :], rec[:, :, 0])
            v.scalar_tensor_tensor(dst2, rec[:, :, 1], dl, tmpB[:, :], ALU.subtract, ALU.mult).then_inc(dve_step, 1)
            dve.wait_ge(dve_step, nth())
            v.tensor_scalar(dst2, dst2, dl, None, ALU.add).then_inc(dve_step, 1)
            dve.wait_ge(dve_step, nth())
            dve.sem_inc(ends_ready, 1)
            v.tensor_scalar(dst2I[:, :], dst2, float(N - 1), None, ALU.min)
            v.memset(cont2[:, 0:1], 0.0)
            v.tensor_tensor(cont2[:, 1:COLS], dst2[:, 1:COLS], dst2[:, 0:COLS - 1], ALU.is_equal).then_inc(dve_step, 1)
            dve.wait_ge(dve_step, nth())
            v.tensor_scalar(sl[:, S_M:S_M + 1], cn, float(COLS - 1), None, ALU.min)
            v.tensor_reduce(sl[:, S_ALLC:S_ALLC + 1], cont2[:, 1:COLS], AXX, ALU.min)
            dve.wait_ge(ends_moved, 32)
            v.tensor_tensor(sl[:, S_ON:S_ON + 1], dl, sl[:, S_NEXT:S_NEXT + 1], ALU.is_equal)
            v.tensor_tensor(sl[:, S_C0:S_C0 + 1], dst2[:, 0:1], sl[:, S_PREV:S_PREV + 1], ALU.is_equal).then_inc(dve_step, 1)
            dve.wait_ge(dve_step, nth())
            v.tensor_tensor(sl[:, S_ALLC:S_ALLC + 1], sl[:, S_ALLC:S_ALLC + 1], sl[:, S_C0:S_C0 + 1], ALU.mult)
            v.tensor_scalar(sl[:, S_NOTON:S_NOTON + 1], sl[:, S_ON:S_ON + 1], -1.0, 1.0, ALU.mult, ALU.add)
            v.tensor_copy(scrA[:, COLS - 1:COLS], sl[:, S_ON:S_ON + 1])
            v.tensor_copy(scrA[:, 0:COLS - 1], cont2[:, 1:COLS]).then_inc(dve_step, 1)
            dve.wait_ge(dve_step, nth())
            v.tensor_scalar(scrA[:, :], scrA[:, :], -1.0, 1.0, ALU.mult, ALU.add)
            v.tensor_scalar(tmpA[:, :], tmpA[:, :], sl[:, S_M:S_M + 1], sl[:, S_NOTON:S_NOTON + 1],
                            ALU.is_equal, ALU.mult).then_inc(dve_step, 1)
            dve.wait_ge(dve_step, nth())
            v.tensor_tensor(scrA[:, :], scrA[:, :], tmpB[:, :], ALU.mult).then_inc(dve_step, 1)
            dve.wait_ge(dve_step, nth())
            v.tensor_tensor(scrA[:, :], scrA[:, :], tmpA[:, :], ALU.max).then_inc(dve_step, 1)
            dve.wait_ge(dve_step, nth())
            v.tensor_scalar(scrB, scrA[:, :], -1.0, 1.0, ALU.mult, ALU.add)
            v.memset(tmpB[:, :], 0.0).then_inc(dve_step, 1)
            dve.wait_ge(dve_step, nth())
            v.tensor_tensor_scan(tmpA[:, :], scrB, tmpB[:, :], 1.0, ALU.mult, ALU.add).then_inc(dve_step, 1)
            dve.wait_ge(dve_step, nth())
            v.tensor_scalar(tmpB[:, 0:1], tmpA[:, 0:1], -1.0, 1.0, ALU.mult, ALU.add)
            v.tensor_tensor(tmpB[:, 1:COLS], tmpA[:, 0:COLS - 1], tmpA[:, 1:COLS], ALU.subtract).then_inc(dve_step, 1)
            dve.wait_ge(dve_step, nth())
            v.tensor_scalar(tmpB[:, :], tmpB[:, :], sl[:, S_C0:S_C0 + 1], None, ALU.mult).then_inc(dve_step, 1)
            dve.wait_ge(dve_step, nth())
            v.tensor_reduce(fr[:, 0:1], tmpB[:, :], AXX, ALU.add)
            v.tensor_tensor(tmpA[:, :], tmpB[:, :], place[:, :], ALU.mult).then_inc(dve_step, 1)
            dve.wait_ge(dve_step, nth())
            v.tensor_reduce(fr[:, 1:2], tmpA[:, :], AXX, ALU.add).then_inc(dve_step, 1)
            dve.wait_ge(dve_step, nth())
            v.tensor_tensor(tmpA[:, :], tmpB[:, :], dst2, ALU.mult).then_inc(dve_step, 1)
            dve.wait_ge(dve_step, nth())
            v.tensor_reduce(fr[:, 2:3], tmpA[:, :], AXX, ALU.add)
            v.tensor_scalar(fr[:, 3:4], fr[:, 0:1], -1.0, 1.0, ALU.mult, ALU.add).then_inc(dve_step, 1)
            dve.wait_ge(dve_step, nth())
            v.scalar_tensor_tensor(fr[:, 4:5], fr[:, 3:4], place[:, 0:1], fr[:, 1:2], ALU.mult, ALU.add)
            v.scalar_tensor_tensor(fidx2[:, 2:3], fr[:, 3:4], float(BIG), fr[:, 2:3], ALU.mult, ALU.add).then_inc(dve_step, 1)
            dve.wait_ge(dve_step, nth())
            v.tensor_scalar(fr[:, 5:6], fr[:, 4:5], float(-N), None, ALU.add).then_inc(dve_step, 1)
            dve.wait_ge(dve_step, nth())
            v.tensor_copy(fidx2[:, 0:1], fr[:, 5:6])
            v.scalar_tensor_tensor(fidx2[:, 1:2], fr[:, 3:4], float(BIG), fr[:, 5:6], ALU.mult, ALU.add).then_inc(dve_step, 1)
            dve.wait_ge(dve_step, nth())
            v.tensor_scalar(scrB, scrA[:, :], float(-BIG), float(BIG), ALU.mult, ALU.add).then_inc(dve_step, 1)
            dve.wait_ge(dve_step, nth())
            v.scalar_tensor_tensor(tmpA[:, :], dst2, 4.0, scrB, ALU.mult, ALU.add)
            v.scalar_tensor_tensor(scrB, tmpB[:, :], float(BIG), scrB, ALU.mult, ALU.add).then_inc(dve_step, 1)
            dve.wait_ge(dve_step, nth())
            v.tensor_scalar(map_at[:, :], tmpA[:, :], 3.0, None, ALU.add)
            v.tensor_scalar(scrA[:, :], place[:, :], float(-N - ZERO), None, ALU.add)
            v.tensor_tensor(nextI[:, :], dst2, scrB, ALU.add).then_inc(dve_step, 1)
            dve.wait_ge(dve_step, nth())
            dve.sem_inc(kept_ready, 1)
            dve.sem_inc(map_ready, 1)
            dense_pairs(NT // 2 - 1 - PAIR2)
            dense_dots(0)
            dense_d(1)
            dense_e(1)
            dense_dots(1)
            dve.wait_ge(f_stored, r_fs.more(16))

            dve.wait_ge(looked_up, 1)
            v.tensor_tensor(dn2[:, :], dn2[:, :], sn2[:, :], ALU.mult).then_inc(dve_step, 1)
            dve.wait_ge(dve_step, nth())
            live_columns()
            v.tensor_scalar(row2, row2, float(-N - ZERO), None, ALU.add)
            v.tensor_tensor(dn2[:, :], dn2[:, :], tmpB[:, :], ALU.mult)
            v.tensor_tensor(seat2, seat2, tmpB[:, :], ALU.mult).then_inc(dve_step, 1)
            dve.wait_ge(dve_step, nth())
            v.tensor_tensor(row2, row2, tmpB[:, :], ALU.mult)
            v.tensor_scalar(map_at[:, :], seat2, float(ZERO), None, ALU.add).then_inc(dve_step, 1)
            dve.wait_ge(dve_step, nth())
            v.tensor_scalar(nextI[:, :], row2, float(ZERO), None, ALU.add).then_inc(dve_step, 1)
            dve.wait_ge(dve_step, nth())
            dve.sem_inc(kept_ready, 1)
            dve.wait_ge(kept_stored, 16 * len(KEPT))
            v.tensor_scalar(tmpA[:, :], idxA[:, :], float(N), None, ALU.is_ge).then_inc(dve_step, 1)
            dve.wait_ge(dve_step, nth())
            v.tensor_scalar(seatf[:, :], idxA[:, :], float(-N - ZERO), None, ALU.add).then_inc(dve_step, 1)
            dve.wait_ge(dve_step, nth())
            v.tensor_tensor(seatf[:, :], seatf[:, :], tmpA[:, :], ALU.mult).then_inc(dve_step, 1)
            dve.wait_ge(dve_step, nth())
            v.tensor_scalar(seatf[:, :], seatf[:, :], float(ZERO), None, ALU.add).then_inc(dve_step, 1)
            dve.wait_ge(dve_step, nth())
            v.tensor_copy(seatI[:, :], seatf[:, :]).then_inc(dve_step, 1)
            dve.wait_ge(dve_step, nth())

            def begin():
                v.memset(carry[:, :], 0.0).then_inc(dve_step, 1)
                dve.wait_ge(dve_step, nth())

            def chain(s, W, go):
                for j in range(CH):
                    before = carry[:, 0:W] if j == 0 else G[:, s, j - 1, 0:W]
                    v.scalar_tensor_tensor(G[:, s, j, 0:W], before, go[:, j:j + 1], G[:, s, j, 0:W],
                                           ALU.mult, ALU.add).then_inc(dve_step, 1)
                    dve.wait_ge(dve_step, nth())
                dve.sem_inc(raw_ready, 1)
                v.tensor_copy(carry[:, 0:W], G[:, s, CH - 1, 0:W]).then_inc(dve_step, 1)
                dve.wait_ge(dve_step, nth())

            def carry_in(W):
                to_pe()
                v.memset(TF[0:W, 0:1], 0.0)
                v.tensor_tensor_scan(TF[0:W, 1:P + 1], allcT[0:W, :], MI[0:W, 0:P], 0.0,
                                     ALU.mult, ALU.add).then_inc(dve_step, 1)
                dve.wait_ge(dve_step, nth())
                v.tensor_tensor(IT[0:W, :], TF[0:W, 0:P], c0T[0:W, :], ALU.mult).then_inc(dve_step, 1)
                dve.wait_ge(dve_step, nth())
                to_pe()
                dve.wait_ge(f_gathered, r_fg.more(16))
                v.tensor_tensor(FR[:, 0, 0:W], FR[:, 0, 0:W], MI[:, 128:128 + W], ALU.add).then_inc(dve_step, 1)
                dve.wait_ge(dve_step, nth())

            def stage_b(m, o, dv, R, ready, s=None):
                v.tensor_tensor(agg[:, 0:R, :], m, o, ALU.add).then_inc(dve_step, 1)
                dve.wait_ge(dve_step, nth())
                if s is not None:
                    dve.sem_inc(used[s], 1)
                v.tensor_tensor(agg[:, 0:R, :], agg[:, 0:R, :], wide(dv), ALU.mult).then_inc(dve_step, 1)
                dve.wait_ge(dve_step, nth())
                dve.sem_inc(mixed_ready, 1)
                dve.wait_ge(stored["b"], r_stored["b"].reg)
                if s is not None:
                    r_stored["b"].skip(16)
                dve.wait_ge(conv_ready, r_conv.more(1))
                v.tensor_tensor(rowsB[:, 0:R, :], TR[:, 0:R * D].rearrange("p (a b) -> p a b", b=D),
                                wide(dv), ALU.mult).then_inc(dve_step, 1)
                dve.wait_ge(dve_step, nth())
                dve.sem_inc(ready, 1)

            begin()
            with dve.Fori(0, NCH // 2) as i:
                fresh()
                for s in (0, 1):
                    c = 2 * i + s
                    v.tensor_copy(chn[:, 0, :], cols(cont, c))
                    v.tensor_copy(chn[:, 1, :], dinv[:, ds(c * CH, CH)]).then_inc(dve_step, 1)
                    dve.wait_ge(dve_step, nth())
                    dve.wait_ge(gathered[s], r_gat[s].more(16 * CH * (1)))
                    chain(s, D, chn[:, 0, :])
                    dve.wait_ge(own_loaded[s], r_own[s].more(16))
                    stage_b(G[:, s, :, 0:D], own[:, s, :, :], chn[:, 1, :], CH,
                            rows_ready, s)
            carry_in(D)
            stage_b(FR[:, :, 0:D], fown[:, :, :], dinv[:, FC:XC], 2, f_ready)
            v.tensor_copy(fown[:, :, :], rowsB[:, 0:2, :]).then_inc(dve_step, 1)
            dve.wait_ge(dve_step, nth())
            dve.wait_ge(f_stored, r_fs.more(16))

            def stage_c(m, o, dv, xr, R, ready, s=None):
                v.tensor_tensor(agg[:, 0:R, :], m, o, ALU.add).then_inc(dve_step, 1)
                dve.wait_ge(dve_step, nth())
                if s is not None:
                    dve.sem_inc(used[s], 1)
                v.tensor_tensor(agg[:, 0:R, :], agg[:, 0:R, :], wide(dv), ALU.mult).then_inc(dve_step, 1)
                dve.wait_ge(dve_step, nth())
                v.tensor_tensor(agg[:, 0:R, :], agg[:, 0:R, :], flat_rows(b4b[:, :], R), ALU.add).then_inc(dve_step, 1)
                dve.wait_ge(dve_step, nth())
                v.tensor_tensor(xr, xr, agg[:, 0:R, :], ALU.add).then_inc(dve_step, 1)
                dve.wait_ge(dve_step, nth())
                dve.wait_ge(stored["c"], r_stored["c"].reg)
                if s is not None:
                    r_stored["c"].skip(16)
                norm(xr, rowsC[:, 0:R, :], R)
                dve.sem_inc(ready, 1)

            begin()
            with dve.Fori(0, NCH // 2) as i:
                fresh()
                for s in (0, 1):
                    c = 2 * i + s
                    v.tensor_copy(chn[:, 0, :], cols(cont, c))
                    v.tensor_copy(chn[:, 1, :], dinv[:, ds(c * CH, CH)]).then_inc(dve_step, 1)
                    dve.wait_ge(dve_step, nth())
                    dve.wait_ge(gathered[s], r_gat[s].more(16 * CH))
                    chain(s, D, chn[:, 0, :])
                    dve.wait_ge(own_loaded[s], r_own[s].more(16))
                    stage_c(G[:, s, :, 0:D], own[:, s, :, :], chn[:, 1, :], xcols(c), CH,
                            rows_ready, s)
            carry_in(D)
            stage_c(FR[:, :, 0:D], fown[:, :, :], dinv[:, FC:XC], X[:, FC:XC, :], 2, f_ready)
            v.tensor_copy(fown[:, :, :], rowsC[:, 0:2, :]).then_inc(dve_step, 1)
            dve.wait_ge(dve_step, nth())
            dve.wait_ge(f_stored, r_fs.more(16))

            begin()
            with dve.Fori(0, NCH // 2) as i:
                fresh()
                for s in (0, 1):
                    c = 2 * i + s
                    g = G[:, s, :, 0:D]
                    v.tensor_copy(chn[:, 0, :], cols(cont, c)).then_inc(dve_step, 1)
                    dve.wait_ge(dve_step, nth())
                    dve.wait_ge(ea_loaded[s], r_ea[s].more(48))
                    dve.wait_ge(gathered[s], r_gat[s].more(16 * CH))
                    v.tensor_tensor(g, g, ea[:, s, :, :], ALU.add).then_inc(dve_step, 1)
                    dve.wait_ge(dve_step, nth())
                    v.tensor_scalar(g, g, 0.0, None, ALU.max).then_inc(dve_step, 1)
                    dve.wait_ge(dve_step, nth())
                    chain(s, D, chn[:, 0, :])
                    dve.wait_ge(own_loaded[s], r_own[s].more(16))
                    v.scalar_tensor_tensor(agg[:, :, :], own[:, s, :, :], eps1[:, 0:1], g,
                                           ALU.mult, ALU.add).then_inc(dve_step, 1)
                    dve.wait_ge(dve_step, nth())
                    dve.sem_inc(mixed_ready, 1)
                    dve.sem_inc(used[s], 1)
                    stage_d(xcols(c), CH, rows_ready)
                    v.tensor_copy(cols(s2V, c), rowsD[:, :, D + 1]).then_inc(dve_step, 1)
                    dve.wait_ge(dve_step, nth())
            carry_in(D)
            v.scalar_tensor_tensor(agg[:, 0:2, :], fown[:, :, :], eps1[:, 0:1], FR[:, :, 0:D],
                                   ALU.mult, ALU.add).then_inc(dve_step, 1)
            dve.wait_ge(dve_step, nth())
            dve.sem_inc(mixed_ready, 1)
            stage_d(X[:, FC:XC, :], 2, f_ready)
            v.tensor_copy(fm[:, 2:3], rowsD[:, 0, D + 1:D + 2]).then_inc(dve_step, 1)
            dve.wait_ge(dve_step, nth())

            def spread():
                v.copy_predicated(s2V[:, :], front[:, :].bitcast(i32),
                                  fm[:, 2:3].to_broadcast([P, COLS])).then_inc(dve_step, 1)
                dve.wait_ge(dve_step, nth())
                v.tensor_tensor(tmpA[:, :], s2V[:, :], ends[:, :], ALU.mult).then_inc(dve_step, 1)
                dve.wait_ge(dve_step, nth())
                v.tensor_tensor_scan(s2E[:, ::-1], goes[:, ::-1], tmpA[:, ::-1], 0.0, ALU.mult, ALU.add).then_inc(dve_step, 1)
                dve.wait_ge(dve_step, nth())
                v.tensor_copy(fm[:, 0:1], s2E[:, 0:1]).then_inc(dve_step, 1)
                dve.wait_ge(dve_step, nth())
                to_pe()
                v.memset(row[:, 0, P:P + 1], 0.0)
                v.tensor_tensor_scan(row[:, 0, 0:P][:, ::-1], noendT[:, ::-1], MI[0:1, 0:P][:, ::-1], 0.0,
                                     ALU.mult, ALU.add).then_inc(dve_step, 1)
                dve.wait_ge(dve_step, nth())
                v.tensor_copy(row[:, 1, 0:P], row[:, 0, 1:P + 1]).then_inc(dve_step, 1)
                dve.wait_ge(dve_step, nth())
                to_pe()
                v.tensor_copy(fm[:, 1:2], MI[:, 128:129]).then_inc(dve_step, 1)
                dve.wait_ge(dve_step, nth())
                v.scalar_tensor_tensor(s2E[:, :], after[:, :], fm[:, 1:2], s2E[:, :], ALU.mult, ALU.add).then_inc(dve_step, 1)
                dve.wait_ge(dve_step, nth())

            def seats_only():
                v.tensor_scalar(idxC[:, :], seatf[:, :], float(N), None, ALU.add).then_inc(dve_step, 1)
                dve.wait_ge(dve_step, nth())
                dve.sem_inc(step_done, 1)

            spread()
            dve.wait_ge(f_stored, r_fs.more(16))
            v.tensor_copy(idxC[:, :], idxA[:, :]).then_inc(dve_step, 1)
            dve.wait_ge(dve_step, nth())
            dve.sem_inc(step_done, 1)

            def step_d(k, first, last=False):
                v.tensor_copy(wk[:, :], tempb[:, ds(k + 1, 1)]).then_inc(dve_step, 1)
                dve.wait_ge(dve_step, nth())
                v.memset(ms[:, 0:1], NEG).then_inc(dve_step, 1)
                dve.wait_ge(dve_step, nth())
                begin()
                with dve.Fori(0, NCH // 2) as i:
                    fresh()
                    for s in (0, 1):
                        c = 2 * i + s
                        g = G[:, s, :, :]
                        r1, s1, e0, e1, a, p, rd, rw = (sm[:, n, :] for n in range(8))
                        v.tensor_copy(chn[:, 0, :], cols(cont, c))
                        v.tensor_copy(chn[:, 1, :], cols(s2E, c))
                        v.tensor_copy(chn[:, 2, :], cols(pen, c)).then_inc(dve_step, 1)
                        dve.wait_ge(dve_step, nth())
                        dve.wait_ge(gathered[s], r_gat[s].more(16 * CH))
                        v.reciprocal(r1, g[:, :, D + 2]).then_inc(dve_step, 1)
                        dve.wait_ge(dve_step, nth())
                        v.tensor_tensor(s1, g[:, :, D], r1, ALU.mult).then_inc(dve_step, 1)
                        dve.wait_ge(dve_step, nth())
                        v.tensor_tensor(e0, s1, chn[:, 1, :], ALU.add).then_inc(dve_step, 1)
                        dve.wait_ge(dve_step, nth())
                        v.scalar_tensor_tensor(e1, e0, LEAK, e0, ALU.mult, ALU.max).then_inc(dve_step, 1)
                        dve.wait_ge(dve_step, nth())
                        v.tensor_tensor_scan(ms[:, 1:CH + 1], chn[:, 2, :], e1, ms[:, 0:1],
                                             ALU.add, ALU.max).then_inc(dve_step, 1)
                        dve.wait_ge(dve_step, nth())
                        v.tensor_tensor(dif[:, 0:CH], ms[:, 0:CH], ms[:, 1:CH + 1], ALU.subtract)
                        v.tensor_tensor(dif[:, CH:2 * CH], e1, ms[:, 1:CH + 1], ALU.subtract).then_inc(dve_step, 1)
                        dve.wait_ge(dve_step, nth())
                        v.tensor_scalar(dif[:, :], dif[:, :], 0.0, None, ALU.min).then_inc(dve_step, 1)
                        dve.wait_ge(dve_step, nth())
                        dve.sem_inc(dif_ready, 1)
                        v.tensor_copy(cols(mx, c), ms[:, 1:CH + 1])
                        v.tensor_copy(ms[:, 0:1], ms[:, CH:CH + 1]).then_inc(dve_step, 1)
                        dve.wait_ge(dve_step, nth())
                        dve.wait_ge(exp_ready, r_exp.more(1))
                        v.tensor_tensor(a, expd[:, 0:CH], chn[:, 0, :], ALU.mult)
                        v.tensor_tensor(p, expd[:, CH:2 * CH], r1, ALU.mult).then_inc(dve_step, 1)
                        dve.wait_ge(dve_step, nth())
                        v.tensor_tensor(g, g, wide(p, AW), ALU.mult).then_inc(dve_step, 1)
                        dve.wait_ge(dve_step, nth())
                        chain(s, AW, a)
                        v.reciprocal(rd, g[:, :, D + 2]).then_inc(dve_step, 1)
                        dve.wait_ge(dve_step, nth())
                        v.tensor_tensor(cols(s2V, c), g[:, :, D + 1], rd, ALU.mult)
                        v.tensor_scalar(rw, rd, wk[:, 0:1], None, ALU.mult).then_inc(dve_step, 1)
                        dve.wait_ge(dve_step, nth())
                        v.tensor_tensor(agg[:, :, :], g[:, :, 0:D], wide(rw), ALU.mult).then_inc(dve_step, 1)
                        dve.wait_ge(dve_step, nth())
                        dve.sem_inc(used[s], 1)
                        v.tensor_tensor(xcols(c), xcols(c), agg[:, :, :], ALU.add).then_inc(dve_step, 1)
                        dve.wait_ge(dve_step, nth())
                        if last:
                            dve.wait_ge(stored["e"], r_stored["e"].reg)
                            r_stored["e"].skip(16)
                            stage_e(xcols(c), CH, rows_ready)
                if first:
                    seats_only()
                v.tensor_copy(mrep[:, :], mx[:, COLS - 1:COLS].to_broadcast([P, AW])).then_inc(dve_step, 1)
                dve.wait_ge(dve_step, nth())
                to_pe()
                v.memset(MF[0:AW, 0:1], NEG)
                v.tensor_scalar(IT[0:AW, :], allcT[0:AW, :], -NEG, NEG, ALU.mult, ALU.add).then_inc(dve_step, 1)
                dve.wait_ge(dve_step, nth())
                v.tensor_tensor_scan(MF[0:AW, 1:P + 1], IT[0:AW, :], MI[0:AW, 0:P], NEG,
                                     ALU.add, ALU.max).then_inc(dve_step, 1)
                dve.wait_ge(dve_step, nth())
                v.tensor_tensor(DT[0:AW, 0, :], MF[0:AW, 0:P], MF[0:AW, 1:P + 1], ALU.subtract)
                v.tensor_tensor(DT[0:AW, 1, :], MI[0:AW, 0:P], MF[0:AW, 1:P + 1], ALU.subtract).then_inc(dve_step, 1)
                dve.wait_ge(dve_step, nth())
                v.tensor_scalar(DT[0:AW, :, :], DT[0:AW, :, :], 0.0, None, ALU.min).then_inc(dve_step, 1)
                dve.wait_ge(dve_step, nth())
                dve.sem_inc(dif_ready, 1)
                to_pe()
                dve.wait_ge(exp_ready, r_exp.more(1))
                v.memset(TF[0:AW, 0:1], 0.0)
                v.tensor_tensor(ET[0:AW, 0, :], ET[0:AW, 0, :], allcT[0:AW, :], ALU.mult)
                v.tensor_tensor(ET[0:AW, 1, :], ET[0:AW, 1, :], MI[0:AW, 0:P], ALU.mult).then_inc(dve_step, 1)
                dve.wait_ge(dve_step, nth())
                v.tensor_tensor_scan(TF[0:AW, 1:P + 1], ET[0:AW, 0, :], ET[0:AW, 1, :], 0.0,
                                     ALU.mult, ALU.add).then_inc(dve_step, 1)
                dve.wait_ge(dve_step, nth())
                v.tensor_tensor(IT[0:AW, :], TF[0:AW, 0:P], c0T[0:AW, :], ALU.mult).then_inc(dve_step, 1)
                dve.wait_ge(dve_step, nth())
                to_pe()
                v.tensor_scalar(DT[0:AW, 0, :], c0T[0:AW, :], -NEG, NEG, ALU.mult, ALU.add).then_inc(dve_step, 1)
                dve.wait_ge(dve_step, nth())
                v.tensor_tensor(TF[0:AW, 0:P], MF[0:AW, 0:P], c0T[0:AW, :], ALU.mult).then_inc(dve_step, 1)
                dve.wait_ge(dve_step, nth())
                v.tensor_tensor(TF[0:AW, 0:P], TF[0:AW, 0:P], DT[0:AW, 0, :], ALU.add).then_inc(dve_step, 1)
                dve.wait_ge(dve_step, nth())
                to_pe()
                v.tensor_copy(fm[:, 1:2], MI[:, 256:257]).then_inc(dve_step, 1)
                dve.wait_ge(dve_step, nth())
                at_front(fm[:, 0:1], mx[:, :])
                v.tensor_tensor(fm[:, 3:4], fm[:, 0:1], fm[:, 1:2], ALU.max).then_inc(dve_step, 1)
                dve.wait_ge(dve_step, nth())
                v.tensor_scalar(fm[:, 4:6], fm[:, 0:2], fm[:, 3:4], None, ALU.subtract).then_inc(dve_step, 1)
                dve.wait_ge(dve_step, nth())
                dve.sem_inc(dif_ready, 1)
                dve.wait_ge(exp_ready, r_exp.more(1))
                dve.wait_ge(f_gathered, r_fg.more(16))
                v.tensor_scalar(FR[:, 0, :], FR[:, 0, :], fm[:, 6:7], None, ALU.mult).then_inc(dve_step, 1)
                dve.wait_ge(dve_step, nth())
                v.scalar_tensor_tensor(FR[:, 0, :], MI[:, 128:128 + AW], fm[:, 7:8], FR[:, 0, :],
                                       ALU.mult, ALU.add).then_inc(dve_step, 1)
                dve.wait_ge(dve_step, nth())
                dve.sem_inc(f_ready, 1)
                v.reciprocal(fm[:, 4:5], FR[:, 0, D + 2:D + 3]).then_inc(dve_step, 1)
                dve.wait_ge(dve_step, nth())
                v.tensor_tensor(fm[:, 2:3], fm[:, 4:5], FR[:, 0, D + 1:D + 2], ALU.mult).then_inc(dve_step, 1)
                dve.wait_ge(dve_step, nth())
                v.tensor_tensor(fm[:, 4:5], fm[:, 4:5], wk[:, :], ALU.mult).then_inc(dve_step, 1)
                dve.wait_ge(dve_step, nth())
                v.scalar_tensor_tensor(X[:, FC, :], FR[:, 0, 0:D], fm[:, 4:5], X[:, FC, :],
                                       ALU.mult, ALU.add).then_inc(dve_step, 1)
                dve.wait_ge(dve_step, nth())
                spread()
                dve.wait_ge(f_stored, r_fs.more(16))

            with dve.Fori(0, K2 // 2 - 1) as i:
                fresh()
                step_d(2 * i, True)
                step_d(2 * i + 1, False)
            fresh()
            step_d(K2 - 2, True)
            step_d(K2 - 1, False, True)
            dve.wait_ge(stored["e"], r_stored["e"].reg)
            stage_e(X[:, FC:XC, :], 2, f_ready)
            dve.wait_ge(f_stored, r_fs.more(16))

            v.tensor_copy(mx[:, :], snE[:, :])
            v.tensor_copy(idxC[:, :], idxA[:, :]).then_inc(dve_step, 1)
            dve.wait_ge(dve_step, nth())
            dve.sem_inc(step_done, 1)
            def step_e(k):
                v.tensor_copy(wk[:, :], mixb[:, ds(k + 1, 1)]).then_inc(dve_step, 1)
                dve.wait_ge(dve_step, nth())
                begin()
                with dve.Fori(0, NCH // 2) as i:
                    fresh()
                    for s in (0, 1):
                        c = 2 * i + s
                        g = G[:, s, :, 0:D]
                        v.tensor_copy(chn[:, 0, :], cols(cont, c))
                        v.tensor_copy(chn[:, 2, :], dnorm[:, ds(c * CH, CH)])
                        v.tensor_copy(chn[:, 1, :], cols(mx, c)).then_inc(dve_step, 1)
                        dve.wait_ge(dve_step, nth())
                        v.tensor_scalar(chn[:, 3, :], chn[:, 2, :], wk[:, 0:1], None, ALU.mult).then_inc(dve_step, 1)
                        dve.wait_ge(dve_step, nth())
                        dve.wait_ge(gathered3[s], r_gat3[s].more(16 * CH))
                        v.tensor_tensor(g, g, wide(chn[:, 1, :]), ALU.mult).then_inc(dve_step, 1)
                        dve.wait_ge(dve_step, nth())
                        chain(s, D, chn[:, 0, :])
                        v.tensor_tensor(agg[:, :, :], g, wide(chn[:, 3, :]), ALU.mult).then_inc(dve_step, 1)
                        dve.wait_ge(dve_step, nth())
                        dve.sem_inc(used[s], 1)
                        v.tensor_tensor(xcols(c), xcols(c), agg[:, :, :], ALU.add).then_inc(dve_step, 1)
                        dve.wait_ge(dve_step, nth())
                carry_in(D)
                dve.sem_inc(f_ready, 1)
                v.tensor_tensor(fm[:, 4:5], dnorm[:, FC:FC + 1], wk[:, :], ALU.mult).then_inc(dve_step, 1)
                dve.wait_ge(dve_step, nth())
                v.scalar_tensor_tensor(X[:, FC, :], FR[:, 0, 0:D], fm[:, 4:5], X[:, FC, :],
                                       ALU.mult, ALU.add).then_inc(dve_step, 1)
                dve.wait_ge(dve_step, nth())
                dve.wait_ge(f_stored, r_fs.more(16))

            step_e(0)
            dve.sem_inc(arrays_free, 1)

            r_sc = [Reached(dve, f"dve_sc{s}") for s in (0, 1)]
            for s in (0, 1):
                r_sc[s].skip(2 * 16 * CH * (NCH // 2))
            with dve.Fori(0, NCH // 2) as i:
                fresh()
                for s in (0, 1):
                    dve.wait_ge(scattered[s], r_sc[s].reg)
                    r_sc[s].skip(16 * CH)
                    v.tensor_copy(G[:, s, :, 0:D], xcols(2 * i + s)).then_inc(dve_step, 1)
                    dve.wait_ge(dve_step, nth())
                    dve.sem_inc(final_ready[s], 1)

            fresh()
            dve.wait_ge(final_stored, 16)
            v.memset(X[:, :, :], 0.0).then_inc(dve_step, 1)
            dve.wait_ge(dve_step, nth())
            v.tensor_copy(allcT[:, :], sl[:, S_C0:S_C0 + 1].to_broadcast([P, P])).then_inc(dve_step, 1)
            dve.wait_ge(dve_step, nth())
            to_pe()
            v.tensor_copy(c0T[:, :], MI[:, 0:P])
            v.tensor_copy(allcT[:, :], sl[:, S_ALLC:S_ALLC + 1].to_broadcast([P, P])).then_inc(dve_step, 1)
            dve.wait_ge(dve_step, nth())
            to_pe()
            v.tensor_copy(allcT[:, :], MI[:, 0:P])
            dve.wait_ge(kept_loaded, 16 * len(KEPT))
            at_front(sl[:, S_DN:S_DN + 1], seatf[:, :])
            short_cols = dve.value_load(shortI[0:1, 0:1], min_val=0, max_val=COLS)
            def short_step(k):
                v.tensor_copy(wk[:, :], mixb[:, ds(k, 1)]).then_inc(dve_step, 1)
                dve.wait_ge(dve_step, nth())
                begin()
                with dve.Fori(0, NCH // 2) as i:
                    with dve.If(i * (2 * CH) < short_cols):
                        fresh()
                        for s in (0, 1):
                            c = 2 * i + s
                            g = G[:, s, :, 0:D]
                            v.tensor_copy(chn[:, 0, :], cols(after, c))
                            v.tensor_copy(chn[:, 1, :], cols(mx, c))
                            v.tensor_copy(chn[:, 2, :], cols(seatf, c)).then_inc(dve_step, 1)
                            dve.wait_ge(dve_step, nth())
                            v.tensor_scalar(chn[:, 3, :], chn[:, 2, :], wk[:, 0:1], None, ALU.mult).then_inc(dve_step, 1)
                            dve.wait_ge(dve_step, nth())
                            dve.wait_ge(gathered3[s], r_gat3[s].more(16 * CH))
                            v.tensor_tensor(g, g, wide(chn[:, 1, :]), ALU.mult).then_inc(dve_step, 1)
                            dve.wait_ge(dve_step, nth())
                            chain(s, D, chn[:, 0, :])
                            v.tensor_tensor(agg[:, :, :], g, wide(chn[:, 3, :]), ALU.mult).then_inc(dve_step, 1)
                            dve.wait_ge(dve_step, nth())
                            dve.sem_inc(used[s], 1)
                            v.tensor_tensor(xcols(c), xcols(c), agg[:, :, :], ALU.add).then_inc(dve_step, 1)
                            dve.wait_ge(dve_step, nth())
                fresh()
                carry_in(D)
                dve.sem_inc(f_ready, 1)
                v.tensor_tensor(fm[:, 4:5], sl[:, S_DN:S_DN + 1], wk[:, :], ALU.mult).then_inc(dve_step, 1)
                dve.wait_ge(dve_step, nth())
                v.scalar_tensor_tensor(X[:, FC, :], FR[:, 0, 0:D], fm[:, 4:5], X[:, FC, :],
                                       ALU.mult, ALU.add).then_inc(dve_step, 1)
                dve.wait_ge(dve_step, nth())
                dve.wait_ge(f_stored, r_fs.more(16))

            with dve.Fori(2, K3 + 1) as k:
                fresh()
                short_step(k)
            with dve.Fori(0, NCH // 2) as i:
                with dve.If(i * (2 * CH) < short_cols):
                    fresh()
                    for s in (0, 1):
                        dve.wait_ge(scattered[s], r_sc[s].reg)
                        r_sc[s].skip(16 * CH)
                        v.tensor_copy(G[:, s, :, 0:D], xcols(2 * i + s)).then_inc(dve_step, 1)
                        dve.wait_ge(dve_step, nth())
                        dve.sem_inc(final_ready[s], 1)


_ARGS = ["x", "src", "dst", "edge_attr_64", "L0_gnn_W3", "L0_gnn_b3", "L0_gnn_W4", "L0_gnn_b4",
         "L1_gnn_W", "L1_gnn_b", "L1_gnn_eps", "L2_gnn_attn_w", "L2_gnn_temp"]


def kernel(**inputs):
    import numpy as np
    import concourse.bacc as bacc
    from concourse import mybir
    from concourse.bass_utils import run_bass_kernel_spmd

    nc = bacc.Bacc("TRN2", target_bir_lowering=False, num_devices=1)
    arrays, args = {}, []
    for name in _ARGS:
        a = np.ascontiguousarray(inputs[name])
        if a.ndim == 0:
            a = a.reshape(1)
        arrays[f"in_{name}"] = a
        args.append(nc.dram_tensor(f"in_{name}", a.shape, mybir.dt.from_np(a.dtype), kind="ExternalInput").ap())
    out = nc.dram_tensor("out", [_N, _D], mybir.dt.float32, kind="ExternalOutput").ap()
    _build(nc, *args, out)
    r = run_bass_kernel_spmd(nc, [arrays], core_ids=[0])
    return r.results[0]["out"]
```
